# Optimizing a Trainium2 kernel written in Bass

```python
import numpy as np
import jax
import jax.numpy as jnp

def _softmax(x, axis=-1):
    return jax.nn.softmax(x, axis=axis)

def _gelu(x):
    return jax.nn.gelu(x, approximate=True)

def _silu(x):
    return jax.nn.silu(x)

def _sigmoid(x):
    return jax.nn.sigmoid(x)

def _layernorm(x, axis=-1, eps=1e-05):
    m = jnp.mean(x, axis=axis, keepdims=True)
    v = jnp.var(x, axis=axis, keepdims=True)
    return (x - m) / jnp.sqrt(v + eps)

def _scatter_add(tgt, idx, src, axis=0):
    return tgt.at[idx].add(src)

def _segment_sum(src, seg, n):
    return jax.ops.segment_sum(src, seg, n)
kernel_name = 'mk_adaln_d1_jaxref_r4_824275'

def setup_inputs(seed: int=0):
    np.random.seed(seed)
    _w = jnp.asarray

    def _L0_attn_setup():
        import jax, jax.numpy as jnp
        import numpy as np
        import math
        NUM_BUCKETS = 32
        MAX_DISTANCE = 128

        def _relative_position_bucket(relative_position):
            rp = jnp.maximum(-relative_position, 0)
            max_exact = NUM_BUCKETS // 2
            is_small = rp < max_exact
            rp_f = jnp.maximum(rp, 1).astype(jnp.float32)
            large = max_exact + (jnp.log(rp_f / max_exact) / math.log(MAX_DISTANCE / max_exact) * (NUM_BUCKETS - max_exact)).astype(jnp.int32)
            large = jnp.minimum(large, NUM_BUCKETS - 1)
            return jnp.where(is_small, rp, large)

        def _t5_rel_bias(bias_table, T):
            ctx = jnp.arange(T, dtype=jnp.int32)[:, None]
            mem = jnp.arange(T, dtype=jnp.int32)[None, :]
            buckets = _relative_position_bucket(mem - ctx)
            values = bias_table[buckets]
            return jnp.transpose(values, (2, 0, 1))[None]
        key = jax.random.key(seed)
        ks = jax.random.split(key, 6)
        B, T, C, H = (2, 512, 256, 16)
        x = jax.random.normal(ks[0], (B, T, C), dtype=jnp.float32)
        W_attn = jax.random.normal(ks[1], (C, 3 * C), dtype=jnp.float32) * 0.02
        b_attn = jnp.zeros((3 * C,), dtype=jnp.float32)
        W_proj = jax.random.normal(ks[2], (C, C), dtype=jnp.float32) * 0.02
        b_proj = jnp.zeros((C,), dtype=jnp.float32)
        bias_table = jax.random.normal(ks[3], (NUM_BUCKETS, H), dtype=jnp.float32) * 0.02
        return {'x': x, 'W_attn': W_attn, 'b_attn': b_attn, 'W_proj': W_proj, 'b_proj': b_proj, 'bias_table': bias_table}
    _L0_attn_in = _L0_attn_setup()

    def _L0_ffn_setup():
        import jax, jax.numpy as jnp
        import numpy as np
        DIM = 256
        HID = 512
        E = 8
        K = 2
        R = 16
        B_, S_ = (2, 256)

        def _lora_in(xf, W, b, A, B):
            base = jnp.einsum('td,ehd->teh', xf, W)
            low = jnp.einsum('ter,ehr->teh', jnp.einsum('td,erd->ter', xf, A), B)
            return base + low + b

        def _lora_out(g, W, b, A, B):
            base = jnp.einsum('teh,edh->ted', g, W)
            low = jnp.einsum('ter,edr->ted', jnp.einsum('teh,erh->ter', g, A), B)
            return base + low + b
        key = jax.random.key(seed)
        ks = jax.random.split(key, 14)
        n = lambda k, shape, scale: jax.random.normal(k, shape, jnp.float32) * scale
        inp = {'x': jax.random.normal(ks[0], (B_, S_, DIM), jnp.float32), 'Wg': n(ks[1], (E, DIM), DIM ** (-0.5)), 'W1': n(ks[2], (E, HID, DIM), DIM ** (-0.5)), 'b1': jnp.zeros((E, HID), jnp.float32), 'A1': n(ks[3], (E, R, DIM), DIM ** (-0.5)), 'B1': n(ks[4], (E, HID, R), 0.01), 'W2': n(ks[5], (E, DIM, HID), HID ** (-0.5)), 'b2': jnp.zeros((E, DIM), jnp.float32), 'A2': n(ks[6], (E, R, HID), HID ** (-0.5)), 'B2': n(ks[7], (E, DIM, R), 0.01), 'W3': n(ks[8], (E, HID, DIM), DIM ** (-0.5)), 'b3': jnp.zeros((E, HID), jnp.float32), 'A3': n(ks[9], (E, R, DIM), DIM ** (-0.5)), 'B3': n(ks[10], (E, HID, R), 0.01)}
        return inp
    _L0_ffn_in = _L0_ffn_setup()
    _L0_c = _w((lambda *s: np.random.randn(*s).astype(np.float32) * 0.05)(8, 256))
    _L0_wmod = _w((lambda *s: np.random.randn(*s).astype(np.float32) * 0.05)(256, 6 * 256) * 256 ** (-0.5))
    _d = {'L0_attn_x': _L0_attn_in['x'], 'L0_attn_W_attn': _L0_attn_in['W_attn'], 'L0_attn_b_attn': _L0_attn_in['b_attn'], 'L0_attn_W_proj': _L0_attn_in['W_proj'], 'L0_attn_b_proj': _L0_attn_in['b_proj'], 'L0_attn_bias_table': _L0_attn_in['bias_table'], 'L0_ffn_Wg': _L0_ffn_in['Wg'], 'L0_ffn_W1': _L0_ffn_in['W1'], 'L0_ffn_b1': _L0_ffn_in['b1'], 'L0_ffn_A1': _L0_ffn_in['A1'], 'L0_ffn_B1': _L0_ffn_in['B1'], 'L0_ffn_W2': _L0_ffn_in['W2'], 'L0_ffn_b2': _L0_ffn_in['b2'], 'L0_ffn_A2': _L0_ffn_in['A2'], 'L0_ffn_B2': _L0_ffn_in['B2'], 'L0_ffn_W3': _L0_ffn_in['W3'], 'L0_ffn_b3': _L0_ffn_in['b3'], 'L0_ffn_A3': _L0_ffn_in['A3'], 'L0_ffn_B3': _L0_ffn_in['B3'], 'L0_c': _L0_c, 'L0_wmod': _L0_wmod}
    _x0 = _d['L0_attn_x']
    _d['L0_attn_x'] = jax.random.normal(jax.random.fold_in(jax.random.key(seed), 1), (8, 512, 256), dtype=_x0.dtype)
    del _x0
    return _d

def reference(L0_attn_x, L0_attn_W_attn, L0_attn_b_attn, L0_attn_W_proj, L0_attn_b_proj, L0_attn_bias_table, L0_ffn_Wg, L0_ffn_W1, L0_ffn_b1, L0_ffn_A1, L0_ffn_B1, L0_ffn_W2, L0_ffn_b2, L0_ffn_A2, L0_ffn_B2, L0_ffn_W3, L0_ffn_b3, L0_ffn_A3, L0_ffn_B3, L0_c, L0_wmod):

    def _L0_attn_ref(x, W_attn, b_attn, W_proj, b_proj, bias_table):
        import jax, jax.numpy as jnp
        import numpy as np
        import math
        NUM_BUCKETS = 32
        MAX_DISTANCE = 128

        def _relative_position_bucket(relative_position):
            rp = jnp.maximum(-relative_position, 0)
            max_exact = NUM_BUCKETS // 2
            is_small = rp < max_exact
            rp_f = jnp.maximum(rp, 1).astype(jnp.float32)
            large = max_exact + (jnp.log(rp_f / max_exact) / math.log(MAX_DISTANCE / max_exact) * (NUM_BUCKETS - max_exact)).astype(jnp.int32)
            large = jnp.minimum(large, NUM_BUCKETS - 1)
            return jnp.where(is_small, rp, large)

        def _t5_rel_bias(bias_table, T):
            ctx = jnp.arange(T, dtype=jnp.int32)[:, None]
            mem = jnp.arange(T, dtype=jnp.int32)[None, :]
            buckets = _relative_position_bucket(mem - ctx)
            values = bias_table[buckets]
            return jnp.transpose(values, (2, 0, 1))[None]
        B, T, C = x.shape
        H = bias_table.shape[1]
        D = C // H
        qkv = x @ W_attn + b_attn
        q, k, v = jnp.split(qkv, 3, axis=-1)
        q = q.reshape(B, T, H, D).transpose(0, 2, 1, 3)
        k = k.reshape(B, T, H, D).transpose(0, 2, 1, 3)
        v = v.reshape(B, T, H, D).transpose(0, 2, 1, 3)
        rel_bias = _t5_rel_bias(bias_table, T)
        att = jnp.einsum('bhtd,bhsd->bhts', q, k) * (1.0 / math.sqrt(D))
        att = att + rel_bias
        causal = jnp.tril(jnp.ones((T, T), dtype=bool))
        att = jnp.where(causal, att, -jnp.inf)
        att = jax.nn.softmax(att, axis=-1)
        y = jnp.einsum('bhts,bhsd->bhtd', att, v)
        y = y.transpose(0, 2, 1, 3).reshape(B, T, C)
        return y @ W_proj + b_proj

    def _L0_ffn_ref(x, Wg, W1, b1, A1, B1, W2, b2, A2, B2, W3, b3, A3, B3):
        import jax, jax.numpy as jnp
        import numpy as np
        DIM = 256
        HID = 512
        E = 8
        K = 2
        R = 16
        B_, S_ = (2, 256)

        def _lora_in(xf, W, b, A, B):
            base = jnp.einsum('td,ehd->teh', xf, W)
            low = jnp.einsum('ter,ehr->teh', jnp.einsum('td,erd->ter', xf, A), B)
            return base + low + b

        def _lora_out(g, W, b, A, B):
            base = jnp.einsum('teh,edh->ted', g, W)
            low = jnp.einsum('ter,edr->ted', jnp.einsum('teh,erh->ter', g, A), B)
            return base + low + b
        orig_shape = x.shape
        xf = x.reshape(-1, x.shape[-1])
        scores = jax.nn.softmax(xf @ Wg.T, axis=-1)
        expert_weights, expert_indices = jax.lax.top_k(scores, K)
        expert_weights = expert_weights / expert_weights.sum(-1, keepdims=True)
        gates = (jax.nn.one_hot(expert_indices, E, dtype=xf.dtype) * expert_weights[..., None]).sum(axis=1)
        h1 = _lora_in(xf, W1, b1, A1, B1)
        h3 = _lora_in(xf, W3, b3, A3, B3)
        g = jax.nn.silu(h1) * h3
        y_e = _lora_out(g, W2, b2, A2, B2)
        y = jnp.einsum('te,ted->td', gates, y_e)
        return y.reshape(orig_shape)
    x = L0_attn_x
    mod = (_silu(L0_c) @ L0_wmod).reshape(L0_c.shape[0], 6, 1, -1)
    sa, ca, ga, sb, cb, gb = (mod[:, 0], mod[:, 1], mod[:, 2], mod[:, 3], mod[:, 4], mod[:, 5])
    ga = (2 * (ga >= 0) - 1) * jnp.maximum(jnp.abs(ga), 0.25)
    gb = (2 * (gb >= 0) - 1) * jnp.maximum(jnp.abs(gb), 0.25)
    h = _layernorm(x, axis=-1) * (1 + ca) + sa
    x = x + ga * _L0_attn_ref(h, L0_attn_W_attn, L0_attn_b_attn, L0_attn_W_proj, L0_attn_b_proj, L0_attn_bias_table)
    h = _layernorm(x, axis=-1) * (1 + cb) + sb
    x = x + gb * _L0_ffn_ref(h, L0_ffn_Wg, L0_ffn_W1, L0_ffn_b1, L0_ffn_A1, L0_ffn_B1, L0_ffn_W2, L0_ffn_b2, L0_ffn_A2, L0_ffn_B2, L0_ffn_W3, L0_ffn_b3, L0_ffn_A3, L0_ffn_B3)
    return x

_drawn_inputs = setup_inputs


def setup_inputs(seed=0):
    import zlib

    import numpy as np

    out = dict(_drawn_inputs(seed))
    spreads = {'L0_attn_b_attn': (0.0, 0.676),
     'L0_attn_b_proj': (0.0, 0.1),
     'L0_ffn_b1': (0.0, 0.689),
     'L0_ffn_b2': (0.0, 1.332),
     'L0_ffn_b3': (0.0, 0.712)}
    factors = {'L0_attn_W_attn': 8.0,
     'L0_attn_W_proj': 5.143,
     'L0_attn_bias_table': 8.0,
     'L0_ffn_A1': 8.0,
     'L0_ffn_B1': 8.0,
     'L0_ffn_A2': 8.0,
     'L0_ffn_B2': 8.0,
     'L0_ffn_A3': 8.0,
     'L0_ffn_B3': 8.0}
    for name, (base, spread) in spreads.items():
        noise = np.random.default_rng([zlib.crc32(name.encode()), seed]).standard_normal(out[name].shape)
        drawn = base * np.exp(spread * noise) if base else spread * noise
        out[name] = jnp.asarray(drawn.astype(out[name].dtype))
    for name, factor in factors.items():
        out[name] = (out[name] * factor).astype(out[name].dtype)
    return out
```

```python
from contextlib import ExitStack

import numpy as np

import concourse.bass as bass
from concourse import mybir

F32 = mybir.dt.float32
F32R = mybir.dt.float32r
I32 = mybir.dt.int32
U32 = mybir.dt.uint32
ALU = mybir.AluOpType
ACT = mybir.ActivationFunctionType
AX = mybir.AxisListType

P = 128
B, T, C = 8, 512, 256
H = 16
D = C // H
E, R, HID = 8, 16, 512
TT = T // P
KC = C // P
HK = HID // P
HH = H // 2
NBUCKET = 32
EPS = 1e-5
MASKED = -1e30
LIN = T + P - 1
FT = 256
REGION = B * T + 2 * FT
BIG = 3e38

TILE_ORDER = [3, 2, 0, 1]
TILE_AT = {3: (0, 0), 2: (1, 0), 0: (1, 384), 1: (2, 0)}
EXPS_AFTER_SLOT = [1, 3, 4]
P_AT = {3: 0, 2: 512, 1: 896, 0: 1152}
TR_AT = {0: (0, 0), 1: (1, 0), 3: (1, 384), 2: (2, 0)}
PT_AT = {0: 0, 1: 512, 3: 896, 2: 1024}
TR_SLOT = [(0, 512), (512, 512), (1024, 256)]
NPROB = 1280

AUX_PRO = ["hT0", "hT1", "q", "k", "v"]
AUX_STEP = {0: ["q1"], 1: ["k1"], 2: ["v1"], 3: ["yT0", "yT1"], 4: ["pr0", "pr1"], 6: ["ytr0"],
            8: ["hT0", "hT1"], 10: ["ytr1"], 11: ["q"], 12: ["k"], 13: ["v"], 14: ["ytr2"],
            15: ["h2T0", "h2T1"], 16: ["lg"], 17: ["pos"], 18: ["ytr3"], 19: ["gab", "csb"]}
STEPS = 20
POST = ["yT0", "yT1", "pr0", "pr1", "h2T0", "h2T1", "lg", "pos"]
AHEAD = ["hT0", "hT1", "q", "k", "v"]


def tasks(kind):
    skip = POST if kind == "first" else AHEAD if kind == "last" else []
    return [t for i in range(STEPS) for t in AUX_STEP.get(i, []) if t not in skip]


def start_turn(kind, b):
    pro, first, loop, last = len(AUX_PRO), len(tasks("first")), len(tasks("loop")), len(tasks("last"))
    if kind == "pro":
        return 0
    if kind == "first":
        return pro
    if kind == "loop":
        return b * loop + (pro + first - loop)
    return pro + first + (B - 2) * loop + (last if kind == "end" else 0)


def turn_of(kind, b, name):
    names = AUX_PRO if kind == "pro" else POST if kind == "end" else tasks(kind)
    return start_turn(kind, b) + names.index(name)


def step_tasks(kind, i):
    skip = POST if kind == "first" else AHEAD if kind == "last" else []
    return [t for t in AUX_STEP.get(i, []) if t not in skip]


def each_batch(eng, body):
    body("first", 0)
    with eng.Fori(1, B - 1) as b:
        body("loop", b)
    body("last", B - 1)


def constants():
    v = np.arange(LIN)
    dist = (T - P) + (P - 1) - v
    rp = np.maximum(dist, 0)
    max_exact = NBUCKET // 2
    large = max_exact + (np.log(np.maximum(rp, 1).astype(np.float32) / np.float32(max_exact))
                         / np.float32(np.log(128 / max_exact)) * np.float32(NBUCKET - max_exact)).astype(np.int32)
    bucket = np.where(rp < max_exact, rp, np.minimum(large, NBUCKET - 1))
    bucket = np.where(dist < 0, NBUCKET, bucket)
    onehot = np.zeros((NBUCKET + 1, LIN), np.float32)
    onehot[bucket, v] = 1.0
    return onehot


def setup(nc, sem, w_attn, b_qk, b_v, w_proj, b_proj, bias_table, onehot, wg, cT, wmod, line_d, k):
    with ExitStack() as ctx:
        def sb(name, shape, dt=F32):
            return ctx.enter_context(nc.sbuf_tensor(name, shape, dt))

        table = sb("table", [NBUCKET + 1, H])
        oh_line = sb("oh_line", [NBUCKET + 1, LIN])
        line = sb("line", [H, LIN])
        c_raw = sb("c_raw", [P, KC, B])
        wmod_cols = sb("wmod_cols", [P, KC, 2 * C])
        bv_col = sb("bv_col", [P, KC])
        iota_i = sb("iota_i", [P, TT, E], I32)
        region_i = sb("region_i", [P, TT, E], I32)
        line_ps = ctx.enter_context(nc.psum_tensor("line_ps", [P, 2, 512], F32))
        mod_ps = ctx.enter_context(nc.psum_tensor("mod_ps", [P, 512], F32))
        bv_ps = ctx.enter_context(nc.psum_tensor("bv_ps", [P, 512], F32))
        loaded, masked, silu_done, line_made, line_out, line_stored, bias_loaded = (
            sem(n) for n in ("loaded", "masked", "silu_done", "line_made", "line_out", "line_stored", "bias_loaded"))
        mod_made, bv_made, scaled, ones_set, iotas, mod_out = (
            sem(n) for n in ("mod_made", "bv_made", "scaled", "ones_set", "iotas", "mod_out"))
        block = ctx.enter_context(nc.Block())
        NLOAD = 11 + 4 * KC

        @block.sync
        def _(sp):
            sp.dma_start(table[0:NBUCKET, :], bias_table).then_inc(loaded, 16)
            sp.dma_start(oh_line[:], onehot).then_inc(loaded, 16)
            sp.dma_start(c_raw[:], cT.rearrange("(k p) b -> p k b", p=P)).then_inc(loaded, 16)
            sp.dma_start(wmod_cols[:], wmod[:, 0:2 * C].rearrange("(k p) n -> p k n", p=P)).then_inc(loaded, 16)
            sp.dma_start(k.wa[:], w_attn.rearrange("(k p) n -> p k n", p=P)).then_inc(loaded, 16)
            sp.dma_start(k.bqk[:], b_qk.rearrange("(m p) -> p m", p=P), allow_slow_non_contiguous=True).then_inc(loaded, 16)
            sp.dma_start(bv_col[:], b_v.rearrange("(m p) -> p m", p=P), allow_slow_non_contiguous=True).then_inc(loaded, 16)
            sp.dma_start(k.bp_row[:], b_proj.rearrange("(a n) -> a n", a=1)).then_inc(loaded, 16)
            sp.dma_start(k.wp[:], w_proj.rearrange("(k p) n -> p k n", p=P)).then_inc(loaded, 16)
            sp.dma_start(k.wg_sb[:], wg.rearrange("(k p) e -> p k e", p=P)).then_inc(loaded, 16)
            for kc in range(KC):
                for n, part in enumerate((2, 5, 3, 4)):
                    sp.dma_start(k.wm_rows[:, kc, n, :], wmod[kc * P:(kc + 1) * P, part * C:(part + 1) * C]
                                 ).then_inc(loaded, 16)
            sp.wait_ge(line_out, 2)
            sp.dma_start(line_d[:, 0:LIN], line[:]).then_inc(line_stored, 16)
            sp.wait_ge(line_stored, 16)
            for p in range(P):
                sp.dma_start(k.bias_w[p:p + 1, :, :], line_d[:, P - 1 - p:P - 1 - p + T].rearrange("(a h) c -> a h c", a=1)
                             ).then_inc(bias_loaded, 16)
            sp.wait_ge(bias_loaded, 16 * P)

        @block.tensor
        def _(pe):
            pe.wait_ge(loaded, 16 * (NLOAD - 1))
            pe.wait_ge(masked, 1)
            pe.matmul(line_ps[0:H, 0, :], table[:], oh_line[:, 0:512], start=True, stop=True).then_inc(line_made, 1)
            pe.matmul(line_ps[0:H, 1, 0:LIN - 512], table[:], oh_line[:, 512:LIN], start=True, stop=True
                      ).then_inc(line_made, 1)
            pe.wait_ge(silu_done, 1)
            for part in range(2):
                for m in range(KC):
                    col = (part * KC + m) * B
                    for kc in range(KC):
                        mm = pe.matmul(mod_ps[:, col:col + B], wmod_cols[:, kc, part * C + m * P:part * C + (m + 1) * P],
                                       k.sc[:, kc, :], start=(kc == 0), stop=(kc == KC - 1))
            mm.then_inc(mod_made, 1)
            for kc in range(KC):
                mm = pe.matmul(bv_ps[0:1, 0:C], bv_col[:, kc:kc + 1], k.wp[:, kc, :], start=(kc == 0), stop=(kc == KC - 1))
            mm.then_inc(bv_made, 1)

        @block.scalar
        def _(act):
            act.wait_ge(loaded, 16 * (NLOAD - 1))
            nc.scalar.activation(k.sc[:], c_raw[:], ACT.Silu).then_inc(silu_done, 1)
            nc.scalar.mul(k.wa[:, :, 0:C], k.wa[:, :, 0:C], D ** -0.5)
            nc.scalar.mul(k.bqk[:, 0:KC], k.bqk[:, 0:KC], D ** -0.5).then_inc(scaled, 1)
            act.wait_ge(line_made, 2)
            nc.scalar.copy(line[:, 0:512], line_ps[0:H, 0, :]).then_inc(line_out, 1)
            nc.scalar.copy(line[:, 512:LIN], line_ps[0:H, 1, 0:LIN - 512]).then_inc(line_out, 1)

        @block.vector
        def _(dve):
            v = nc.vector
            v.memset(table[NBUCKET:NBUCKET + 1, :], MASKED).then_inc(masked, 1)
            v.memset(k.carry[:], 0.0)
            v.memset(k.neghalf[:], -0.5)
            dve.wait_ge(iotas, 2)
            v.tensor_copy(k.iota_e[:], iota_i[:])
            v.tensor_copy(k.region[:], region_i[:])
            dve.wait_ge(mod_made, 1)
            v.tensor_copy(k.mod_c[:, 0, :, :], mod_ps[:, 0:KC * B].rearrange("p (k b) -> p k b", k=KC))
            v.tensor_scalar(k.mod_c[:, 1, :, :], mod_ps[:, KC * B:2 * KC * B].rearrange("p (k b) -> p k b", k=KC),
                            1.0, None, ALU.add)
            dve.wait_ge(bv_made, 1)
            v.tensor_tensor(k.bp_row[:], k.bp_row[:], bv_ps[0:1, 0:C], ALU.add).then_inc(mod_out, 1)

        @block.gpsimd
        def _(pool):
            g = nc.gpsimd
            g.iota(iota_i[:], [[0, TT], [1, E]], base=0, channel_multiplier=0).then_inc(iotas, 1)
            g.iota(region_i[:], [[0, TT], [REGION, E]], base=0, channel_multiplier=0).then_inc(iotas, 1)
            g.memset(k.ones[:], 1.0).then_inc(ones_set, 1)
            pool.wait_ge(ones_set, 1)
            g.affine_select(k.ident[:], k.ones[:], [[1, P]], ALU.is_equal, 0.0, base=0, channel_multiplier=-1)
            g.affine_select(k.before[:], k.ones[:], [[1, P]], ALU.is_gt, 0.0, base=0, channel_multiplier=-1)


class Kept:
    pass


def attention(nc, sem, x, qk_d, x1_d, rows_d, gb_d, k):
    with ExitStack() as ctx:
        def sb(name, shape, dt=F32):
            return ctx.enter_context(nc.sbuf_tensor(name, shape, dt))

        q_st = [sb(f"q_st{m}", [P, HH, T], F32R) for m in range(2)]
        k_st = [sb(f"k_st{m}", [P, HH // 2, T], F32R) for m in range(2)]
        v_sb = [sb(f"v_sb{m}", [P, TT, HH, 2 * D]) for m in range(2)]
        probs = [sb(f"probs{i}", [P, NPROB]) for i in range(2)]
        probs_t = sb("probs_t", [P, 8, NPROB])
        neg_max = sb("neg_max", [P, 4, TT])
        part_hi = [sb(f"part_hi{i}", [P, T], F32R) for i in range(2)]
        part_lo = [sb(f"part_lo{i}", [P, T], F32R) for i in range(2)]
        scb = sb("scb", [P, KC, P])
        mod_b = sb("mod_b", [P, 2, KC])
        xin = sb("xin", [P, TT, C])
        h_t = sb("h_t", [P, KC, T])
        stats = [sb(f"stats{i}", [P, TT, 6]) for i in range(2)]
        mv = [sb(f"mv{i}", [P, TT, 2]) for i in range(2)]
        var = [sb(f"var{i}", [P, TT]) for i in range(2)]
        rstd = [sb(f"rstd{i}", [P, TT]) for i in range(2)]
        y_un = sb("y_un", [P, T])
        recips = sb("recips", [P, TT, 4])
        y_tok = sb("y_tok", [P, TT, C])
        y_t = sb("y_t", [P, KC, T])
        gab = sb("gab", [P, 2 * C])
        g_sgn = sb("g_sgn", [P, 2 * C])
        csb = sb("csb", [P, 2 * C])
        xr = sb("xr", [P, TT, C])
        h2 = xr
        x1 = sb("x1", [P, TT, C])
        h2_t = y_t
        logits = sb("logits", [P, TT, E])
        top8 = sb("top8", [P, TT, 8])
        idx8 = sb("idx8", [P, TT, 8], U32)
        idxf = sb("idxf", [P, 2, TT])
        chosen = sb("chosen", [P, 2, TT, E])
        both = sb("both", [P, TT, E])
        both_sum = sb("both_sum", [P, E])
        gap = sb("gap", [P, TT])
        gexp = sb("gexp", [P, TT])
        gden = sb("gden", [P, TT])
        gates = sb("gates", [P, 2, TT])
        place = sb("place", [P, TT, E])
        chosen_place = sb("chosen_place", [P, 2, TT, E])
        slot_f = sb("slot_f", [P, 2, TT])
        slot_b = sb("slot_b", [P, 2 * TT], I32)

        s_bank = [ctx.enter_context(nc.psum_tensor(f"s_bank{i}", [P, 512], F32)) for i in range(4)]
        t_bank = [ctx.enter_context(nc.psum_tensor(f"t_bank{i}", [P, 512], F32)) for i in range(2)]
        y_bank = ctx.enter_context(nc.psum_tensor("y_bank", [P, 512], F32))
        aux = ctx.enter_context(nc.psum_tensor("aux", [P, 512], F32))

        cleared = sem("cleared")
        x_in, xr_in, x1_kept, gb_kept, scattered = (sem(n) for n in ("x_in", "xr_in", "x1_kept", "gb_kept", "scattered"))
        scored, biased, exped, transposed = (sem(n) for n in ("scored", "biased", "exped", "transposed"))
        pt_dve, pt_act, pv_done, y_copied, y_recip = (sem(n) for n in ("pt_dve", "pt_act", "pv_done", "y_copied", "y_recip"))
        aux_ready, aux_free, hi_done = (sem(n) for n in ("aux_ready", "aux_free", "hi_done"))
        stored = [sem(f"stored{i}") for i in range(2)]
        stacked = [sem(f"stacked{i}") for i in range(2)]
        stats_done, mv_done, var_done, rstd_done, normed = (
            [sem(f"{n}{i}") for i in range(2)] for n in ("stats_done", "mv_done", "var_done", "rstd_done", "normed"))
        mod_b_set, scb_set, gab_done, x1_done, h2_scaled, h2_done, rows_free = (
            sem(n) for n in ("mod_b_set", "scb_set", "gab_done", "x1_done", "h2_scaled", "h2_done", "rows_free"))
        top_done, idx_done, idxf_done, chosen_done, both_done, summed, carried, gap_done, exp_done, den_done, g1_done, g2_done = (
            sem(n) for n in ("top_done", "idx_done", "idxf_done", "chosen_done", "both_done", "summed", "carried",
                             "gap_done", "exp_done", "den_done", "g1_done", "g2_done"))
        sign_done, weighed, slot_f_done, slot_done, sb_done = (sem(n) for n in ("sign_done", "weighed", "slot_f_done", "slot_done", "sb_done"))

        def nth_part(kind, b, name):
            return 1 if kind == "pro" else 2 * b + (2 if name[1:] else 3)

        block = ctx.enter_context(nc.Block())

        @block.sync
        def _(sp):
            def load_x(b):
                sp.dma_start(xin[:], x[b].rearrange("(t p) c -> p t c", p=P)).then_inc(x_in, 16)

            def stack(kind, b, name):
                i, m = (0 if name[0] == "q" else 1), (1 if name[1:] else 0)
                sp.wait_ge(aux_free, turn_of(kind, b, name) + 1)
                d = qk_d[i][m]
                n = nth_part(kind, b, name)
                sp.dma_start(d[0], part_hi[i][:].bitcast(F32)).then_inc(stored[i], 16)
                sp.dma_start(d[1], part_lo[i][:].bitcast(F32)).then_inc(stored[i], 16)
                sp.wait_ge(stored[i], 32 * n)
                for hh in range(2):
                    for blk in range(4):
                        part = blk % 2 if i == 0 else blk // 2
                        rows = slice(64 * hh + D * blk, 64 * hh + D * (blk + 1))
                        src = d[part].rearrange("(r a d) t -> a d r t", a=2, d=D)[hh]
                        dst = (q_st[m][rows, hh:HH:2, :] if i == 0 else k_st[m][rows, :, :]).bitcast(F32)
                        sp.dma_start(dst, src).then_inc(stacked[i], 16)

            def load_residual(p):
                sp.wait_ge(rows_free, p + 1)
                sp.dma_start(xr[:], x[p].rearrange("(t p) c -> p t c", p=P)).then_inc(xr_in, 16)

            def keep_x1(p):
                sp.wait_ge(x1_done, p + 1)
                sp.dma_start(x1_d[p].rearrange("(t p) c -> p t c", p=P), x1[:]).then_inc(x1_kept, 16)

            sp.sem_inc(x1_kept, 16)
            load_x(0)
            sp.wait_ge(cleared, 4)
            stack("pro", 0, "q")
            stack("pro", 0, "k")

            def body(kind, b):
                if kind != "last":
                    sp.wait_ge(aux_free, start_turn(kind, b))
                    load_x(b + 1)
                for i in range(STEPS):
                    if i == 2 and kind != "first":
                        load_residual(b - 1)
                    if i == 5 and kind != "first":
                        keep_x1(b - 1)
                    for name in step_tasks(kind, i):
                        if name in ("q1", "k1", "q", "k"):
                            stack(kind, b, name)
                sp.wait_ge(gab_done, b + 1)
                sp.dma_start(gb_d[bass.ds(b, 1), :], gab[0:1, C:2 * C]).then_inc(gb_kept, 16)

            each_batch(sp, body)
            load_residual(B - 1)
            keep_x1(B - 1)
            sp.wait_ge(x1_kept, 16 * (B + 1))
            sp.wait_ge(gb_kept, 16 * B)

        @block.tensor
        def _(pe):
            def task(kind, b, name):
                turn = turn_of(kind, b, name)
                if kind != "pro" or turn:
                    pe.wait_ge(aux_free, turn)
                bb = 0 if kind == "pro" else b + 1 if name in AHEAD else b - 1 if name in POST else b
                m = 1 if name[1:] == "1" else 0
                if name[:2] == "hT":
                    kc = int(name[-1])
                    pe.wait_ge(normed[0], bb + 1)
                    for tt in range(TT):
                        mm = pe.transpose(aux[:, tt * P:(tt + 1) * P], xin[:, tt, kc * P:(kc + 1) * P], k.ident[:])
                elif name in ("q", "q1", "k", "k1"):
                    col = (C if name[0] == "k" else 0) + m * P
                    for kc in range(KC):
                        mm = pe.matmul(aux[:, :], k.wa[:, kc, col:col + P], h_t[:, kc, :], start=(kc == 0), stop=(kc == KC - 1))
                elif name in ("v", "v1"):
                    col = 2 * C + m * P
                    for tt in range(TT):
                        for kc in range(KC):
                            mm = pe.matmul(aux[:, tt * P:(tt + 1) * P], h_t[:, kc, tt * P:(tt + 1) * P],
                                           k.wa[:, kc, col:col + P], start=(kc == 0), stop=(kc == KC - 1))
                elif name in ("gab", "csb"):
                    n = 0 if name == "gab" else 2
                    pe.wait_ge(scb_set, b + 1)
                    for kc in range(KC):
                        mm = pe.matmul(aux[:, :], scb[:, kc, :], k.wm_rows[:, kc, n:n + 2, :].rearrange("p a n -> p (a n)"),
                                       start=(kc == 0), stop=(kc == KC - 1))
                elif name[:3] == "ytr":
                    pe.wait_ge(y_copied, 4 * b + int(name[-1]) + 1)
                    for tt in range(TT):
                        mm = pe.transpose(aux[:, tt * P:(tt + 1) * P], y_un[:, tt * P:(tt + 1) * P], k.ident[:])
                elif name[:2] == "yT":
                    kc = int(name[-1])
                    for tt in range(TT):
                        mm = pe.transpose(aux[:, tt * P:(tt + 1) * P], y_tok[:, tt, kc * P:(kc + 1) * P], k.ident[:])
                elif name[:2] == "pr":
                    for u in range(2):
                        tt = 2 * int(name[-1]) + u
                        cols = slice(u * C, (u + 1) * C)
                        for kc in range(KC):
                            pe.matmul(aux[:, cols], y_t[:, kc, tt * P:(tt + 1) * P], k.wp[:, kc, :], start=(kc == 0), stop=False)
                        mm = pe.matmul(aux[:, cols], k.ones[0:1, :], k.bp_row[0:1, :], start=False, stop=True)
                elif name[:3] == "h2T":
                    kc = int(name[-1])
                    pe.wait_ge(h2_done, bb + 1)
                    for tt in range(TT):
                        mm = pe.transpose(aux[:, tt * P:(tt + 1) * P], h2[:, tt, kc * P:(kc + 1) * P], k.ident[:])
                elif name == "lg":
                    for tt in range(TT):
                        for kc in range(KC):
                            mm = pe.matmul(aux[:, tt * E:(tt + 1) * E], h2_t[:, kc, tt * P:(tt + 1) * P], k.wg_sb[:, kc, :],
                                           start=(kc == 0), stop=(kc == KC - 1))
                elif name == "pos":
                    pe.wait_ge(both_done, bb + 1)
                    pe.wait_ge(carried, bb + 1)
                    for tt in range(TT):
                        cols = slice(tt * E, (tt + 1) * E)
                        pe.matmul(aux[:, cols], k.before[:], both[:, tt, :], start=True, stop=False)
                        for u in range(tt):
                            pe.matmul(aux[:, cols], k.ones[:], both[:, u, :], start=False, stop=False)
                        mm = pe.matmul(aux[:, cols], k.ones[:], k.carry[:], start=False, stop=True)
                mm.then_inc(aux_ready, 1)

            def scores(b, h):
                m, hl = h // HH, h % HH
                if hl == 0:
                    for i in range(2):
                        pe.wait_ge(stacked[i], 128 * (2 * b + m + 1))
                for j in TILE_ORDER:
                    slot, col = TILE_AT[j]
                    n = 3 * h + slot
                    if col == 0 and n >= 4:
                        pe.wait_ge(exped, 4 * H * b + 4 * ((n - 4) // 3) + EXPS_AFTER_SLOT[(n - 4) % 3])
                    w = (j + 1) * P
                    mm = pe.matmul(s_bank[n % 4][:, col:col + w], q_st[m][:, hl, j * P:(j + 1) * P],
                                   k_st[m][:, hl // 2, 0:w], start=True, stop=True)
                    if j != 2:
                        mm.then_inc(scored, 1)

            def transposes(b, h):
                pe.wait_ge(exped, 4 * H * b + 4 * (h + 1))
                for slot in range(3):
                    n = 3 * h + slot
                    if n >= 2:
                        hp, sp_ = (n - 2) // 3, (n - 2) % 3
                        if sp_ == 1:
                            pe.wait_ge(pt_act, H * b + hp + 1)
                        else:
                            pe.wait_ge(pt_dve, 2 * H * b + 2 * hp + (1 if sp_ == 0 else 2))
                    for st in (s for s in (0, 1, 3, 2) if TR_AT[s][0] == slot):
                        for j in range(st, TT):
                            col = TR_AT[st][1] + (j - st) * P
                            src = P_AT[j] + st * P
                            mm = pe.transpose(t_bank[n % 2][:, col:col + P], probs[h % 2][:, src:src + P], k.ident[:])
                    mm.then_inc(transposed, 1)

            def values(kind, b, g):
                m = g // 2
                pe.wait_ge(pt_dve, 2 * H * b + 8 * (g + 1))
                pe.wait_ge(pt_act, H * b + 4 * (g + 1))
                if kind != "first" or g:
                    pe.wait_ge(y_copied, 4 * b + g)
                for st in range(TT):
                    w = (TT - st) * P
                    for hq in range(4):
                        h = 4 * g + hq
                        mm = pe.matmul(y_bank[32 * hq:32 * hq + 32, st * P:T], v_sb[m][:, st, h % HH, :],
                                       probs_t[:, h % 8, PT_AT[st]:PT_AT[st] + w], start=(st == 0), stop=(st == TT - 1),
                                       skip_group_check=True)
                mm.then_inc(pv_done, 1)

            for name in AUX_PRO:
                task("pro", 0, name)

            def body(kind, b):
                for i in range(STEPS):
                    if i < H:
                        scores(b, i)
                    if 1 <= i <= H:
                        transposes(b, i - 1)
                    if i % 4 == 1 and i >= 5:
                        values(kind, b, (i - 5) // 4)
                    for name in step_tasks(kind, i):
                        task(kind, b, name)

            each_batch(pe, body)
            for name in POST:
                task("end", B, name)

        @block.scalar
        def _(act):
            def task(kind, b, name):
                turn = turn_of(kind, b, name)
                bb = 0 if kind == "pro" else b + 1 if name in AHEAD else b - 1 if name in POST else b
                if name == "pos":
                    act.wait_ge(gap_done, bb + 1)
                    nc.scalar.activation(gexp[:], gap[:], ACT.Exp).then_inc(exp_done, 1)
                if name not in ("hT0", "hT1", "q", "q1", "k", "k1", "v", "v1", "yT0", "yT1", "h2T0", "h2T1", "csb"):
                    return
                act.wait_ge(aux_ready, turn + 1)
                m = 1 if name[1:] == "1" else 0
                if name[:2] == "hT":
                    kc = int(name[-1])
                    act.wait_ge(mod_b_set, bb + 1)
                    nc.scalar.activation(h_t[:, kc, :], aux[:, :], ACT.Identity, bias=mod_b[:, 0, kc:kc + 1],
                                         scale=mod_b[:, 1, kc:kc + 1]).then_inc(aux_free, 1)
                elif name[0] in "qk":
                    i = 0 if name[0] == "q" else 1
                    if kind != "pro":
                        act.wait_ge(stored[i], 32 * (nth_part(kind, b, name) - 1))
                    nc.scalar.activation(part_hi[i][:], aux[:, :], ACT.Identity, bias=k.bqk[:, 2 * i + m:2 * i + m + 1]
                                         ).then_inc(hi_done, 1)
                elif name[0] == "v":
                    if kind == "pro":
                        act.wait_ge(cleared, 4)
                    nc.scalar.copy(v_sb[m][:, :, :, 0:D], aux[:, :].rearrange("p (t h d) -> p t h d", t=TT, d=D)
                                   ).then_inc(aux_free, 1)
                elif name[:2] == "yT":
                    nc.scalar.copy(y_t[:, int(name[-1]), :], aux[:, :]).then_inc(aux_free, 1)
                elif name[:3] == "h2T":
                    nc.scalar.copy(h2_t[:, int(name[-1]), :], aux[:, :]).then_inc(aux_free, 1)
                elif name == "csb":
                    nc.scalar.copy(csb[:, 0:C], aux[:, 0:C])
                    nc.scalar.add(csb[:, C:2 * C], aux[:, C:2 * C], 1.0).then_inc(aux_free, 1)

            for name in AUX_PRO:
                task("pro", 0, name)

            def body(kind, b):
                for i in range(STEPS):
                    if i < H:
                        if kind != "first":
                            act.wait_ge(transposed, 3 * H * b + 3 * (i - 1))
                        elif i >= 2:
                            act.wait_ge(transposed, 3 * (i - 1))
                        for q, j in enumerate(TILE_ORDER):
                            slot, col = TILE_AT[j]
                            w = (j + 1) * P
                            act.wait_ge(biased, 4 * H * b + 4 * i + EXPS_AFTER_SLOT[slot])
                            nc.scalar.activation(probs[i % 2][:, P_AT[j]:P_AT[j] + w], s_bank[(3 * i + slot) % 4][:, col:col + w],
                                                 ACT.Exp, bias=neg_max[:, i % 4, j:j + 1], scale=-1.0).then_inc(exped, 1)
                    if 1 <= i <= H:
                        h = i - 1
                        act.wait_ge(transposed, 3 * H * b + 3 * h + 2)
                        if h >= 8:
                            act.wait_ge(pv_done, 4 * b + h // 4 - 1)
                        nc.scalar.copy(probs_t[:, h % 8, 512:1024], t_bank[(3 * h + 1) % 2][:, :]).then_inc(pt_act, 1)
                    if i % 4 == 1 and i >= 5:
                        g = (i - 5) // 4
                        act.wait_ge(pv_done, 4 * b + g + 1)
                        if g:
                            act.wait_ge(aux_free, turn_of(kind, b, f"ytr{g - 1}") + 1)
                        elif kind != "first":
                            act.wait_ge(aux_free, start_turn(kind, b))
                        nc.scalar.copy(y_un[:, :], y_bank[:, :]).then_inc(y_copied, 1)
                    for name in step_tasks(kind, i):
                        task(kind, b, name)

            each_batch(act, body)
            for name in POST:
                task("end", B, name)

        @block.vector
        def _(dve):
            v = nc.vector

            def ln_stats(i, n, src, ready, value):
                dve.wait_ge(ready, value)
                dve.nop(nofuse=True)
                for tt in range(TT):
                    ins = v.bn_stats(stats[i][:, tt, :], src[:, tt, :])
                ins.then_inc(stats_done[i], 1)
                dve.wait_ge(stats_done[i], n)
                dve.nop(nofuse=True)
                for tt in range(TT):
                    ins = v.bn_aggr(mv[i][:, tt, :], stats[i][:, tt, :])
                ins.then_inc(mv_done[i], 1)

            def router_choice(p, turn):
                v.tensor_copy(logits[:], aux[:, 0:TT * E].rearrange("p (t e) -> p t e", t=TT)).then_inc(aux_free, 1)
                dve.wait_ge(aux_free, turn + 1)
                dve.nop(nofuse=True)
                for tt in range(TT):
                    ins = v.max(top8[:, tt, :], logits[:, tt, :])
                ins.then_inc(top_done, 1)
                dve.wait_ge(top_done, p + 1)
                dve.nop(nofuse=True)
                for tt in range(TT):
                    ins = v.max_index(idx8[:, tt, :], top8[:, tt, :], logits[:, tt, :])
                ins.then_inc(idx_done, 1)
                v.tensor_tensor(gap[:], top8[:, :, 1], top8[:, :, 0], ALU.subtract).then_inc(gap_done, 1)
                dve.wait_ge(idx_done, p + 1)
                v.tensor_copy(idxf[:], idx8[:, :, 0:2].rearrange("p t n -> p n t")).then_inc(idxf_done, 1)
                dve.wait_ge(idxf_done, p + 1)
                for n in range(2):
                    ins = v.tensor_tensor(chosen[:, n, :, :], k.iota_e[:],
                                          idxf[:, n, :].unsqueeze(2).to_broadcast([P, TT, E]), ALU.is_equal)
                ins.then_inc(chosen_done, 1)
                dve.wait_ge(chosen_done, p + 1)
                v.tensor_tensor(both[:], chosen[:, 0, :, :], chosen[:, 1, :, :], ALU.add).then_inc(both_done, 1)

            def router_slots(p, turn):
                v.tensor_tensor(place[:], aux[:, 0:TT * E].rearrange("p (t e) -> p t e", t=TT), k.region[:], ALU.add
                                ).then_inc(aux_free, 1)
                v.tensor_reduce(both_sum[:], both[:].rearrange("p t e -> p e t"), AX.X, ALU.add).then_inc(summed, 1)
                dve.wait_ge(summed, p + 1)
                v.tensor_tensor(k.carry[:], k.carry[:], both_sum[:], ALU.add).then_inc(carried, 1)
                dve.wait_ge(aux_free, turn + 1)
                for n in range(2):
                    ins = v.tensor_tensor(chosen_place[:, n, :, :], chosen[:, n, :, :], place[:], ALU.mult)
                ins.then_inc(weighed, 1)
                dve.wait_ge(weighed, p + 1)
                v.tensor_reduce(slot_f[:], chosen_place[:], AX.X, ALU.add).then_inc(slot_f_done, 1)
                dve.wait_ge(rows_free, p + 1)
                dve.wait_ge(slot_f_done, p + 1)
                v.tensor_copy(slot_b[:], slot_f[:].rearrange("p n t -> p (n t)")).then_inc(slot_done, 1)
                dve.wait_ge(exp_done, p + 1)
                v.tensor_scalar(gden[:], gexp[:], 1.0, None, ALU.add).then_inc(den_done, 1)
                dve.wait_ge(den_done, p + 1)
                v.reciprocal(gates[:, 0, :], gden[:]).then_inc(g1_done, 1)
                dve.wait_ge(g1_done, p + 1)
                v.tensor_tensor(gates[:, 1, :], gexp[:], gates[:, 0, :], ALU.mult).then_inc(g2_done, 1)

            def task(kind, b, name):
                turn = turn_of(kind, b, name)
                bb = b - 1 if name in POST else b
                if name in ("hT0", "hT1", "v", "v1", "yT0", "yT1", "h2T0", "h2T1", "csb"):
                    return
                m = 1 if name[1:] == "1" else 0
                if name in ("q", "q1", "k", "k1"):
                    i = 0 if name[0] == "q" else 1
                    dve.wait_ge(hi_done, 2 * nth_part(kind, b, name) - 1 + i)
                    v.scalar_tensor_tensor(out=part_lo[i][:], in0=aux[:, :], scalar=k.bqk[:, 2 * i + m:2 * i + m + 1],
                                           in1=part_hi[i][:].bitcast(F32), op0=ALU.add, op1=ALU.subtract).then_inc(aux_free, 1)
                    return
                dve.wait_ge(aux_ready, turn + 1)
                if name[:3] == "ytr":
                    g = int(name[-1])
                    ps = aux[:, :].rearrange("p (t h d) -> p t h d", t=TT, h=4)
                    v.reciprocal(recips[:], ps[:, :, :, D]).then_inc(y_recip, 1)
                    dve.wait_ge(y_recip, 4 * b + g + 1)
                    v.tensor_tensor(y_tok[:, :, 4 * D * g:4 * D * (g + 1)].rearrange("p t (h d) -> p t h d", h=4),
                                    ps[:, :, :, 0:D], recips[:].unsqueeze(3).to_broadcast([P, TT, 4, D]), ALU.mult
                                    ).then_inc(aux_free, 1)
                elif name[:2] == "pr":
                    i = int(name[-1])
                    dve.wait_ge(x1_kept, 16 * (bb + 1))
                    v.tensor_tensor(x1[:, 2 * i:2 * i + 2, :], aux[:, :].rearrange("p (u c) -> p u c", u=2),
                                    gab[:, 0:C].unsqueeze(1).to_broadcast([P, 2, C]), ALU.mult).then_inc(aux_free, 1)
                elif name == "lg":
                    router_choice(bb, turn)
                elif name == "pos":
                    router_slots(bb, turn)
                elif name == "gab":
                    if kind != "first":
                        dve.wait_ge(gb_kept, 16 * b)
                    v.tensor_scalar(g_sgn[:], aux[:, :], 0.0, 2.0, ALU.is_ge, ALU.mult).then_inc(sign_done, 1)
                    dve.wait_ge(sign_done, 3 * b + 1)
                    v.tensor_scalar(g_sgn[:], g_sgn[:], -1.0, None, ALU.add).then_inc(sign_done, 1)
                    dve.wait_ge(sign_done, 3 * b + 2)
                    v.tensor_tensor(gab[:], g_sgn[:], aux[:, :], ALU.mult).then_inc(sign_done, 1)
                    dve.wait_ge(sign_done, 3 * b + 3)
                    v.scalar_tensor_tensor(out=gab[:], in0=gab[:], scalar=0.25, in1=g_sgn[:], op0=ALU.max, op1=ALU.mult
                                           ).then_inc(gab_done, 1)
                    dve.wait_ge(gab_done, b + 1)
                    dve.sem_inc(aux_free, 1)

            dve.sem_inc(carried, 1)
            for m in range(2):
                v.memset(q_st[m][:].bitcast(F32), 0.0).then_inc(cleared, 1)
                v.memset(v_sb[m][:], 1.0).then_inc(cleared, 1)
            ln_stats(0, 1, xin, x_in, 16)
            for name in AUX_PRO:
                task("pro", 0, name)

            def body(kind, b):
                for i in range(STEPS):
                    if i < H:
                        for j in TILE_ORDER:
                            slot, col = TILE_AT[j]
                            w = (j + 1) * P
                            s = s_bank[(3 * i + slot) % 4][:, col:col + w]
                            if j != 0:
                                dve.wait_ge(scored, 3 * H * b + 3 * i + slot + 1)
                                dve.nop(nofuse=True)
                            v.tensor_tensor_reduce(s, s, k.bias_w[:, i, T - w:T], -1.0, BIG, ALU.add, ALU.min,
                                                   neg_max[:, i % 4, j:j + 1]).then_inc(biased, 1)
                    if 1 <= i <= H:
                        h = i - 1
                        if h >= 8:
                            dve.wait_ge(pv_done, 4 * b + h // 4 - 1)
                        for slot in (0, 2):
                            at, w = TR_SLOT[slot]
                            dve.wait_ge(transposed, 3 * H * b + 3 * h + slot + 1)
                            v.tensor_copy(probs_t[:, h % 8, at:at + w], t_bank[(3 * h + slot) % 2][:, 0:w]).then_inc(pt_dve, 1)
                    if i == 2 and kind != "last":
                        ln_stats(0, b + 2, xin, x_in, 16 * (b + 2))
                    if i == 8 and kind != "first":
                        ln_stats(1, b, x1, x1_done, b)
                    for name in step_tasks(kind, i):
                        task(kind, b, name)

            each_batch(dve, body)
            for name in POST:
                if name == "h2T0":
                    ln_stats(1, B, x1, x1_done, B)
                task("end", B, name)

        @block.gpsimd
        def _(pool):
            g = nc.gpsimd

            def normalise(i, n, src, dst):
                pool.wait_ge(mv_done[i], n)
                pool.nop(nofuse=True)
                g.tensor_scalar(var[i][:], mv[i][:, :, 1], EPS, None, ALU.add).then_inc(var_done[i], 1)
                pool.wait_ge(var_done[i], n)
                pool.nop(nofuse=True)
                g.tensor_tensor(rstd[i][:], var[i][:], k.neghalf[:], ALU.pow).then_inc(rstd_done[i], 1)
                pool.wait_ge(rstd_done[i], n)
                pool.nop(nofuse=True)
                for tt in range(TT):
                    ins = g.tensor_scalar(dst[:, tt, :], src[:, tt, :], mv[i][:, tt, 0:1], rstd[i][:, tt:tt + 1],
                                          ALU.subtract, ALU.mult)
                ins.then_inc(normed[i], 1)

            def set_mod_b(b):
                g.tensor_copy(mod_b[:].unsqueeze(3), k.mod_c[:, :, :, bass.ds(b, 1)]).then_inc(mod_b_set, 1)

            def after(kind, b):
                p = b - 1
                pool.wait_ge(aux_free, turn_of(kind, b, "pr1") + 1)
                pool.wait_ge(xr_in, 16 * (p + 1))
                g.tensor_tensor(x1[:], x1[:], xr[:], ALU.add).then_inc(x1_done, 1)
                pool.wait_ge(x1_done, p + 1)
                normalise(1, p + 1, x1, h2)
                pool.wait_ge(normed[1], p + 1)
                g.tensor_tensor(h2[:], h2[:], csb[:, C:2 * C].unsqueeze(1).to_broadcast([P, TT, C]), ALU.mult
                                ).then_inc(h2_scaled, 1)
                pool.wait_ge(h2_scaled, p + 1)
                g.tensor_tensor(h2[:], h2[:], csb[:, 0:C].unsqueeze(1).to_broadcast([P, TT, C]), ALU.add
                                ).then_inc(h2_done, 1)
                pool.wait_ge(h2_done, p + 1)
                pool.wait_ge(slot_done, p + 1)
                pool.wait_ge(g2_done, p + 1)
                pool.nop(nofuse=True)
                g.tensor_copy(k.slots_all[:, bass.ds(p, 1), :], slot_b[:].unsqueeze(1))
                g.tensor_copy(k.gates_all[:, bass.ds(p, 1), :], gates[:].rearrange("p n t -> p (n t)").unsqueeze(1)
                              ).then_inc(sb_done, 1)
                pool.wait_ge(sb_done, p + 1)
                pool.nop(nofuse=True)
                for n in range(2 * TT):
                    g.indirect_dma_start(rows_d, bass.IndirectOffsetOnAxis(ap=slot_b[:, n:n + 1].bitcast(U32), axis=0),
                                         h2[:, n % TT, :], None).then_inc(scattered, 16)
                pool.wait_ge(scattered, 16 * 2 * TT * (p + 1))
                pool.sem_inc(rows_free, 1)

            pool.sem_inc(rows_free, 1)
            normalise(0, 1, xin, xin)
            set_mod_b(0)

            def body(kind, b):
                pool.wait_ge(aux_free, start_turn(kind, b))
                pool.nop(nofuse=True)
                if kind != "last":
                    set_mod_b(b + 1)
                g.tensor_copy(scb[:], k.sc[:, :, bass.ds(b, 1)].to_broadcast([P, KC, P])).then_inc(scb_set, 1)
                if kind != "last":
                    normalise(0, b + 2, xin, xin)
                if kind != "first":
                    after(kind, b)

            each_batch(pool, body)
            after("end", B)
def experts(nc, sem, w1, w3, w2, a1, a3, a2, lb1, lb3, lb2, b1, b3, b2, rows_d, y_d, k):
    with ExitStack() as ctx:
        def sb(name, shape, dt=F32):
            return ctx.enter_context(nc.sbuf_tensor(name, shape, dt))

        raw = [sb(f"raw{i}", [P, 6, HID]) for i in range(2)]
        w_hi = [sb(f"w_hi{i}", [P, 6, HID], F32R) for i in range(2)]
        w_lo = [sb(f"w_lo{i}", [P, 6, HID], F32R) for i in range(2)]
        a_diag = sb("a_diag", [P, E, 2 * C + HID])
        lb_all = sb("lb_all", [P, 2 * HID + C])
        b13 = sb("b13", [P, 2, E, HK])
        b2_rows = sb("b2_rows", [P, E, C])
        tile_in = sb("tile_in", [P, 2, C])
        x_hi = sb("x_hi", [P, KC, FT], F32R)
        x_lo = sb("x_lo", [P, KC, FT], F32R)
        silu = sb("silu", [P, HK, FT])
        g_full = sb("g_full", [P, HK, FT])
        g_hi = sb("g_hi", [P, HK, FT], F32R)
        g_lo = sb("g_lo", [P, HK, FT], F32R)
        y_sb = sb("y_sb", [P, 2, C])
        zeros = sb("zeros", [P, 2, C])
        cnt = sb("cnt", [P, E], I32)
        cnt_up = sb("cnt_up", [P, E], I32)
        cnt_sh = sb("cnt_sh", [P, E], I32)
        n_tiles = sb("n_tiles", [P, E], I32)
        h_bank = [ctx.enter_context(nc.psum_tensor(f"h_bank{i}", [P, 512], F32)) for i in range(4)]
        yb = [ctx.enter_context(nc.psum_tensor(f"yb{i}", [P, 512], F32)) for i in range(2)]
        turn_bank = ctx.enter_context(nc.psum_tensor("turn_bank", [P, 512], F32))
        cnt_bank = ctx.enter_context(nc.psum_tensor("cnt_bank", [P, 512], F32))

        lora_in, diag_clear, counted, cnt_read, cnt_done, padded = (
            sem(n) for n in ("lora_in", "diag_clear", "counted", "cnt_read", "cnt_done", "padded"))
        raw_in = [sem(f"raw_in{i}") for i in range(2)]
        folded, merged, split_hi, split_done = (sem(n) for n in ("folded", "merged", "split_hi", "split_done"))
        rows_in, turned, x_hi_done, x_split = (sem(n) for n in ("rows_in", "turned", "x_hi_done", "x_split"))
        h_ready, silu_ready, h_read, g_hi_done, g_split, y_ready, y_read, y_kept = (
            sem(n) for n in ("h_ready", "silu_ready", "h_read", "g_hi_done", "g_split", "y_ready", "y_read", "y_kept"))
        NRAW = 6
        NLORA = 6 + 3 * E

        def tile_counts(eng):
            eng.wait_ge(cnt_done, 4)
            n, base = [], [0]
            for e in range(E):
                n.append(eng.value_load(n_tiles[0:1, e:e + 1], min_val=1, max_val=B * T // FT))
                base.append(eng.snap(base[-1] + n[-1]))
            return n, base

        block = ctx.enter_context(nc.Block())

        @block.sync
        def _(sp):
            def load_weights(e):
                i = e % 2
                for kc in range(KC):
                    sp.dma_start(raw[i][:, kc, :], w1[e, kc * P:(kc + 1) * P, :]).then_inc(raw_in[i], 16)
                    sp.dma_start(raw[i][:, KC + kc, :], w3[e, kc * P:(kc + 1) * P, :]).then_inc(raw_in[i], 16)
                for j in range(2):
                    sp.dma_start(raw[i][:, 4 + j, :].rearrange("p (a c) -> p a c", a=2),
                                 w2[e, 2 * j * P:2 * (j + 1) * P, :].rearrange("(a p) c -> p a c", p=P)).then_inc(raw_in[i], 16)

            load_weights(0)
            for n, src in enumerate((b1, b3)):
                sp.dma_start(b13[:, n, :, :], src.rearrange("e (m p) -> p e m", p=P), allow_slow_non_contiguous=True
                             ).then_inc(lora_in, 16)
            sp.dma_start(b2_rows[:], b2.rearrange("e c -> (e c)").partition_broadcast(P).rearrange("p (e c) -> p e c", e=E)
                         ).then_inc(lora_in, 16)
            sp.dma_start(lb_all[:, 0:HID], lb1).then_inc(lora_in, 16)
            sp.dma_start(lb_all[:, HID:2 * HID], lb3).then_inc(lora_in, 16)
            sp.dma_start(lb_all[:, 2 * HID:2 * HID + C], lb2).then_inc(lora_in, 16)
            sp.wait_ge(diag_clear, 1)
            for e in range(E):
                rows = slice(R * e, R * (e + 1))
                for src, at, w in ((a1, 0, C), (a3, C, C), (a2, 2 * C, HID)):
                    sp.dma_start(a_diag[rows, e, at:at + w], src[rows, :]).then_inc(lora_in, 16)
            n, base = tile_counts(sp)
            for e in range(E):
                last = sp.value_load(cnt[0:1, e:e + 1], min_val=0, max_val=B * T)
                sp.dma_start(rows_d[bass.ds(last + e * REGION, FT), :].rearrange("(u p) c -> p u c", p=P), zeros[:]
                             ).then_inc(padded, 16)
            sp.wait_ge(padded, 16 * E)

            def load_rows(first_row, g):
                sp.wait_ge(turned, g + 1)
                sp.dma_start(tile_in[:], rows_d[bass.ds(first_row, FT), :].rearrange("(u p) c -> p u c", p=P)
                             ).then_inc(rows_in, 16)

            for e in range(E):
                if e + 1 < E:
                    if e:
                        sp.wait_ge(split_done, e)
                    load_weights(e + 1)
                with sp.Fori(0, n[e]) as i:
                    load_rows(i * FT + e * REGION, base[e] + i)
            load_rows(0, base[E])

        @block.tensor
        def _(pe):
            pe.matmul(cnt_bank[:, 0:E], k.ones[:], k.carry[:], start=True, stop=True).then_inc(counted, 1)

            def fold(e):
                if e == 0:
                    pe.wait_ge(lora_in, 16 * NLORA)
                if e >= 2:
                    pe.wait_ge(h_read, 4 * base[e - 1] + 4)
                for j in range(6):
                    if j >= 4 or e == 1:
                        pe.wait_ge(merged, max(6 * e + j - 3, 1) if j >= 4 else 6)
                    bank = h_bank[j % 4]
                    if j < 4:
                        mm = pe.matmul(bank[:, :], a_diag[:, e, j * P:(j + 1) * P], lb_all[:, (j // 2) * HID:(j // 2 + 1) * HID],
                                       start=True, stop=True)
                    else:
                        for u in range(2):
                            mc = 2 * (j - 4) + u
                            mm = pe.matmul(bank[:, u * C:(u + 1) * C], a_diag[:, e, 2 * C + mc * P:2 * C + (mc + 1) * P],
                                           lb_all[:, 2 * HID:2 * HID + C], start=True, stop=True)
                    mm.then_inc(folded, 1)

            def turn():
                for u in range(2):
                    for kc in range(KC):
                        mm = pe.transpose(turn_bank[:, kc * FT + u * P:kc * FT + (u + 1) * P],
                                          tile_in[:, u, kc * P:(kc + 1) * P], k.ident[:])
                mm.then_inc(turned, 1)

            pe.sem_inc(turned, 1)
            pe.sem_inc(y_ready, 1)
            n, base = tile_counts(pe)
            fold(0)
            pe.wait_ge(rows_in, 16)
            turn()
            for e in range(E):
                if e + 1 < E:
                    fold(e + 1)
                    pe.wait_ge(merged, 6 * (e + 2))
                pe.wait_ge(split_done, e + 1)
                hi, lo = w_hi[e % 2], w_lo[e % 2]
                with pe.Fori(0, n[e]) as i:
                    g = base[e] + i
                    pe.wait_ge(x_split, g + 1)
                    for m in range(HK):
                        pe.wait_ge(h_read, 4 * g + (m + 1))
                        for which in range(2):
                            parts = [(kc, w, xs) for kc in range(KC) for w, xs in ((hi, x_hi), (hi, x_lo), (lo, x_hi))]
                            for q, (kc, w, xs) in enumerate(parts):
                                mm = pe.matmul(h_bank[m][:, which * FT:(which + 1) * FT], w[:, 2 * which + kc, m * P:(m + 1) * P],
                                               xs[:, kc, :], start=(q == 0), stop=(q == len(parts) - 1))
                        mm.then_inc(h_ready, 1)
                    pe.wait_ge(rows_in, 16 * g + 32)
                    turn()
                    pe.wait_ge(y_read, g + 1)
                    for m in range(HK):
                        pe.wait_ge(g_split, 4 * g + (m + 1))
                        for u in range(2):
                            for q, (gs, w) in enumerate(((g_hi, hi), (g_lo, hi), (g_hi, lo))):
                                mm = pe.matmul(yb[u][:, 0:C], gs[:, m, u * P:(u + 1) * P],
                                               w[:, 4 + m // 2, (m % 2) * C:(m % 2 + 1) * C],
                                               start=(m == 0 and q == 0), stop=(m == HK - 1 and q == 2))
                    mm.then_inc(y_ready, 1)

        @block.scalar
        def _(act):
            n, base = tile_counts(act)

            def take_high(g):
                act.wait_ge(turned, g + 2)
                nc.scalar.copy(x_hi[:], turn_bank[:, :].rearrange("p (k t) -> p k t", k=KC)).then_inc(x_hi_done, 1)

            take_high(0)
            act.wait_ge(lora_in, 16 * NLORA)
            for e in range(E):
                with act.Fori(0, n[e]) as i:
                    g = base[e] + i
                    for m in range(HK + 1):
                        if m < HK:
                            act.wait_ge(h_ready, 4 * g + (m + 1))
                            act.wait_ge(h_read, 4 * g + (m + 1))
                            nc.scalar.activation(silu[:, m, :], h_bank[m][:, 0:FT], ACT.Silu, bias=b13[:, 0, e, m:m + 1]
                                                 ).then_inc(silu_ready, 1)
                        if m:
                            if m == 1:
                                act.wait_ge(y_ready, g + 1)
                            act.wait_ge(h_read, 4 * g + (m + 4))
                            nc.scalar.copy(g_hi[:, m - 1, :], g_full[:, m - 1, :]).then_inc(g_hi_done, 1)
                    take_high(g + 1)
                    act.wait_ge(y_read, g + 2)
                    act.dma_start(y_d[bass.ds(i * FT + e * REGION, FT), :].rearrange("(u p) c -> p u c", p=P), y_sb[:]
                                  ).then_inc(y_kept, 16)
            act.wait_ge(y_kept, 16 * base[E] + 16)
            act.nop(nofuse=True)

        @block.vector
        def _(dve):
            v = nc.vector
            v.memset(zeros[:], 0.0)
            v.memset(a_diag[:], 0.0).then_inc(diag_clear, 1)
            dve.wait_ge(counted, 1)
            v.tensor_copy(cnt[:], cnt_bank[:, 0:E])
            v.tensor_scalar(cnt_up[:], cnt_bank[:, 0:E], float(FT - 1), None, ALU.add).then_inc(cnt_done, 1)
            dve.wait_ge(cnt_done, 1)
            v.tensor_scalar(cnt_sh[:], cnt_up[:], FT.bit_length() - 1, None, ALU.logical_shift_right).then_inc(cnt_done, 1)
            dve.wait_ge(cnt_done, 2)
            v.tensor_scalar(n_tiles[:], cnt_sh[:], 1.0, None, ALU.max).then_inc(cnt_done, 1)
            dve.wait_ge(cnt_done, 3)
            dve.sem_inc(cnt_done, 1)
            dve.sem_inc(h_read, 4)
            dve.sem_inc(y_read, 1)
            dve.sem_inc(y_kept, 16)
            n, base = tile_counts(dve)

            def merge(e):
                dve.wait_ge(raw_in[e % 2], 16 * NRAW * (e // 2 + 1))
                for j in range(6):
                    dve.wait_ge(folded, 6 * e + j + 1)
                    v.tensor_tensor(raw[e % 2][:, j, :], raw[e % 2][:, j, :], h_bank[j % 4][:, :], ALU.add).then_inc(merged, 1)

            def take_low(g):
                dve.wait_ge(x_hi_done, g + 1)
                v.tensor_tensor(x_lo[:], turn_bank[:, :].rearrange("p (k t) -> p k t", k=KC), x_hi[:].bitcast(F32),
                                ALU.subtract).then_inc(x_split, 1)

            merge(0)
            take_low(0)
            for e in range(E):
                if e + 1 < E:
                    merge(e + 1)
                with dve.Fori(0, n[e]) as i:
                    g = base[e] + i
                    for m in range(HK + 1):
                        if m < HK:
                            dve.wait_ge(silu_ready, 4 * g + (m + 1))
                            v.scalar_tensor_tensor(out=g_full[:, m, :], in0=h_bank[m][:, FT:2 * FT], scalar=b13[:, 1, e, m:m + 1],
                                                   in1=silu[:, m, :], op0=ALU.add, op1=ALU.mult).then_inc(h_read, 1)
                        if m:
                            dve.wait_ge(g_hi_done, 4 * g + m)
                            v.tensor_tensor(g_lo[:, m - 1, :], g_full[:, m - 1, :], g_hi[:, m - 1, :].bitcast(F32), ALU.subtract
                                            ).then_inc(g_split, 1)
                    take_low(g + 1)
                    dve.wait_ge(y_kept, 16 * g + 16)
                    dve.wait_ge(y_ready, g + 2)
                    for u in range(2):
                        ins = v.tensor_tensor(y_sb[:, u, :], yb[u][:, 0:C], b2_rows[:, e, :], ALU.add)
                    ins.then_inc(y_read, 1)

        @block.gpsimd
        def _(pool):
            g = nc.gpsimd
            n, base = tile_counts(pool)
            for e in range(E):
                i = e % 2
                pool.wait_ge(merged, 6 * (e + 1))
                if e >= 2:
                    pool.wait_ge(y_ready, base[e - 1] + 1)
                    pool.nop(nofuse=True)
                for j in range(6):
                    ins = g.tensor_copy(w_hi[i][:, j, :], raw[i][:, j, :])
                ins.then_inc(split_hi, 1)
                pool.wait_ge(split_hi, e + 1)
                for j in range(6):
                    ins = g.tensor_tensor(w_lo[i][:, j, :], raw[i][:, j, :], w_hi[i][:, j, :].bitcast(F32), ALU.subtract)
                ins.then_inc(split_done, 1)


def combine(nc, sem, x1_d, y_d, gb_d, out, k):
    with ExitStack() as ctx:
        def sb(name, shape, dt=F32):
            return ctx.enter_context(nc.sbuf_tensor(name, shape, dt))

        slots = [sb(f"slots{i}", [P, 2 * TT], I32) for i in range(2)]
        gates = [sb(f"gates_of{i}", [P, 2 * TT]) for i in range(2)]
        y12 = [sb(f"y12_{i}", [P, 2, TT, C]) for i in range(2)]
        gb_row = [sb(f"gb_row{i}", [P, C]) for i in range(2)]
        x1 = [sb(f"x1_of{i}", [P, TT, C]) for i in range(2)]
        first = [sb(f"first{i}", [P, TT, C]) for i in range(2)]
        mixed = sb("mixed", [P, TT, C])
        scaled = sb("scaled_mix", [P, TT, C])
        res = [sb(f"res{i}", [P, TT, C]) for i in range(2)]
        taken = sem("taken")
        got, x1_in, res_done, res_kept = ([sem(f"{n}{i}") for i in range(2)] for n in ("got", "x1_in", "res_done", "res_kept"))
        weighted, mix_done, mix_scaled = (sem(n) for n in ("weighted", "mix_done", "mix_scaled"))
        block = ctx.enter_context(nc.Block())

        @block.gpsimd
        def _(pool):
            g = nc.gpsimd
            with pool.Fori(0, B // 2) as q:
                for i in range(2):
                    b = 2 * q + i
                    pool.wait_ge(res_done[i], q + 1)
                    pool.nop(nofuse=True)
                    g.tensor_copy(slots[i][:].unsqueeze(1), k.slots_all[:, bass.ds(b, 1), :])
                    g.tensor_copy(gates[i][:].unsqueeze(1), k.gates_all[:, bass.ds(b, 1), :]).then_inc(taken, 1)
                    pool.wait_ge(taken, b + 1)
                    pool.nop(nofuse=True)
                    for n in range(2 * TT):
                        g.indirect_dma_start(y12[i][:, n // TT, n % TT, :], None, y_d,
                                             bass.IndirectOffsetOnAxis(ap=slots[i][:, n:n + 1].bitcast(U32), axis=0)
                                             ).then_inc(got[i], 16)

        @block.sync
        def _(sp):
            def load(b, i, q):
                sp.wait_ge(res_done[i], q + 1)
                sp.dma_start(x1[i][:], x1_d[b].rearrange("(t p) c -> p t c", p=P)).then_inc(x1_in[i], 16)
                sp.dma_start(gb_row[i][:], gb_d[bass.ds(b, 1), :].partition_broadcast(P)).then_inc(x1_in[i], 16)

            for i in range(2):
                sp.sem_inc(res_kept[i], 16)
            with sp.Fori(0, B // 2) as q:
                for i in range(2):
                    load(2 * q + i, i, q)
                for i in range(2):
                    sp.wait_ge(res_done[i], q + 2)
                    sp.dma_start(out[2 * q + i].rearrange("(t p) c -> p t c", p=P), res[i][:]).then_inc(res_kept[i], 16)
            for i in range(2):
                sp.wait_ge(res_kept[i], 16 * (B // 2 + 1))

        @block.scalar
        def _(act):
            with act.Fori(0, B // 2) as q:
                for i in range(2):
                    act.wait_ge(got[i], 128 * q + 128)
                    act.wait_ge(taken, 2 * q + (i + 1))
                    act.wait_ge(res_done[i], q + 1)
                    for tt in range(TT):
                        ins = nc.scalar.activation(first[i][:, tt, :], y12[i][:, 0, tt, :], ACT.Copy, scale=gates[i][:, tt:tt + 1])
                    ins.then_inc(weighted, 1)

        @block.vector
        def _(dve):
            v = nc.vector
            for i in range(2):
                dve.sem_inc(res_done[i], 1)
            with dve.Fori(0, B // 2) as q:
                for i in range(2):
                    b = 2 * q + i
                    dve.wait_ge(weighted, b + 1)
                    for tt in range(TT):
                        ins = v.scalar_tensor_tensor(out=mixed[:, tt, :], in0=y12[i][:, 1, tt, :],
                                                     scalar=gates[i][:, TT + tt:TT + tt + 1], in1=first[i][:, tt, :],
                                                     op0=ALU.mult, op1=ALU.add)
                    ins.then_inc(mix_done, 1)
                    dve.wait_ge(x1_in[i], 32 * q + 32)
                    dve.wait_ge(mix_done, b + 1)
                    v.tensor_tensor(scaled[:], mixed[:], gb_row[i][:].unsqueeze(1).to_broadcast([P, TT, C]), ALU.mult
                                    ).then_inc(mix_scaled, 1)
                    dve.wait_ge(mix_scaled, b + 1)
                    dve.wait_ge(res_kept[i], 16 * q + 16)
                    v.tensor_tensor(res[i][:], scaled[:], x1[i][:], ALU.add).then_inc(res_done[i], 1)
def build(nc, x, w_attn, b_qk, b_v, w_proj, b_proj, bias_table, onehot, wg, cT, wmod,
          w1, w3, w2, a1, a3, a2, lb1, lb3, lb2, b1, b3, b2, out):
    with ExitStack() as ctx:
        def dram(name, shape, dt=F32):
            return nc.dram_tensor(name, shape, dt, kind="Internal").ap()

        def sem(name):
            return ctx.enter_context(nc.semaphore(name))

        def sb(inner, name, shape, dt=F32):
            return inner.enter_context(nc.sbuf_tensor(name, shape, dt))

        line_d = dram("line_d", [H, LIN + 1])
        qk_d = [[dram(f"qk_d{i}{m}", [2, P, T]) for m in range(2)] for i in range(2)]
        x1_d = dram("x1_d", [B, T, C])
        rows_d = dram("rows_d", [E * REGION, C])
        y_d = dram("y_d", [E * REGION, C])
        gb_d = dram("gb_d", [B, C])
        k = Kept()
        k.ident = sb(ctx, "ident", [P, P])
        k.ones = sb(ctx, "ones", [P, P])
        k.carry = sb(ctx, "carry", [P, E])
        k.slots_all = sb(ctx, "slots_all", [P, B, 2 * TT], I32)
        k.gates_all = sb(ctx, "gates_all", [P, B, 2 * TT])
        with ExitStack() as inner:
            k.before = sb(inner, "before", [P, P])
            k.iota_e = sb(inner, "iota_e", [P, TT, E])
            k.region = sb(inner, "region", [P, TT, E])
            k.neghalf = sb(inner, "neghalf", [P, TT])
            k.bias_w = sb(inner, "bias_w", [P, H, T])
            k.wa = sb(inner, "wa", [P, KC, 3 * C])
            k.wp = sb(inner, "wp", [P, KC, C])
            k.wg_sb = sb(inner, "wg_sb", [P, KC, E])
            k.bqk = sb(inner, "bqk", [P, 2 * KC])
            k.bp_row = sb(inner, "bp_row", [1, C])
            k.sc = sb(inner, "sc", [P, KC, B])
            k.wm_rows = sb(inner, "wm_rows", [P, KC, 4, C])
            k.mod_c = sb(inner, "mod_c", [P, 2, KC, B])
            setup(nc, sem, w_attn, b_qk, b_v, w_proj, b_proj, bias_table, onehot, wg, cT, wmod, line_d, k)
            attention(nc, sem, x, qk_d, x1_d, rows_d, gb_d, k)
        with ExitStack() as inner:
            blank = sb(inner, "blank", [P, C])
            blank_set, blank_out = sem("blank_set"), sem("blank_out")
            with nc.Block() as block:
                @block.vector
                def _(dve):
                    nc.vector.memset(blank[:], 0.0).then_inc(blank_set, 1)

                @block.sync
                def _(sp):
                    sp.wait_ge(blank_set, 1)
                    for e in range(E):
                        sp.dma_start(y_d[e * REGION:(e + 1) * REGION, :].rearrange("(a p) c -> p a c", p=P),
                                     blank[:].unsqueeze(1).to_broadcast([P, REGION // P, C])).then_inc(blank_out, 16)
                    sp.wait_ge(blank_out, 16 * E)
        experts(nc, sem, w1, w3, w2, a1, a3, a2, lb1, lb3, lb2, b1, b3, b2, rows_d, y_d, k)
        combine(nc, sem, x1_d, y_d, gb_d, out, k)


def kernel(L0_attn_x, L0_attn_W_attn, L0_attn_b_attn, L0_attn_W_proj, L0_attn_b_proj, L0_attn_bias_table,
           L0_ffn_Wg, L0_ffn_W1, L0_ffn_b1, L0_ffn_A1, L0_ffn_B1, L0_ffn_W2, L0_ffn_b2, L0_ffn_A2, L0_ffn_B2,
           L0_ffn_W3, L0_ffn_b3, L0_ffn_A3, L0_ffn_B3, L0_c, L0_wmod):
    from concourse import bacc
    from concourse.bass_utils import run_bass_kernel_spmd

    def t(a, *axes):
        return np.transpose(np.asarray(a), axes)

    arrays = dict(
        x=L0_attn_x, w_attn=L0_attn_W_attn, b_qk=L0_attn_b_attn[:2 * C], b_v=L0_attn_b_attn[2 * C:],
        w_proj=L0_attn_W_proj, b_proj=L0_attn_b_proj, bias_table=L0_attn_bias_table, onehot=constants(),
        wg=t(L0_ffn_Wg, 1, 0), cT=t(L0_c, 1, 0), wmod=L0_wmod,
        w1=t(L0_ffn_W1, 0, 2, 1), w3=t(L0_ffn_W3, 0, 2, 1), w2=t(L0_ffn_W2, 0, 2, 1),
        a1=np.reshape(L0_ffn_A1, (E * R, C)), a3=np.reshape(L0_ffn_A3, (E * R, C)), a2=np.reshape(L0_ffn_A2, (E * R, HID)),
        lb1=t(L0_ffn_B1, 0, 2, 1).reshape(E * R, HID), lb3=t(L0_ffn_B3, 0, 2, 1).reshape(E * R, HID),
        lb2=t(L0_ffn_B2, 0, 2, 1).reshape(E * R, C), b1=L0_ffn_b1, b3=L0_ffn_b3, b2=L0_ffn_b2)
    arrays = {f"in_{name}": np.ascontiguousarray(a) for name, a in arrays.items()}
    nc = bacc.Bacc("TRN2", target_bir_lowering=False, num_devices=1)
    args = {name[3:]: nc.dram_tensor(name, a.shape, mybir.dt.from_np(a.dtype), kind="ExternalInput").ap()
            for name, a in arrays.items()}
    out = nc.dram_tensor("out_x", [B, T, C], F32, kind="ExternalOutput").ap()
    build(nc, out=out, **args)
    result = run_bass_kernel_spmd(nc, [arrays], core_ids=[0])
    return result.results[0]["out_x"]
```

```python
from contextlib import ExitStack

import numpy as np

import concourse.bass as bass
from concourse import mybir

F32 = mybir.dt.float32
F32R = mybir.dt.float32r
I32 = mybir.dt.int32
U32 = mybir.dt.uint32
ALU = mybir.AluOpType
ACT = mybir.ActivationFunctionType
AX = mybir.AxisListType

P = 128
B, T, C = 8, 512, 256
H = 16
D = C // H
E, R, HID = 8, 16, 512
TT = T // P
KC = C // P
HK = HID // P
HH = H // 2
NBUCKET = 32
EPS = 1e-5
MASKED = -1e30
LIN = T + P - 1
FT = 256
REGION = B * T + 2 * FT
BIG = 3e38

TILE_ORDER = [3, 2, 0, 1]
TILE_AT = {3: (0, 0), 2: (1, 0), 0: (1, 384), 1: (2, 0)}
EXPS_AFTER_SLOT = [1, 3, 4]
P_AT = {3: 0, 2: 512, 1: 896, 0: 1152}
TR_AT = {0: (0, 0), 1: (1, 0), 3: (1, 384), 2: (2, 0)}
PT_AT = {0: 0, 1: 512, 3: 896, 2: 1024}
TR_SLOT = [(0, 512), (512, 512), (1024, 256)]
NPROB = 1280

STEPS = H
AUX_PRO = ["hT0", "hT1", "q", "k"]
AUX_MID = {0: "q1", 1: "k1", 2: "ytr2", 3: "v0", 5: "v1", 6: "ytr3", 7: "yT1", 9: "hT0", 10: "q", 11: "k",
           12: "ytr0", 13: "h2T0", 14: "lg", 15: "pos"}
AUX_END = {6: "yT0", 7: "pr0", 8: "pr1", 9: "hT1", 13: "h2T1", 14: "ytr1"}
POST = ["ytr2", "ytr3", "yT0", "yT1", "pr0", "pr1", "h2T0", "h2T1", "lg", "pos"]
AHEAD = ["hT0", "hT1", "q", "k"]
LONG = ["q", "k", "q1", "k1", "v0", "v1", "pr0", "pr1", "lg", "pos"]
LAG = 2
PV_PARTS = [[0], [1], [2, 3]]
PV_AT = {6: (0, 0, 0), 7: (0, 0, 1), 8: (0, 0, 2), 10: (0, 1, 0), 11: (0, 1, 1), 12: (0, 1, 2),
         14: (0, 2, 0), 15: (0, 2, 1), 0: (1, 2, 2), 2: (1, 3, 0), 3: (1, 3, 1), 4: (1, 3, 2)}


def step_tasks(kind, i, places=(AUX_MID, AUX_END)):
    names = [place[i] for place in places if i in place]
    if kind == "end":
        return [t for t in names if t in POST]
    skip = POST if kind == "first" else AHEAD if kind == "last" else []
    return [t for t in names if t not in skip]


def reads_of(kind, i, place):
    here = step_tasks(kind, i, [(AUX_MID, AUX_END)[place]])
    before = step_tasks(kind, i, [AUX_MID]) if place else step_tasks(kind, i - 1, [AUX_END])
    return [t for t in before if t in LONG] + [t for t in here if t not in LONG]


def tasks(kind):
    return [t for i in range(STEPS) for t in step_tasks(kind, i)]


def start_turn(kind, b):
    pro, first, loop, last = len(AUX_PRO), len(tasks("first")), len(tasks("loop")), len(tasks("last"))
    if kind == "pro":
        return 0
    if kind == "first":
        return pro
    if kind == "loop":
        return b * loop + (pro + first - loop)
    return pro + first + (B - 2) * loop + (last if kind == "end" else 0)


def turn_of(kind, b, name):
    names = AUX_PRO if kind == "pro" else tasks(kind)
    return start_turn(kind, b) + names.index(name)


def transposed_head(kind, b, i):
    if i >= LAG:
        return None if kind == "end" else (b, i - LAG)
    return None if kind == "first" else (b - 1, H - LAG + i)


def values_part(kind, b, i):
    if i not in PV_AT:
        return None
    back, g, part = PV_AT[i]
    if (back and kind == "first") or (not back and kind == "end"):
        return None
    return b - back, g, part


def each_batch(eng, body):
    body("first", 0)
    with eng.Fori(1, B - 1) as b:
        body("loop", b)
    body("last", B - 1)
    body("end", B)


def constants():
    v = np.arange(LIN)
    dist = (T - P) + (P - 1) - v
    rp = np.maximum(dist, 0)
    max_exact = NBUCKET // 2
    large = max_exact + (np.log(np.maximum(rp, 1).astype(np.float32) / np.float32(max_exact))
                         / np.float32(np.log(128 / max_exact)) * np.float32(NBUCKET - max_exact)).astype(np.int32)
    bucket = np.where(rp < max_exact, rp, np.minimum(large, NBUCKET - 1))
    bucket = np.where(dist < 0, NBUCKET, bucket)
    onehot = np.zeros((NBUCKET + 1, LIN), np.float32)
    onehot[bucket, v] = 1.0
    return onehot


def setup(nc, sem, w_attn, b_qk, b_v, w_proj, b_proj, bias_table, onehot, wg, cT, wmod, mod_d, k):
    with ExitStack() as ctx:
        def sb(name, shape, dt=F32):
            return ctx.enter_context(nc.sbuf_tensor(name, shape, dt))

        table = sb("table", [NBUCKET + 1, H])
        oh_line = sb("oh_line", [NBUCKET + 1, LIN])
        c_raw = sb("c_raw", [P, KC, B])
        wmod_cols = sb("wmod_cols", [P, KC, 2 * C])
        bv_col = sb("bv_col", [P, KC])
        wm_rows = sb("wm_rows", [P, KC, 4, C])
        sign = sb("sign", [B, 2, C])
        mod_rows = sb("mod_rows", [B, 4, C])
        mod_g = mod_rows[:, 0:4:3, :]
        token_i = sb("token_i", [P, TT], I32)
        iota_i = sb("iota_i", [P, TT, E], I32)
        region_i = sb("region_i", [P, TT, E], I32)
        line_ps = ctx.enter_context(nc.psum_tensor("line_ps", [P, 2, 512], F32))
        mod_ps = ctx.enter_context(nc.psum_tensor("mod_ps", [P, 512], F32))
        row_ps = ctx.enter_context(nc.psum_tensor("row_ps", [P, 2, 512], F32))
        bv_ps = ctx.enter_context(nc.psum_tensor("bv_ps", [P, 512], F32))
        loaded, masked, silu_done, line_made, rows_made, rows_step, rows_kept = (
            sem(n) for n in ("loaded", "masked", "silu_done", "line_made", "rows_made", "rows_step", "rows_kept"))
        mod_made, bv_made, scaled, ones_set, iotas, bp_step, g_signed = (
            sem(n) for n in ("mod_made", "bv_made", "scaled", "ones_set", "iotas", "bp_step", "g_signed"))
        block = ctx.enter_context(nc.Block())
        NLOAD = 10 + 4 * KC

        @block.sync
        def _(sp):
            sp.dma_start(table[0:NBUCKET, :], bias_table).then_inc(loaded, 16)
            sp.dma_start(oh_line[:], onehot).then_inc(loaded, 16)
            sp.dma_start(c_raw[:], cT.rearrange("(k p) b -> p k b", p=P)).then_inc(loaded, 16)
            sp.dma_start(wmod_cols[:], wmod[:, 0:2 * C].rearrange("(k p) n -> p k n", p=P)).then_inc(loaded, 16)
            sp.dma_start(k.wa[:], w_attn.rearrange("(k p) n -> p k n", p=P)).then_inc(loaded, 16)
            sp.dma_start(k.bqk[:], b_qk.rearrange("(m p) -> p m", p=P), allow_slow_non_contiguous=True).then_inc(loaded, 16)
            sp.dma_start(bv_col[:], b_v.rearrange("(m p) -> p m", p=P), allow_slow_non_contiguous=True).then_inc(loaded, 16)
            sp.dma_start(k.bp_row[:], b_proj.rearrange("(a n) -> a n", a=1)).then_inc(loaded, 16)
            sp.dma_start(k.wp[:], w_proj.rearrange("(k p) n -> p k n", p=P)).then_inc(loaded, 16)
            sp.dma_start(k.wg_sb[:], wg.rearrange("(k p) e -> p k e", p=P)).then_inc(loaded, 16)
            for kc in range(KC):
                for n, part in enumerate((2, 3, 4, 5)):
                    sp.dma_start(wm_rows[:, kc, n, :], wmod[kc * P:(kc + 1) * P, part * C:(part + 1) * C]
                                 ).then_inc(loaded, 16)
            sp.wait_ge(rows_step, 4)
            sp.dma_start(mod_d, mod_rows[:].rearrange("b n c -> b (n c)")).then_inc(rows_kept, 16)
            sp.wait_ge(rows_kept, 16)

        @block.tensor
        def _(pe):
            pe.wait_ge(loaded, 16 * NLOAD)
            pe.wait_ge(masked, 1)
            pe.matmul(line_ps[0:H, 0, :], table[:], oh_line[:, 0:512], start=True, stop=True).then_inc(line_made, 1)
            pe.matmul(line_ps[0:H, 1, 0:LIN - 512], table[:], oh_line[:, 512:LIN], start=True, stop=True
                      ).then_inc(line_made, 1)
            pe.wait_ge(silu_done, 1)
            for part in range(2):
                for m in range(KC):
                    col = (part * KC + m) * B
                    for kc in range(KC):
                        mm = pe.matmul(mod_ps[:, col:col + B], wmod_cols[:, kc, part * C + m * P:part * C + (m + 1) * P],
                                       k.sc[:, kc, :], start=(kc == 0), stop=(kc == KC - 1))
            mm.then_inc(mod_made, 1)
            for n in range(2):
                for kc in range(KC):
                    mm = pe.matmul(row_ps[0:B, n, :], k.sc[:, kc, :], wm_rows[:, kc, 2 * n:2 * n + 2, :].rearrange("p a n -> p (a n)"),
                                   start=(kc == 0), stop=(kc == KC - 1))
            mm.then_inc(rows_made, 1)
            for kc in range(KC):
                mm = pe.matmul(bv_ps[0:1, 0:C], bv_col[:, kc:kc + 1], k.wp[:, kc, :], start=(kc == 0), stop=(kc == KC - 1))
            mm.then_inc(bv_made, 1)

        @block.scalar
        def _(act):
            act.wait_ge(loaded, 16 * NLOAD)
            nc.scalar.activation(k.sc[:], c_raw[:], ACT.Silu).then_inc(silu_done, 1)
            nc.scalar.mul(k.wa[:, :, 0:C], k.wa[:, :, 0:C], D ** -0.5)
            nc.scalar.mul(k.bqk[:, 0:KC], k.bqk[:, 0:KC], D ** -0.5).then_inc(scaled, 1)
            act.wait_ge(line_made, 2)
            nc.scalar.copy(k.line[:, 0:512], line_ps[0:H, 0, :])
            nc.scalar.copy(k.line[:, 512:LIN], line_ps[0:H, 1, 0:LIN - 512])

        @block.vector
        def _(dve):
            v = nc.vector
            v.memset(table[NBUCKET:NBUCKET + 1, :], MASKED).then_inc(masked, 1)
            v.memset(k.carry[:], 0.0)
            v.memset(k.neghalf[:], -0.5)
            v.memset(k.to_next[:], float(T))
            dve.wait_ge(iotas, 3)
            v.tensor_copy(k.token[:], token_i[:])
            v.tensor_copy(k.iota_e[:], iota_i[:])
            v.tensor_copy(k.region[:], region_i[:])
            dve.wait_ge(mod_made, 1)
            v.tensor_copy(k.mod_c[:, 0, :, :], mod_ps[:, 0:KC * B].rearrange("p (k b) -> p k b", k=KC))
            v.tensor_scalar(k.mod_c[:, 1, :, :], mod_ps[:, KC * B:2 * KC * B].rearrange("p (k b) -> p k b", k=KC),
                            1.0, None, ALU.add)
            dve.wait_ge(bv_made, 1)
            v.tensor_tensor(k.bp_row[:], k.bp_row[:], bv_ps[0:1, 0:C], ALU.add).then_inc(bp_step, 1)
            v.memset(k.bp_parts[:].bitcast(F32), 0.0).then_inc(bp_step, 1)
            dve.wait_ge(bp_step, 2)
            v.tensor_copy(k.bp_parts[0:1, :], k.bp_row[:]).then_inc(bp_step, 1)
            dve.wait_ge(bp_step, 3)
            v.tensor_tensor(k.bp_parts[32:33, :], k.bp_row[:], k.bp_parts[0:1, :].bitcast(F32), ALU.subtract)
            dve.wait_ge(ones_set, 1)
            v.tensor_copy(k.ones_r[:], k.ones[:])
            dve.wait_ge(rows_made, 1)
            v.tensor_copy(mod_rows[:], row_ps[0:B, :, :].rearrange("b a (n c) -> b (a n) c", n=2)).then_inc(rows_step, 1)
            dve.wait_ge(rows_step, 1)
            v.tensor_scalar(mod_rows[:, 2, :], mod_rows[:, 2, :], 1.0, None, ALU.add)
            v.tensor_scalar(sign[:], mod_g, 0.0, 2.0, ALU.is_ge, ALU.mult).then_inc(rows_step, 1)
            dve.wait_ge(rows_step, 2)
            v.tensor_scalar(sign[:], sign[:], -1.0, None, ALU.add).then_inc(rows_step, 1)
            dve.wait_ge(rows_step, 3)
            v.tensor_tensor(mod_g, sign[:], mod_g, ALU.mult).then_inc(g_signed, 1)
            dve.wait_ge(g_signed, 1)
            v.scalar_tensor_tensor(out=mod_g, in0=mod_g, scalar=0.25, in1=sign[:], op0=ALU.max, op1=ALU.mult
                                   ).then_inc(rows_step, 1)

        @block.gpsimd
        def _(pool):
            g = nc.gpsimd
            g.iota(iota_i[:], [[0, TT], [1, E]], base=0, channel_multiplier=0).then_inc(iotas, 1)
            g.iota(region_i[:], [[0, TT], [REGION, E]], base=0, channel_multiplier=0).then_inc(iotas, 1)
            g.iota(token_i[:], [[P, TT]], base=-T, channel_multiplier=1).then_inc(iotas, 1)
            g.memset(k.ones[:], 1.0).then_inc(ones_set, 1)
            pool.wait_ge(ones_set, 1)
            g.affine_select(k.ident[:], k.ones[:], [[1, P]], ALU.is_equal, 0.0, base=0, channel_multiplier=-1)
            g.affine_select(k.before[:], k.ones[:], [[1, P]], ALU.is_gt, 0.0, base=0, channel_multiplier=-1)


class Kept:
    pass


def attention(nc, sem, x, line_d, qk_d, x1_d, rows_d, mod_d, k):
    with ExitStack() as ctx:
        def sb(name, shape, dt=F32):
            return ctx.enter_context(nc.sbuf_tensor(name, shape, dt))

        q_st = [sb(f"q_st{m}", [P, HH, T], F32R) for m in range(2)]
        k_st = [sb(f"k_st{m}", [P, HH // 2, T], F32R) for m in range(2)]
        v_sb = [sb(f"v_sb{m}", [P, TT, HH, 2 * D]) for m in range(2)]
        probs = [sb(f"probs{i}", [P, NPROB]) for i in range(4)]
        probs_t = sb("probs_t", [P, 8, NPROB])
        neg_max = sb("neg_max", [P, 4, TT])
        part_hi = [sb(f"part_hi{i}", [P, T], F32R) for i in range(2)]
        part_lo = [sb(f"part_lo{i}", [P, T], F32R) for i in range(2)]
        mod_b = sb("mod_b", [P, 2, KC])
        xin = sb("xin", [P, TT, C])
        h_t = sb("h_t", [P, KC, T])
        stats = [sb(f"stats{i}", [P, TT, 6]) for i in range(2)]
        mv = [sb(f"mv{i}", [P, TT, 2]) for i in range(2)]
        var = [sb(f"var{i}", [P, TT]) for i in range(2)]
        rstd = [sb(f"rstd{i}", [P, TT]) for i in range(2)]
        y_un = sb("y_un", [P, T])
        recips = sb("recips", [P, TT, 4])
        y_tok = sb("y_tok", [P, TT, C])
        y_t = sb("y_t", [P, KC, T])
        mod_row = sb("mod_row", [P, 3, C])
        rows = sb("rows", [P, TT, C + 2])
        h2 = rows[:, :, 0:C]
        x1 = sb("x1", [P, TT, C])
        h2_t = y_t
        logits = sb("logits", [P, TT, E])
        top8 = sb("top8", [P, TT, 8])
        idx8 = sb("idx8", [P, TT, 8], U32)
        idxf = sb("idxf", [P, 2, TT])
        chosen = sb("chosen", [P, 2, TT, E])
        both = sb("both", [P, TT, E])
        both_sum = sb("both_sum", [P, E])
        gap = sb("gap", [P, TT])
        gexp = sb("gexp", [P, TT])
        gden = sb("gden", [P, TT])
        gates = sb("gates", [P, 2, TT])
        place = sb("place", [P, TT, E])
        chosen_place = sb("chosen_place", [P, 2, TT, E])
        slot_f = sb("slot_f", [P, 2, TT])
        slot_b = sb("slot_b", [P, 2 * TT], I32)

        s_bank = [ctx.enter_context(nc.psum_tensor(f"s_bank{i}", [P, 512], F32)) for i in range(4)]
        t_bank = [ctx.enter_context(nc.psum_tensor(f"t_bank{i}", [P, 512], F32)) for i in range(2)]
        y_bank = ctx.enter_context(nc.psum_tensor("y_bank", [P, 512], F32))
        aux = ctx.enter_context(nc.psum_tensor("aux", [P, 512], F32))

        cleared = sem("cleared")
        x_in, xr_in, x1_kept, scattered, bias_in = (sem(n) for n in ("x_in", "xr_in", "x1_kept", "scattered", "bias_in"))
        lines_out = [sem(f"lines_out{i}") for i in range(4)]
        scored, biased, exped, transposed = (sem(n) for n in ("scored", "biased", "exped", "transposed"))
        pt_dve, pt_act, pv_done, y_copied, y_recip = (sem(n) for n in ("pt_dve", "pt_act", "pv_done", "y_copied", "y_recip"))
        aux_ready, aux_free, hi_done = (sem(n) for n in ("aux_ready", "aux_free", "hi_done"))
        stored = [sem(f"stored{i}") for i in range(2)]
        stacked = [sem(f"stacked{i}") for i in range(2)]
        stats_done, mv_done, var_done, rstd_done, normed = (
            [sem(f"{n}{i}") for i in range(2)] for n in ("stats_done", "mv_done", "var_done", "rstd_done", "normed"))
        mod_b_set, x1_done, h2_scaled, h2_done, rows_named, rows_free = (
            sem(n) for n in ("mod_b_set", "x1_done", "h2_scaled", "h2_done", "rows_named", "rows_free"))
        top_done, idx_done, idxf_done, chosen_done, both_done, summed, carried, gap_done, exp_done, den_done, g1_done, g2_done = (
            sem(n) for n in ("top_done", "idx_done", "idxf_done", "chosen_done", "both_done", "summed", "carried",
                             "gap_done", "exp_done", "den_done", "g1_done", "g2_done"))
        weighed, slot_f_done, slot_done, kept = (sem(n) for n in ("weighed", "slot_f_done", "slot_done", "kept"))

        def nth_part(kind, b, name):
            return 1 if kind == "pro" else 2 * b + (2 if name[1:] else 3)

        block = ctx.enter_context(nc.Block())

        @block.sync
        def _(sp):
            def load_x(b):
                sp.dma_start(xin[:], x[b].rearrange("(t p) c -> p t c", p=P)).then_inc(x_in, 16)

            def stack(kind, b, name):
                i, m = (0 if name[0] == "q" else 1), (1 if name[1:] else 0)
                sp.wait_ge(aux_free, turn_of(kind, b, name) + 1)
                d = qk_d[i][m]
                n = nth_part(kind, b, name)
                sp.dma_start(d[0], part_hi[i][:].bitcast(F32)).then_inc(stored[i], 16)
                sp.dma_start(d[1], part_lo[i][:].bitcast(F32)).then_inc(stored[i], 16)
                sp.wait_ge(stored[i], 32 * n)
                for hh in range(2):
                    for blk in range(4):
                        part = blk % 2 if i == 0 else blk // 2
                        rows = slice(64 * hh + D * blk, 64 * hh + D * (blk + 1))
                        src = d[part].rearrange("(r a d) t -> a d r t", a=2, d=D)[hh]
                        dst = (q_st[m][rows, hh:HH:2, :] if i == 0 else k_st[m][rows, :, :]).bitcast(F32)
                        sp.dma_start(dst, src).then_inc(stacked[i], 16)

            def load_residual(p):
                sp.wait_ge(rows_free, p + 1)
                sp.dma_start(h2, x[p].rearrange("(t p) c -> p t c", p=P)).then_inc(xr_in, 16)
                sp.dma_start(mod_row[:].rearrange("p n c -> p (n c)"),
                             mod_d[bass.ds(p, 1), 0:3 * C].partition_broadcast(P)).then_inc(xr_in, 16)

            def keep_x1(p):
                sp.wait_ge(x1_done, p + 1)
                sp.dma_start(x1_d[p].rearrange("(t p) c -> p t c", p=P), x1[:]).then_inc(x1_kept, 16)

            def load_bias(g):
                heads = slice(4 * g, 4 * g + 4)
                sp.dma_start(line_d[heads, :, 0:LIN], k.line[heads, :].unsqueeze(1).to_broadcast([4, P, LIN])).then_inc(lines_out[g], 16)
                sp.wait_ge(lines_out[g], 16)
                skewed = line_d[heads].rearrange("h r u -> h (r u)")[:, P - 1:P - 1 + P * LIN].rearrange("h (p u) -> p h u", u=LIN)
                sp.dma_start(k.bias_w[:, heads, :], skewed[:, :, 0:T]).then_inc(bias_in, 16)

            sp.sem_inc(x1_kept, 16)
            load_x(0)
            load_bias(0)
            sp.wait_ge(cleared, 4)
            stack("pro", 0, "q")
            stack("pro", 0, "k")
            for g in range(1, 4):
                load_bias(g)

            def body(kind, b):
                if kind in ("first", "loop"):
                    sp.wait_ge(aux_free, start_turn(kind, b))
                    load_x(b + 1)
                for i in range(STEPS):
                    if i == 2 and kind != "first":
                        load_residual(b - 1)
                    for name in step_tasks(kind, i):
                        if name in ("q1", "k1", "q", "k"):
                            stack(kind, b, name)
                    if i == 9 and kind != "first":
                        keep_x1(b - 1)

            each_batch(sp, body)
            sp.wait_ge(x1_kept, 16 * (B + 1))

        @block.tensor
        def _(pe):
            def task(kind, b, name):
                turn = turn_of(kind, b, name)
                if kind != "pro" or turn:
                    pe.wait_ge(aux_free, turn)
                bb = 0 if kind == "pro" else b + 1 if name in AHEAD else b - 1 if name in POST else b
                m = 1 if name[1:] == "1" else 0
                if name[:2] == "hT":
                    kc = int(name[-1])
                    pe.wait_ge(normed[0], bb + 1)
                    for tt in range(TT):
                        mm = pe.transpose(aux[:, tt * P:(tt + 1) * P], xin[:, tt, kc * P:(kc + 1) * P], k.ident[:])
                elif name in ("q", "q1", "k", "k1"):
                    col = (C if name[0] == "k" else 0) + m * P
                    for kc in range(KC):
                        mm = pe.matmul(aux[:, :], k.wa[:, kc, col:col + P], h_t[:, kc, :], start=(kc == 0), stop=(kc == KC - 1))
                elif name in ("v0", "v1"):
                    col = 2 * C + m * P
                    for tt in range(TT):
                        for kc in range(KC):
                            mm = pe.matmul(aux[:, tt * P:(tt + 1) * P], h_t[:, kc, tt * P:(tt + 1) * P],
                                           k.wa[:, kc, col:col + P], start=(kc == 0), stop=(kc == KC - 1))
                elif name[:3] == "ytr":
                    pe.wait_ge(y_copied, 4 * bb + int(name[-1]) + 1)
                    for tt in range(TT):
                        mm = pe.transpose(aux[:, tt * P:(tt + 1) * P], y_un[:, tt * P:(tt + 1) * P], k.ident[:])
                elif name[:2] == "yT":
                    kc = int(name[-1])
                    for tt in range(TT):
                        mm = pe.transpose(aux[:, tt * P:(tt + 1) * P], y_tok[:, tt, kc * P:(kc + 1) * P], k.ident[:])
                elif name[:2] == "pr":
                    for u in range(2):
                        tt = 2 * int(name[-1]) + u
                        cols = slice(u * C, (u + 1) * C)
                        for kc in range(KC):
                            pe.matmul(aux[:, cols], y_t[:, kc, tt * P:(tt + 1) * P], k.wp[:, kc, :], start=(kc == 0), stop=False)
                        mm = pe.matmul(aux[:, cols], k.ones_r[:], k.bp_parts[:], start=False, stop=True)
                elif name[:3] == "h2T":
                    kc = int(name[-1])
                    pe.wait_ge(h2_done, bb + 1)
                    for tt in range(TT):
                        mm = pe.transpose(aux[:, tt * P:(tt + 1) * P], h2[:, tt, kc * P:(kc + 1) * P], k.ident[:])
                elif name == "lg":
                    for tt in range(TT):
                        for kc in range(KC):
                            mm = pe.matmul(aux[:, tt * E:(tt + 1) * E], h2_t[:, kc, tt * P:(tt + 1) * P], k.wg_sb[:, kc, :],
                                           start=(kc == 0), stop=(kc == KC - 1))
                elif name == "pos":
                    pe.wait_ge(both_done, bb + 1)
                    pe.wait_ge(carried, bb + 1)
                    pe.matmul(aux[:, 0:TT * E], k.before[:], both[:].rearrange("p t e -> p (t e)"), start=True, stop=False)
                    for u in range(TT - 1):
                        pe.matmul(aux[:, (u + 1) * E:TT * E], k.ones[:], both[:, u:u + 1, :].to_broadcast([P, TT - 1 - u, E]),
                                  start=False, stop=False)
                    mm = pe.matmul(aux[:, 0:TT * E], k.ones[:], k.carry[:].unsqueeze(1).to_broadcast([P, TT, E]),
                                   start=False, stop=True)
                mm.then_inc(aux_ready, 1)

            def scores(kind, b, h, slots):
                m, hl = h // HH, h % HH
                if hl == 0 and 0 in slots:
                    for i in range(2):
                        pe.wait_ge(stacked[i], 128 * (2 * b + m + 1))
                for j in TILE_ORDER:
                    slot, col = TILE_AT[j]
                    if slot not in slots:
                        continue
                    n = 3 * h + slot
                    if col == 0 and (kind != "first" or n >= 4):
                        pe.wait_ge(exped, 4 * H * b + 4 * ((n - 4) // 3) + EXPS_AFTER_SLOT[(n - 4) % 3])
                    w = (j + 1) * P
                    mm = pe.matmul(s_bank[n % 4][:, col:col + w], q_st[m][:, hl, j * P:(j + 1) * P],
                                   k_st[m][:, hl // 2, 0:w], start=True, stop=True)
                    if j != 2:
                        mm.then_inc(scored, 1)

            def transposes(kind, b, h, slots):
                if 0 in slots:
                    pe.wait_ge(exped, 4 * H * b + 4 * (h + 1))
                for slot in slots:
                    n = 3 * h + slot
                    if n >= 2 or kind != "first":
                        hp, sp_ = (n - 2) // 3, (n - 2) % 3
                        if sp_ == 1:
                            pe.wait_ge(pt_act, H * b + hp + 1)
                        else:
                            pe.wait_ge(pt_dve, 2 * H * b + 2 * hp + (1 if sp_ == 0 else 2))
                    for st in (s for s in (0, 1, 3, 2) if TR_AT[s][0] == slot):
                        for j in range(st, TT):
                            col = TR_AT[st][1] + (j - st) * P
                            src = P_AT[j] + st * P
                            mm = pe.transpose(t_bank[n % 2][:, col:col + P], probs[h % 4][:, src:src + P], k.ident[:])
                    mm.then_inc(transposed, 1)

            def values(kind, b, g, part):
                m = g // 2
                if part == 0:
                    pe.wait_ge(pt_dve, 2 * H * b + 8 * (g + 1))
                    pe.wait_ge(pt_act, H * b + 4 * (g + 1))
                    if kind != "first" or g:
                        pe.wait_ge(y_copied, 4 * b + g)
                for st in PV_PARTS[part]:
                    w = (TT - st) * P
                    for hq in range(4):
                        h = 4 * g + hq
                        mm = pe.matmul(y_bank[32 * hq:32 * hq + 32, st * P:T], v_sb[m][:, st, h % HH, :],
                                       probs_t[:, h % 8, PT_AT[st]:PT_AT[st] + w], start=(st == 0), stop=(st == TT - 1),
                                       skip_group_check=True)
                if part == len(PV_PARTS) - 1:
                    mm.then_inc(pv_done, 1)

            for name in AUX_PRO:
                task("pro", 0, name)
            scores("first", 0, 0, (0, 1))

            def body(kind, b):
                for i in range(STEPS):
                    turned, part = transposed_head(kind, b, i), values_part(kind, b, i)
                    after = ((kind, b, i + 1) if i + 1 < H else ("loop", b + 1, 0)) if kind != "end" else None
                    if kind == "last" and i + 1 == H:
                        after = None
                    if kind != "end":
                        scores(kind, b, i, (2,))
                    if turned:
                        transposes(kind, *turned, (1,))
                    for name in step_tasks(kind, i, [AUX_MID]):
                        task(kind, b, name)
                    if after:
                        scores(*after, (0,))
                    if turned:
                        transposes(kind, *turned, (2,))
                    if after:
                        scores(*after, (1,))
                    if i + 1 < STEPS:
                        turned = transposed_head(kind, b, i + 1)
                    else:
                        turned = (b, H - LAG) if kind != "end" else None
                    if turned:
                        transposes(kind if i + 1 < STEPS else "loop", *turned, (0,))
                    if part:
                        values(kind, *part)
                    for name in step_tasks(kind, i, [AUX_END]):
                        task(kind, b, name)

            each_batch(pe, body)

        @block.scalar
        def _(act):
            def task(kind, b, name):
                turn = turn_of(kind, b, name)
                bb = 0 if kind == "pro" else b + 1 if name in AHEAD else b - 1 if name in POST else b
                if name == "pos":
                    act.wait_ge(gap_done, bb + 1)
                    nc.scalar.activation(gexp[:], gap[:], ACT.Exp).then_inc(exp_done, 1)
                if name not in ("hT0", "hT1", "q", "q1", "k", "k1", "v0", "v1", "yT0", "yT1", "h2T0", "h2T1"):
                    return
                act.wait_ge(aux_ready, turn + 1)
                m = 1 if name[1:] == "1" else 0
                if name[:2] == "hT":
                    kc = int(name[-1])
                    act.wait_ge(mod_b_set, bb + 1)
                    nc.scalar.activation(h_t[:, kc, :], aux[:, :], ACT.Identity, bias=mod_b[:, 0, kc:kc + 1],
                                         scale=mod_b[:, 1, kc:kc + 1]).then_inc(aux_free, 1)
                elif name[0] in "qk":
                    i = 0 if name[0] == "q" else 1
                    if kind != "pro":
                        act.wait_ge(stored[i], 32 * (nth_part(kind, b, name) - 1))
                    nc.scalar.activation(part_hi[i][:], aux[:, :], ACT.Identity, bias=k.bqk[:, 2 * i + m:2 * i + m + 1]
                                         ).then_inc(hi_done, 1)
                elif name[0] == "v":
                    if kind == "first":
                        act.wait_ge(cleared, 4)
                    nc.scalar.copy(v_sb[m][:, :, :, 0:D], aux[:, :].rearrange("p (t h d) -> p t h d", t=TT, d=D)
                                   ).then_inc(aux_free, 1)
                elif name[:2] == "yT":
                    nc.scalar.copy(y_t[:, int(name[-1]), :], aux[:, :]).then_inc(aux_free, 1)
                elif name[:3] == "h2T":
                    nc.scalar.copy(h2_t[:, int(name[-1]), :], aux[:, :]).then_inc(aux_free, 1)

            def exps(kind, b, i, slots):
                if 0 in slots and (kind != "first" or i >= 4):
                    act.wait_ge(transposed, 3 * H * b + 3 * (i - 3))
                for j in TILE_ORDER:
                    slot, col = TILE_AT[j]
                    if slot not in slots:
                        continue
                    w = (j + 1) * P
                    act.wait_ge(biased, 4 * H * b + 4 * i + EXPS_AFTER_SLOT[slot])
                    nc.scalar.activation(probs[i % 4][:, P_AT[j]:P_AT[j] + w], s_bank[(3 * i + slot) % 4][:, col:col + w],
                                         ACT.Exp, bias=neg_max[:, i % 4, j:j + 1], scale=-1.0).then_inc(exped, 1)

            def copy_transposed(kind, b, h):
                act.wait_ge(transposed, 3 * H * b + 3 * h + 2)
                if kind != "first" or h >= 8:
                    act.wait_ge(pv_done, 4 * b + h // 4 - 1)
                nc.scalar.copy(probs_t[:, h % 8, 512:1024], t_bank[(3 * h + 1) % 2][:, :]).then_inc(pt_act, 1)

            def copy_sums(kind, b, i, p, g):
                act.wait_ge(pv_done, 4 * p + g + 1)
                if g == 2:
                    act.wait_ge(aux_free, start_turn(kind, b))
                elif g or kind != "first":
                    act.wait_ge(aux_free, turn_of(kind, b, f"ytr{(g - 1) % 4}") + 1)
                nc.scalar.copy(y_un[:, :], y_bank[:, :]).then_inc(y_copied, 1)

            for name in AUX_PRO:
                task("pro", 0, name)

            def body(kind, b):
                for i in range(STEPS):
                    turned, part = transposed_head(kind, b, i), values_part(kind, b, i - 1)
                    if kind != "end":
                        exps(kind, b, i, (0, 1))
                    if turned:
                        copy_transposed(kind, *turned)
                    if part and part[2] == len(PV_PARTS) - 1:
                        copy_sums(kind, b, i, *part[:2])
                    for name in reads_of(kind, i, 0):
                        task(kind, b, name)
                    if kind != "end":
                        exps(kind, b, i, (2,))
                    for name in reads_of(kind, i, 1):
                        task(kind, b, name)

            each_batch(act, body)

        @block.vector
        def _(dve):
            v = nc.vector

            def ln_stats(i, n, src, ready, value):
                dve.wait_ge(ready, value)
                dve.nop(nofuse=True)
                for tt in range(TT):
                    ins = v.bn_stats(stats[i][:, tt, :], src[:, tt, :])
                ins.then_inc(stats_done[i], 1)
                dve.wait_ge(stats_done[i], n)
                dve.nop(nofuse=True)
                for tt in range(TT):
                    ins = v.bn_aggr(mv[i][:, tt, :], stats[i][:, tt, :])
                ins.then_inc(mv_done[i], 1)

            def router_choice(p, turn):
                dve.wait_ge(rows_free, p + 1)
                v.tensor_copy(logits[:], aux[:, 0:TT * E].rearrange("p (t e) -> p t e", t=TT)).then_inc(aux_free, 1)
                dve.wait_ge(aux_free, turn + 1)
                dve.nop(nofuse=True)
                for tt in range(TT):
                    ins = v.max(top8[:, tt, :], logits[:, tt, :])
                ins.then_inc(top_done, 1)
                dve.wait_ge(top_done, p + 1)
                dve.nop(nofuse=True)
                for tt in range(TT):
                    ins = v.max_index(idx8[:, tt, :], top8[:, tt, :], logits[:, tt, :])
                ins.then_inc(idx_done, 1)
                v.tensor_tensor(gap[:], top8[:, :, 1], top8[:, :, 0], ALU.subtract).then_inc(gap_done, 1)
                dve.wait_ge(idx_done, p + 1)
                v.tensor_copy(idxf[:], idx8[:, :, 0:2].rearrange("p t n -> p n t")).then_inc(idxf_done, 1)
                dve.wait_ge(idxf_done, p + 1)
                for n in range(2):
                    ins = v.tensor_tensor(chosen[:, n, :, :], k.iota_e[:],
                                          idxf[:, n, :].unsqueeze(2).to_broadcast([P, TT, E]), ALU.is_equal)
                ins.then_inc(chosen_done, 1)
                dve.wait_ge(chosen_done, p + 1)
                v.tensor_tensor(both[:], chosen[:, 0, :, :], chosen[:, 1, :, :], ALU.add).then_inc(both_done, 1)

            def router_slots(p, turn):
                v.tensor_tensor(place[:], aux[:, 0:TT * E].rearrange("p (t e) -> p t e", t=TT), k.region[:], ALU.add
                                ).then_inc(aux_free, 1)
                v.tensor_reduce(both_sum[:], both[:].rearrange("p t e -> p e t"), AX.X, ALU.add).then_inc(summed, 1)
                dve.wait_ge(summed, p + 1)
                v.tensor_tensor(k.carry[:], k.carry[:], both_sum[:], ALU.add).then_inc(carried, 1)
                dve.wait_ge(aux_free, turn + 1)
                for n in range(2):
                    ins = v.tensor_tensor(chosen_place[:, n, :, :], chosen[:, n, :, :], place[:], ALU.mult)
                ins.then_inc(weighed, 1)
                dve.wait_ge(weighed, p + 1)
                v.tensor_reduce(slot_f[:], chosen_place[:], AX.X, ALU.add).then_inc(slot_f_done, 1)
                dve.wait_ge(slot_f_done, p + 1)
                v.tensor_copy(slot_b[:], slot_f[:].rearrange("p n t -> p (n t)")).then_inc(slot_done, 1)
                dve.wait_ge(exp_done, p + 1)
                v.tensor_scalar(gden[:], gexp[:], 1.0, None, ALU.add).then_inc(den_done, 1)
                dve.wait_ge(den_done, p + 1)
                v.reciprocal(gates[:, 0, :], gden[:]).then_inc(g1_done, 1)
                dve.wait_ge(g1_done, p + 1)
                v.tensor_tensor(gates[:, 1, :], gexp[:], gates[:, 0, :], ALU.mult).then_inc(g2_done, 1)

            def task(kind, b, name):
                turn = turn_of(kind, b, name)
                bb = b - 1 if name in POST else b
                if name in ("hT0", "hT1", "v0", "v1", "yT0", "yT1", "h2T0", "h2T1"):
                    return
                m = 1 if name[1:] == "1" else 0
                if name in ("q", "q1", "k", "k1"):
                    i = 0 if name[0] == "q" else 1
                    dve.wait_ge(hi_done, 2 * nth_part(kind, b, name) - 1 + i)
                    v.scalar_tensor_tensor(out=part_lo[i][:], in0=aux[:, :], scalar=k.bqk[:, 2 * i + m:2 * i + m + 1],
                                           in1=part_hi[i][:].bitcast(F32), op0=ALU.add, op1=ALU.subtract).then_inc(aux_free, 1)
                    return
                dve.wait_ge(aux_ready, turn + 1)
                if name[:3] == "ytr":
                    g = int(name[-1])
                    ps = aux[:, :].rearrange("p (t h d) -> p t h d", t=TT, h=4)
                    v.reciprocal(recips[:], ps[:, :, :, D]).then_inc(y_recip, 1)
                    dve.wait_ge(y_recip, 4 * bb + g + 1)
                    v.tensor_tensor(y_tok[:, :, 4 * D * g:4 * D * (g + 1)].rearrange("p t (h d) -> p t h d", h=4),
                                    ps[:, :, :, 0:D], recips[:].unsqueeze(3).to_broadcast([P, TT, 4, D]), ALU.mult
                                    ).then_inc(aux_free, 1)
                elif name[:2] == "pr":
                    i = int(name[-1])
                    dve.wait_ge(x1_kept, 16 * (bb + 1))
                    dve.wait_ge(xr_in, 32 * (bb + 1))
                    v.tensor_tensor(x1[:, 2 * i:2 * i + 2, :], aux[:, :].rearrange("p (u c) -> p u c", u=2),
                                    mod_row[:, 0:1, :].to_broadcast([P, 2, C]), ALU.mult).then_inc(aux_free, 1)
                elif name == "lg":
                    router_choice(bb, turn)
                elif name == "pos":
                    router_slots(bb, turn)

            dve.sem_inc(carried, 1)
            for m in range(2):
                v.memset(q_st[m][:].bitcast(F32), 0.0).then_inc(cleared, 1)
                v.memset(v_sb[m][:], 1.0).then_inc(cleared, 1)
            ln_stats(0, 1, xin, x_in, 16)
            for name in AUX_PRO:
                task("pro", 0, name)

            def add_bias(kind, b, i, slots):
                for j in TILE_ORDER:
                    slot, col = TILE_AT[j]
                    if slot not in slots:
                        continue
                    w = (j + 1) * P
                    s = s_bank[(3 * i + slot) % 4][:, col:col + w]
                    if j != 0:
                        dve.wait_ge(scored, 3 * H * b + 3 * i + slot + 1)
                        dve.nop(nofuse=True)
                    v.tensor_tensor_reduce(s, s, k.bias_w[:, i, T - w:T], -1.0, BIG, ALU.add, ALU.min,
                                           neg_max[:, i % 4, j:j + 1]).then_inc(biased, 1)

            def copy_transposed(kind, b, h, slot):
                if slot == 0 and (kind != "first" or h >= 8):
                    dve.wait_ge(pv_done, 4 * b + h // 4 - 1)
                at, w = TR_SLOT[slot]
                dve.wait_ge(transposed, 3 * H * b + 3 * h + slot + 1)
                v.tensor_copy(probs_t[:, h % 8, at:at + w], t_bank[(3 * h + slot) % 2][:, 0:w]).then_inc(pt_dve, 1)

            def body(kind, b):
                for i in range(STEPS):
                    turned = transposed_head(kind, b, i)
                    if kind == "first" and i % 4 == 0:
                        dve.wait_ge(bias_in, 16 * (i // 4 + 1))
                    if kind != "end":
                        add_bias(kind, b, i, (0,))
                    if turned:
                        copy_transposed(kind, *turned, 0)
                    if kind != "end":
                        add_bias(kind, b, i, (1,))
                    if i == 2 and kind in ("first", "loop"):
                        ln_stats(0, b + 2, xin, x_in, 16 * (b + 2))
                    if i == 10 and kind != "first":
                        ln_stats(1, b, x1, x1_done, b)
                    if kind != "end":
                        add_bias(kind, b, i, (2,))
                    for name in reads_of(kind, i, 0):
                        task(kind, b, name)
                    if turned:
                        copy_transposed(kind, *turned, 2)
                    for name in reads_of(kind, i, 1):
                        task(kind, b, name)

            each_batch(dve, body)

        @block.gpsimd
        def _(pool):
            g = nc.gpsimd

            def normalise(i, n, src, dst):
                pool.wait_ge(mv_done[i], n)
                pool.nop(nofuse=True)
                g.tensor_scalar(var[i][:], mv[i][:, :, 1], EPS, None, ALU.add).then_inc(var_done[i], 1)
                pool.wait_ge(var_done[i], n)
                pool.nop(nofuse=True)
                g.tensor_tensor(rstd[i][:], var[i][:], k.neghalf[:], ALU.pow).then_inc(rstd_done[i], 1)
                pool.wait_ge(rstd_done[i], n)
                pool.nop(nofuse=True)
                for tt in range(TT):
                    ins = g.tensor_scalar(dst[:, tt, :], src[:, tt, :], mv[i][:, tt, 0:1], rstd[i][:, tt:tt + 1],
                                          ALU.subtract, ALU.mult)
                ins.then_inc(normed[i], 1)

            def set_mod_b(b):
                g.tensor_copy(mod_b[:].unsqueeze(3), k.mod_c[:, :, :, bass.ds(b, 1)]).then_inc(mod_b_set, 1)

            def after(kind, b):
                p = b - 1
                pool.wait_ge(aux_free, turn_of(kind, b, "pr1") + 1)
                pool.wait_ge(xr_in, 32 * (p + 1))
                g.tensor_tensor(x1[:], x1[:], h2, ALU.add).then_inc(x1_done, 1)
                pool.wait_ge(x1_done, p + 1)
                normalise(1, p + 1, x1, h2)
                pool.wait_ge(normed[1], p + 1)
                g.tensor_tensor(h2, h2, mod_row[:, 2:3, :].to_broadcast([P, TT, C]), ALU.mult
                                ).then_inc(h2_scaled, 1)
                pool.wait_ge(h2_scaled, p + 1)
                g.tensor_tensor(h2, h2, mod_row[:, 1:2, :].to_broadcast([P, TT, C]), ALU.add
                                ).then_inc(h2_done, 1)
                g.tensor_tensor(rows[:, :, C], rows[:, :, C], k.to_next[:], ALU.add)
                pool.wait_ge(slot_done, p + 1)
                pool.wait_ge(g2_done, p + 1)
                pool.nop(nofuse=True)
                g.tensor_copy(rows[:, :, C + 1], idxf[:, 0, :]).then_inc(rows_named, 1)
                g.tensor_copy(k.gates_all[:, bass.ds(p, 1), :], gates[:].rearrange("p n t -> p (n t)").unsqueeze(1)
                              ).then_inc(kept, 1)
                pool.wait_ge(rows_named, p + 1)
                pool.nop(nofuse=True)
                for n in range(2 * TT):
                    g.indirect_dma_start(rows_d, bass.IndirectOffsetOnAxis(ap=slot_b[:, n:n + 1].bitcast(U32), axis=0),
                                         rows[:, n % TT, :], None).then_inc(scattered, 16)
                pool.wait_ge(kept, p + 1)
                pool.wait_ge(scattered, 16 * 2 * TT * (p + 1))
                pool.sem_inc(rows_free, 1)

            pool.sem_inc(rows_free, 1)
            g.tensor_copy(rows[:, :, C], k.token[:])
            normalise(0, 1, xin, xin)
            set_mod_b(0)

            def body(kind, b):
                if kind in ("first", "loop"):
                    pool.wait_ge(aux_free, start_turn(kind, b))
                    pool.nop(nofuse=True)
                    set_mod_b(b + 1)
                    normalise(0, b + 2, xin, xin)
                if kind != "first":
                    after(kind, b)

            each_batch(pool, body)
def experts(nc, sem, w1, w3, w2, a1, a3, a2, lb1, lb3, lb2, b1, b3, b2, rows_d, y_d, k):
    with ExitStack() as ctx:
        def sb(name, shape, dt=F32):
            return ctx.enter_context(nc.sbuf_tensor(name, shape, dt))

        raw = [sb(f"raw{i}", [P, 6, HID]) for i in range(2)]
        w_hi = [sb(f"w_hi{i}", [P, 6, HID], F32R) for i in range(2)]
        w_lo = [sb(f"w_lo{i}", [P, 6, HID], F32R) for i in range(2)]
        a_diag = sb("a_diag", [P, E, 2 * C + HID])
        lb_all = sb("lb_all", [P, 2 * HID + C])
        b13 = sb("b13", [P, 2, E, HK])
        b2_rows = sb("b2_rows", [P, E, C])
        tile_in = sb("tile_in", [P, 2, C + 2])
        second = sb("second", [P, 2])
        names = sb("names", [P, 2, 2])
        goal = sb("goal", [P, 2], I32)
        x_hi = sb("x_hi", [P, KC, FT], F32R)
        x_lo = sb("x_lo", [P, KC, FT], F32R)
        silu = sb("silu", [P, HK, FT])
        g_full = sb("g_full", [P, HK, FT])
        g_hi = sb("g_hi", [P, HK, FT], F32R)
        g_lo = sb("g_lo", [P, HK, FT], F32R)
        y_sb = sb("y_sb", [P, 2, C])
        padding = sb("padding", [P, 2, C + 2])
        pad_i = sb("pad_i", [P, 2], I32)
        cnt = sb("cnt", [P, E], I32)
        cnt_up = sb("cnt_up", [P, E], I32)
        cnt_sh = sb("cnt_sh", [P, E], I32)
        n_tiles = sb("n_tiles", [P, E], I32)
        h_bank = [ctx.enter_context(nc.psum_tensor(f"h_bank{i}", [P, 512], F32)) for i in range(4)]
        yb = [ctx.enter_context(nc.psum_tensor(f"yb{i}", [P, 512], F32)) for i in range(2)]
        turn_bank = ctx.enter_context(nc.psum_tensor("turn_bank", [P, 512], F32))
        cnt_bank = ctx.enter_context(nc.psum_tensor("cnt_bank", [P, 512], F32))

        pads_named, lora_in, diag_clear, counted, cnt_read, cnt_done, padded = (
            sem(n) for n in ("pads_named", "lora_in", "diag_clear", "counted", "cnt_read", "cnt_done", "padded"))
        raw_in = [sem(f"raw_in{i}") for i in range(2)]
        folded, merged, split_hi, split_done = (sem(n) for n in ("folded", "merged", "split_hi", "split_done"))
        rows_in, turned, x_hi_done, x_split = (sem(n) for n in ("rows_in", "turned", "x_hi_done", "x_split"))
        names_taken, second_done, goal_set = (sem(n) for n in ("names_taken", "second_done", "goal_set"))
        h_ready, silu_ready, h_read, g_hi_done, g_split, y_ready, y_read, y_kept, y_gone = (
            sem(n) for n in ("h_ready", "silu_ready", "h_read", "g_hi_done", "g_split", "y_ready", "y_read", "y_kept", "y_gone"))
        NRAW = 6
        NLORA = 6 + 3 * E

        def tile_counts(eng):
            eng.wait_ge(cnt_done, 4)
            n, base = [], [0]
            for e in range(E):
                n.append(eng.value_load(n_tiles[0:1, e:e + 1], min_val=1, max_val=B * T // FT))
                base.append(eng.snap(base[-1] + n[-1]))
            return n, base

        block = ctx.enter_context(nc.Block())

        @block.sync
        def _(sp):
            def load_weights(e):
                i = e % 2
                for kc in range(KC):
                    sp.dma_start(raw[i][:, kc, :], w1[e, kc * P:(kc + 1) * P, :]).then_inc(raw_in[i], 16)
                    sp.dma_start(raw[i][:, KC + kc, :], w3[e, kc * P:(kc + 1) * P, :]).then_inc(raw_in[i], 16)
                for j in range(2):
                    sp.dma_start(raw[i][:, 4 + j, :].rearrange("p (a c) -> p a c", a=2),
                                 w2[e, 2 * j * P:2 * (j + 1) * P, :].rearrange("(a p) c -> p a c", p=P)).then_inc(raw_in[i], 16)

            load_weights(0)
            for n, src in enumerate((b1, b3)):
                sp.dma_start(b13[:, n, :, :], src.rearrange("e (m p) -> p e m", p=P), allow_slow_non_contiguous=True
                             ).then_inc(lora_in, 16)
            sp.dma_start(b2_rows[:], b2.rearrange("e c -> (e c)").partition_broadcast(P).rearrange("p (e c) -> p e c", e=E)
                         ).then_inc(lora_in, 16)
            sp.dma_start(lb_all[:, 0:HID], lb1).then_inc(lora_in, 16)
            sp.dma_start(lb_all[:, HID:2 * HID], lb3).then_inc(lora_in, 16)
            sp.dma_start(lb_all[:, 2 * HID:2 * HID + C], lb2).then_inc(lora_in, 16)
            sp.wait_ge(diag_clear, 1)
            for e in range(E):
                rows = slice(R * e, R * (e + 1))
                for src, at, w in ((a1, 0, C), (a3, C, C), (a2, 2 * C, HID)):
                    sp.dma_start(a_diag[rows, e, at:at + w], src[rows, :]).then_inc(lora_in, 16)
            n, base = tile_counts(sp)
            for e in range(E):
                last = sp.value_load(cnt[0:1, e:e + 1], min_val=0, max_val=B * T)
                sp.dma_start(rows_d[bass.ds(last + e * REGION, FT), :].rearrange("(u p) c -> p u c", p=P), padding[:]
                             ).then_inc(padded, 16)
            sp.wait_ge(padded, 16 * E)

            def load_rows(first_row, g):
                sp.wait_ge(turned, g + 1)
                sp.wait_ge(names_taken, g + 1)
                sp.dma_start(tile_in[:], rows_d[bass.ds(first_row, FT), :].rearrange("(u p) c -> p u c", p=P)
                             ).then_inc(rows_in, 16)

            for e in range(E):
                if e + 1 < E:
                    if e:
                        sp.wait_ge(split_done, e)
                    load_weights(e + 1)
                with sp.Fori(0, n[e]) as i:
                    load_rows(i * FT + e * REGION, base[e] + i)
            load_rows(0, base[E])

        @block.tensor
        def _(pe):
            pe.matmul(cnt_bank[:, 0:E], k.ones[:], k.carry[:], start=True, stop=True).then_inc(counted, 1)

            def fold(e):
                if e == 0:
                    pe.wait_ge(lora_in, 16 * NLORA)
                if e >= 2:
                    pe.wait_ge(h_read, 4 * base[e - 1] + 4)
                for j in range(6):
                    if j >= 4 or e == 1:
                        pe.wait_ge(merged, max(6 * e + j - 3, 1) if j >= 4 else 6)
                    bank = h_bank[j % 4]
                    if j < 4:
                        mm = pe.matmul(bank[:, :], a_diag[:, e, j * P:(j + 1) * P], lb_all[:, (j // 2) * HID:(j // 2 + 1) * HID],
                                       start=True, stop=True)
                    else:
                        for u in range(2):
                            mc = 2 * (j - 4) + u
                            mm = pe.matmul(bank[:, u * C:(u + 1) * C], a_diag[:, e, 2 * C + mc * P:2 * C + (mc + 1) * P],
                                           lb_all[:, 2 * HID:2 * HID + C], start=True, stop=True)
                    mm.then_inc(folded, 1)

            def turn():
                for u in range(2):
                    for kc in range(KC):
                        mm = pe.transpose(turn_bank[:, kc * FT + u * P:kc * FT + (u + 1) * P],
                                          tile_in[:, u, kc * P:(kc + 1) * P], k.ident[:])
                mm.then_inc(turned, 1)

            pe.sem_inc(turned, 1)
            pe.sem_inc(y_ready, 1)
            n, base = tile_counts(pe)
            fold(0)
            pe.wait_ge(rows_in, 16)
            turn()
            for e in range(E):
                if e + 1 < E:
                    fold(e + 1)
                    pe.wait_ge(merged, 6 * (e + 2))
                pe.wait_ge(split_done, e + 1)
                hi, lo = w_hi[e % 2], w_lo[e % 2]
                with pe.Fori(0, n[e]) as i:
                    g = base[e] + i
                    pe.wait_ge(x_split, g + 1)
                    for m in range(HK):
                        pe.wait_ge(h_read, 4 * g + (m + 1))
                        for which in range(2):
                            parts = [(kc, w, xs) for kc in range(KC) for w, xs in ((hi, x_hi), (hi, x_lo), (lo, x_hi))]
                            for q, (kc, w, xs) in enumerate(parts):
                                mm = pe.matmul(h_bank[m][:, which * FT:(which + 1) * FT], w[:, 2 * which + kc, m * P:(m + 1) * P],
                                               xs[:, kc, :], start=(q == 0), stop=(q == len(parts) - 1))
                        mm.then_inc(h_ready, 1)
                    pe.wait_ge(rows_in, 16 * g + 32)
                    turn()
                    pe.wait_ge(y_read, g + 1)
                    for m in range(HK):
                        pe.wait_ge(g_split, 4 * g + (m + 1))
                        for u in range(2):
                            for q, (gs, w) in enumerate(((g_hi, hi), (g_lo, hi), (g_hi, lo))):
                                mm = pe.matmul(yb[u][:, 0:C], gs[:, m, u * P:(u + 1) * P],
                                               w[:, 4 + m // 2, (m % 2) * C:(m % 2 + 1) * C],
                                               start=(m == 0 and q == 0), stop=(m == HK - 1 and q == 2))
                    mm.then_inc(y_ready, 1)

        @block.scalar
        def _(act):
            n, base = tile_counts(act)

            def take_high(g):
                act.wait_ge(turned, g + 2)
                nc.scalar.copy(x_hi[:], turn_bank[:, :].rearrange("p (k t) -> p k t", k=KC)).then_inc(x_hi_done, 1)

            take_high(0)
            act.wait_ge(lora_in, 16 * NLORA)
            for e in range(E):
                with act.Fori(0, n[e]) as i:
                    g = base[e] + i
                    for m in range(HK + 1):
                        if m < HK:
                            act.wait_ge(h_ready, 4 * g + (m + 1))
                            act.wait_ge(h_read, 4 * g + (m + 1))
                            nc.scalar.activation(silu[:, m, :], h_bank[m][:, 0:FT], ACT.Silu, bias=b13[:, 0, e, m:m + 1]
                                                 ).then_inc(silu_ready, 1)
                        if m:
                            if m == 1:
                                act.wait_ge(y_ready, g + 1)
                            act.wait_ge(h_read, 4 * g + (m + 4))
                            nc.scalar.copy(g_hi[:, m - 1, :], g_full[:, m - 1, :]).then_inc(g_hi_done, 1)
                    take_high(g + 1)

        @block.vector
        def _(dve):
            v = nc.vector
            v.memset(padding[:, :, 0:C], 0.0)
            dve.wait_ge(pads_named, 1)
            v.tensor_copy(padding[:, :, C], pad_i[:])
            v.memset(padding[:, :, C + 1], 0.0)
            v.memset(a_diag[:], 0.0).then_inc(diag_clear, 1)
            dve.wait_ge(counted, 1)
            v.tensor_copy(cnt[:], cnt_bank[:, 0:E])
            v.tensor_scalar(cnt_up[:], cnt_bank[:, 0:E], float(FT - 1), None, ALU.add).then_inc(cnt_done, 1)
            dve.wait_ge(cnt_done, 1)
            v.tensor_scalar(cnt_sh[:], cnt_up[:], FT.bit_length() - 1, None, ALU.logical_shift_right).then_inc(cnt_done, 1)
            dve.wait_ge(cnt_done, 2)
            v.tensor_scalar(n_tiles[:], cnt_sh[:], 1.0, None, ALU.max).then_inc(cnt_done, 1)
            dve.wait_ge(cnt_done, 3)
            dve.sem_inc(cnt_done, 1)
            dve.sem_inc(h_read, 4)
            dve.sem_inc(y_read, 1)
            dve.sem_inc(y_gone, 1)
            dve.sem_inc(names_taken, 1)
            n, base = tile_counts(dve)

            def merge(e):
                dve.wait_ge(raw_in[e % 2], 16 * NRAW * (e // 2 + 1))
                for j in range(6):
                    dve.wait_ge(folded, 6 * e + j + 1)
                    v.tensor_tensor(raw[e % 2][:, j, :], raw[e % 2][:, j, :], h_bank[j % 4][:, :], ALU.add).then_inc(merged, 1)

            def take_low(g):
                dve.wait_ge(x_hi_done, g + 1)
                v.tensor_tensor(x_lo[:], turn_bank[:, :].rearrange("p (k t) -> p k t", k=KC), x_hi[:].bitcast(F32),
                                ALU.subtract).then_inc(x_split, 1)

            def take_names(g):
                dve.wait_ge(x_hi_done, g + 1)
                v.tensor_copy(names[:], tile_in[:, :, C:C + 2]).then_inc(names_taken, 1)

            merge(0)
            take_low(0)
            take_names(0)
            for e in range(E):
                if e + 1 < E:
                    merge(e + 1)
                with dve.Fori(0, n[e]) as i:
                    g = base[e] + i
                    for m in range(HK + 1):
                        if m < HK:
                            dve.wait_ge(silu_ready, 4 * g + (m + 1))
                            v.scalar_tensor_tensor(out=g_full[:, m, :], in0=h_bank[m][:, FT:2 * FT], scalar=b13[:, 1, e, m:m + 1],
                                                   in1=silu[:, m, :], op0=ALU.add, op1=ALU.mult).then_inc(h_read, 1)
                        if m:
                            dve.wait_ge(g_hi_done, 4 * g + m)
                            v.tensor_tensor(g_lo[:, m - 1, :], g_full[:, m - 1, :], g_hi[:, m - 1, :].bitcast(F32), ALU.subtract
                                            ).then_inc(g_split, 1)
                    dve.wait_ge(y_gone, g + 1)
                    dve.wait_ge(names_taken, g + 2)
                    v.tensor_scalar(second[:], names[:, :, 1], float(e), float(B * T), ALU.not_equal, ALU.mult
                                    ).then_inc(second_done, 1)
                    dve.wait_ge(second_done, g + 1)
                    v.tensor_tensor(goal[:], second[:], names[:, :, 0], ALU.add).then_inc(goal_set, 1)
                    take_low(g + 1)
                    dve.wait_ge(goal_set, g + 1)
                    take_names(g + 1)
                    dve.wait_ge(y_ready, g + 2)
                    for u in range(2):
                        ins = v.tensor_tensor(y_sb[:, u, :], yb[u][:, 0:C], b2_rows[:, e, :], ALU.add)
                    ins.then_inc(y_read, 1)

        @block.gpsimd
        def _(pool):
            g = nc.gpsimd
            g.iota(pad_i[:], [[P, 2]], base=2 * B * T, channel_multiplier=1).then_inc(pads_named, 1)
            n, base = tile_counts(pool)

            def split(e):
                i = e % 2
                pool.wait_ge(merged, 6 * (e + 1))
                if e >= 2:
                    pool.wait_ge(y_ready, base[e - 1] + 1)
                    pool.nop(nofuse=True)
                for j in range(6):
                    ins = g.tensor_copy(w_hi[i][:, j, :], raw[i][:, j, :])
                ins.then_inc(split_hi, 1)
                pool.wait_ge(split_hi, e + 1)
                for j in range(6):
                    ins = g.tensor_tensor(w_lo[i][:, j, :], raw[i][:, j, :], w_hi[i][:, j, :].bitcast(F32), ALU.subtract)
                ins.then_inc(split_done, 1)

            split(0)
            for e in range(E):
                if e + 1 < E:
                    split(e + 1)
                with pool.Fori(0, n[e]) as i:
                    t = base[e] + i
                    pool.wait_ge(goal_set, t + 1)
                    pool.wait_ge(y_read, t + 2)
                    pool.nop(nofuse=True)
                    for u in range(2):
                        g.indirect_dma_start(y_d, bass.IndirectOffsetOnAxis(ap=goal[:, u:u + 1].bitcast(U32), axis=0),
                                             y_sb[:, u, :], None).then_inc(y_kept, 16)
                    pool.wait_ge(y_kept, 32 * t + 32)
                    pool.sem_inc(y_gone, 1)


def combine(nc, sem, x1_d, y_d, mod_d, out, k):
    with ExitStack() as ctx:
        def sb(name, shape, dt=F32):
            return ctx.enter_context(nc.sbuf_tensor(name, shape, dt))

        y12 = [sb(f"y12_{i}", [P, 2, TT, C]) for i in range(2)]
        gb_row = [sb(f"gb_row{i}", [P, C]) for i in range(2)]
        x1 = [sb(f"x1_of{i}", [P, TT, C]) for i in range(2)]
        first = [sb(f"first{i}", [P, TT, C]) for i in range(2)]
        mixed = [sb(f"mixed{i}", [P, TT, C]) for i in range(2)]
        scaled = [sb(f"scaled_mix{i}", [P, TT, C]) for i in range(2)]
        res = [sb(f"res{i}", [P, TT, C]) for i in range(2)]
        y_in, x1_in, res_kept = ([sem(f"{n}{i}") for i in range(2)] for n in ("y_in", "x1_in", "res_kept"))
        weighted, mix_done, mix_scaled, res_done = (sem(n) for n in ("weighted", "mix_done", "mix_scaled", "res_done"))
        block = ctx.enter_context(nc.Block())

        @block.sync
        def _(sp):
            for b in range(B):
                i = b % 2
                if b >= 2:
                    sp.wait_ge(res_done, b - 1)
                for n in range(2):
                    at = n * B * T + b * T
                    sp.dma_start(y12[i][:, n, :, :], y_d[at:at + T, :].rearrange("(t p) c -> p t c", p=P)).then_inc(y_in[i], 16)
                sp.dma_start(gb_row[i][:], mod_d[b:b + 1, 3 * C:4 * C].partition_broadcast(P)).then_inc(x1_in[i], 16)
                sp.dma_start(x1[i][:], x1_d[b].rearrange("(t p) c -> p t c", p=P)).then_inc(x1_in[i], 16)

        @block.scalar
        def _(act):
            def keep(b):
                act.wait_ge(res_done, b + 1)
                act.dma_start(out[b].rearrange("(t p) c -> p t c", p=P), res[b % 2][:]).then_inc(res_kept[b % 2], 16)

            for b in range(B):
                i = b % 2
                act.wait_ge(y_in[i], 32 * (b // 2 + 1))
                if b >= 2:
                    act.wait_ge(mix_done, b - 1)
                for tt in range(TT):
                    ins = nc.scalar.activation(first[i][:, tt, :], y12[i][:, 0, tt, :], ACT.Copy, scale=k.gates_all[:, b, tt:tt + 1])
                ins.then_inc(weighted, 1)
                if b:
                    keep(b - 1)
            keep(B - 1)
            for i in range(2):
                act.wait_ge(res_kept[i], 16 * (B // 2))

        @block.vector
        def _(dve):
            v = nc.vector
            for b in range(B):
                i = b % 2
                dve.wait_ge(weighted, b + 1)
                for tt in range(TT):
                    ins = v.scalar_tensor_tensor(out=mixed[i][:, tt, :], in0=y12[i][:, 1, tt, :],
                                                 scalar=k.gates_all[:, b, TT + tt:TT + tt + 1], in1=first[i][:, tt, :],
                                                 op0=ALU.mult, op1=ALU.add)
                ins.then_inc(mix_done, 1)
                dve.wait_ge(x1_in[i], 32 * (b // 2 + 1))
                dve.wait_ge(mix_done, b + 1)
                v.tensor_tensor(scaled[i][:], mixed[i][:], gb_row[i][:].unsqueeze(1).to_broadcast([P, TT, C]), ALU.mult
                                ).then_inc(mix_scaled, 1)
                if b >= 2:
                    dve.wait_ge(res_kept[i], 16 * (b // 2))
                dve.wait_ge(mix_scaled, b + 1)
                v.tensor_tensor(res[i][:], scaled[i][:], x1[i][:], ALU.add).then_inc(res_done, 1)
def build(nc, x, w_attn, b_qk, b_v, w_proj, b_proj, bias_table, onehot, wg, cT, wmod,
          w1, w3, w2, a1, a3, a2, lb1, lb3, lb2, b1, b3, b2, out):
    with ExitStack() as ctx:
        def dram(name, shape, dt=F32):
            return nc.dram_tensor(name, shape, dt, kind="Internal").ap()

        def sem(name):
            return ctx.enter_context(nc.semaphore(name))

        def sb(inner, name, shape, dt=F32):
            return inner.enter_context(nc.sbuf_tensor(name, shape, dt))

        line_d = dram("line_d", [H, P, LIN + 1])
        qk_d = [[dram(f"qk_d{i}{m}", [2, P, T]) for m in range(2)] for i in range(2)]
        x1_d = dram("x1_d", [B, T, C])
        rows_d = dram("rows_d", [E * REGION, C + 2])
        y_d = dram("y_d", [3 * B * T + FT, C])
        mod_d = dram("mod_d", [B, 4 * C])
        k = Kept()
        k.ident = sb(ctx, "ident", [P, P])
        k.ones = sb(ctx, "ones", [P, P])
        k.carry = sb(ctx, "carry", [P, E])
        k.gates_all = sb(ctx, "gates_all", [P, B, 2 * TT])
        with ExitStack() as inner:
            k.before = sb(inner, "before", [P, P])
            k.iota_e = sb(inner, "iota_e", [P, TT, E])
            k.region = sb(inner, "region", [P, TT, E])
            k.neghalf = sb(inner, "neghalf", [P, TT])
            k.bias_w = sb(inner, "bias_w", [P, H, T])
            k.wa = sb(inner, "wa", [P, KC, 3 * C])
            k.wp = sb(inner, "wp", [P, KC, C])
            k.wg_sb = sb(inner, "wg_sb", [P, KC, E])
            k.bqk = sb(inner, "bqk", [P, 2 * KC])
            k.bp_parts = sb(inner, "bp_parts", [P, C], F32R)
            k.ones_r = sb(inner, "ones_r", [P, P], F32R)
            k.bp_row = sb(inner, "bp_row", [1, C])
            k.sc = sb(inner, "sc", [P, KC, B])
            k.line = sb(inner, "line", [H, LIN])
            k.token = sb(inner, "token", [P, TT])
            k.to_next = sb(inner, "to_next", [P, TT])
            k.mod_c = sb(inner, "mod_c", [P, 2, KC, B])
            setup(nc, sem, w_attn, b_qk, b_v, w_proj, b_proj, bias_table, onehot, wg, cT, wmod, mod_d, k)
            attention(nc, sem, x, line_d, qk_d, x1_d, rows_d, mod_d, k)
        experts(nc, sem, w1, w3, w2, a1, a3, a2, lb1, lb3, lb2, b1, b3, b2, rows_d, y_d, k)
        combine(nc, sem, x1_d, y_d, mod_d, out, k)


def kernel(L0_attn_x, L0_attn_W_attn, L0_attn_b_attn, L0_attn_W_proj, L0_attn_b_proj, L0_attn_bias_table,
           L0_ffn_Wg, L0_ffn_W1, L0_ffn_b1, L0_ffn_A1, L0_ffn_B1, L0_ffn_W2, L0_ffn_b2, L0_ffn_A2, L0_ffn_B2,
           L0_ffn_W3, L0_ffn_b3, L0_ffn_A3, L0_ffn_B3, L0_c, L0_wmod):
    from concourse import bacc
    from concourse.bass_utils import run_bass_kernel_spmd

    def t(a, *axes):
        return np.transpose(np.asarray(a), axes)

    arrays = dict(
        x=L0_attn_x, w_attn=L0_attn_W_attn, b_qk=L0_attn_b_attn[:2 * C], b_v=L0_attn_b_attn[2 * C:],
        w_proj=L0_attn_W_proj, b_proj=L0_attn_b_proj, bias_table=L0_attn_bias_table, onehot=constants(),
        wg=t(L0_ffn_Wg, 1, 0), cT=t(L0_c, 1, 0), wmod=L0_wmod,
        w1=t(L0_ffn_W1, 0, 2, 1), w3=t(L0_ffn_W3, 0, 2, 1), w2=t(L0_ffn_W2, 0, 2, 1),
        a1=np.reshape(L0_ffn_A1, (E * R, C)), a3=np.reshape(L0_ffn_A3, (E * R, C)), a2=np.reshape(L0_ffn_A2, (E * R, HID)),
        lb1=t(L0_ffn_B1, 0, 2, 1).reshape(E * R, HID), lb3=t(L0_ffn_B3, 0, 2, 1).reshape(E * R, HID),
        lb2=t(L0_ffn_B2, 0, 2, 1).reshape(E * R, C), b1=L0_ffn_b1, b3=L0_ffn_b3, b2=L0_ffn_b2)
    arrays = {f"in_{name}": np.ascontiguousarray(a) for name, a in arrays.items()}
    nc = bacc.Bacc("TRN2", target_bir_lowering=False, num_devices=1)
    args = {name[3:]: nc.dram_tensor(name, a.shape, mybir.dt.from_np(a.dtype), kind="ExternalInput").ap()
            for name, a in arrays.items()}
    out = nc.dram_tensor("out_x", [B, T, C], F32, kind="ExternalOutput").ap()
    build(nc, out=out, **args)
    result = run_bass_kernel_spmd(nc, [arrays], core_ids=[0])
    return result.results[0]["out_x"]
```

```python
from contextlib import ExitStack

import numpy as np

import concourse.bass as bass
from concourse import mybir

F32 = mybir.dt.float32
F32R = mybir.dt.float32r
I32 = mybir.dt.int32
U32 = mybir.dt.uint32
ALU = mybir.AluOpType
ACT = mybir.ActivationFunctionType
AX = mybir.AxisListType

P = 128
B, T, C = 8, 512, 256
H = 16
D = C // H
E, R, HID = 8, 16, 512
TT = T // P
KC = C // P
HK = HID // P
HH = H // 2
NBUCKET = 32
EPS = 1e-5
MASKED = -1e30
LIN = T + P - 1
FT = 256
REGION = B * T + 2 * FT
BIG = 3e38
LOWROWS = 3 * 32
ACOLS = 2 * C + HID
LOWCOLS = ACOLS + 2 * HID + C

TILE_ORDER = [3, 2, 0, 1]
TILE_AT = {3: (0, 0), 2: (1, 0), 0: (1, 384), 1: (2, 0)}
EXPS_AFTER_SLOT = [1, 3, 4]
P_AT = {3: 0, 2: 512, 1: 896, 0: 1152}
TR_AT = {0: (0, 0), 1: (1, 0), 3: (1, 384), 2: (2, 0)}
PT_AT = {0: 0, 1: 512, 3: 896, 2: 1024}
TR_SLOT = [(0, 512), (512, 512), (1024, 256)]
NPROB = 1280

STEPS = H
AUX_PRO = ["hT0", "hT1", "q", "k"]
AUX_MID = {0: "q1", 1: "k1", 2: "ytr2", 3: "v0", 5: "v1", 6: "ytr3", 7: "yT1", 9: "hT0", 10: "q", 11: "k",
           12: "ytr0", 13: "h2T0", 14: "lg", 15: "pos"}
AUX_END = {6: "yT0", 7: "pr0", 8: "pr1", 9: "hT1", 13: "h2T1", 14: "ytr1"}
POST = ["ytr2", "ytr3", "yT0", "yT1", "pr0", "pr1", "h2T0", "h2T1", "lg", "pos"]
AHEAD = ["hT0", "hT1", "q", "k"]
LONG = ["q", "k", "q1", "k1", "v0", "v1", "pr0", "pr1", "lg", "pos"]
NORM_STEP = 11
LAG = 2
PV_PARTS = [[0], [1], [2, 3]]
PV_AT = {6: (0, 0, 0), 7: (0, 0, 1), 9: (0, 0, 2), 10: (0, 1, 0), 11: (0, 1, 1), 12: (0, 1, 2),
         14: (0, 2, 0), 15: (0, 2, 1), 0: (1, 2, 2), 2: (1, 3, 0), 3: (1, 3, 1), 4: (1, 3, 2)}


def step_tasks(kind, i, places=(AUX_MID, AUX_END)):
    names = [place[i] for place in places if i in place]
    if kind == "end":
        return [t for t in names if t in POST]
    skip = POST if kind == "first" else AHEAD if kind == "last" else []
    return [t for t in names if t not in skip]


def reads_of(kind, i, place):
    here = step_tasks(kind, i, [(AUX_MID, AUX_END)[place]])
    before = step_tasks(kind, i, [AUX_MID]) if place else step_tasks(kind, i - 1, [AUX_END])
    return [t for t in before if t in LONG] + [t for t in here if t not in LONG]


def tasks(kind):
    return [t for i in range(STEPS) for t in step_tasks(kind, i)]


def start_turn(kind, b):
    pro, first, loop, last = len(AUX_PRO), len(tasks("first")), len(tasks("loop")), len(tasks("last"))
    if kind == "pro":
        return 0
    if kind == "first":
        return pro
    if kind == "loop":
        return b * loop + (pro + first - loop)
    return pro + first + (B - 2) * loop + (last if kind == "end" else 0)


def turn_of(kind, b, name):
    names = AUX_PRO if kind == "pro" else tasks(kind)
    return start_turn(kind, b) + names.index(name)


def transposed_head(kind, b, i):
    if i >= LAG:
        return None if kind == "end" else (b, i - LAG)
    return None if kind == "first" else (b - 1, H - LAG + i)


def values_part(kind, b, i):
    if i not in PV_AT:
        return None
    back, g, part = PV_AT[i]
    if (back and kind == "first") or (not back and kind == "end"):
        return None
    return b - back, g, part


def each_batch(eng, body):
    body("first", 0)
    with eng.Fori(1, B - 1) as b:
        body("loop", b)
    body("last", B - 1)
    body("end", B)


def constants():
    v = np.arange(LIN)
    dist = (T - P) + (P - 1) - v
    rp = np.maximum(dist, 0)
    max_exact = NBUCKET // 2
    large = max_exact + (np.log(np.maximum(rp, 1).astype(np.float32) / np.float32(max_exact))
                         / np.float32(np.log(128 / max_exact)) * np.float32(NBUCKET - max_exact)).astype(np.int32)
    bucket = np.where(rp < max_exact, rp, np.minimum(large, NBUCKET - 1))
    bucket = np.where(dist < 0, NBUCKET, bucket)
    onehot = np.zeros((NBUCKET + 1, LIN), np.float32)
    onehot[bucket, v] = 1.0
    return onehot


def setup(nc, sem, x, w_attn, b_qk, b_v, w_proj, b_proj, bias_table, onehot, wg, cT, wmod, mod_d, k):
    with ExitStack() as ctx:
        def sb(name, shape, dt=F32):
            return ctx.enter_context(nc.sbuf_tensor(name, shape, dt))

        table = sb("table", [NBUCKET + 1, H])
        oh_line = sb("oh_line", [NBUCKET + 1, LIN])
        c_raw = sb("c_raw", [P, KC, B])
        wmod_cols = sb("wmod_cols", [P, KC, 2 * C])
        bv_col = sb("bv_col", [P, KC])
        wm_rows = sb("wm_rows", [P, KC, 4, C])
        sign = sb("sign", [B, 2, C])
        mod_rows = sb("mod_rows", [B, 4, C])
        mod_g = mod_rows[:, 0:4:3, :]
        token_i = sb("token_i", [P, TT], I32)
        pad_i = sb("pad_i", [P, 2, 2], I32)
        iota_i = sb("iota_i", [P, TT, E], I32)
        region_i = sb("region_i", [P, TT, E], I32)
        line_ps = ctx.enter_context(nc.psum_tensor("line_ps", [P, 2, 512], F32))
        mod_ps = ctx.enter_context(nc.psum_tensor("mod_ps", [P, 512], F32))
        row_ps = ctx.enter_context(nc.psum_tensor("row_ps", [P, 2, 512], F32))
        bv_ps = ctx.enter_context(nc.psum_tensor("bv_ps", [P, 512], F32))
        loaded, masked, silu_done, line_made, rows_made, rows_step, rows_kept = (
            sem(n) for n in ("loaded", "masked", "silu_done", "line_made", "rows_made", "rows_step", "rows_kept"))
        mod_made, bv_made, scaled, ones_set, iotas, bp_step, g_signed, pad_cleared = (
            sem(n) for n in ("mod_made", "bv_made", "scaled", "ones_set", "iotas", "bp_step", "g_signed", "pad_cleared"))
        block = ctx.enter_context(nc.Block())
        x0_in, x0_step = sem("x0_in"), sem("x0_step")
        stats, mv, var, rstd = (sb(n, [P, TT, w]) for n, w in (("stats", 6), ("mv", 2), ("var", 1), ("rstd", 1)))
        NLOAD = 11

        @block.sync
        def _(sp):
            sp.dma_start(k.xin[:], x[0].rearrange("(t p) c -> p t c", p=P)).then_inc(x0_in, 16)
            sp.dma_start(table[0:NBUCKET, :], bias_table).then_inc(loaded, 16)
            sp.dma_start(oh_line[:], onehot).then_inc(loaded, 16)
            sp.dma_start(c_raw[:], cT.rearrange("(k p) b -> p k b", p=P)).then_inc(loaded, 16)
            sp.dma_start(wmod_cols[:], wmod[:, 0:2 * C].rearrange("(k p) n -> p k n", p=P)).then_inc(loaded, 16)
            sp.dma_start(k.wa[:], w_attn.rearrange("(k p) n -> p k n", p=P)).then_inc(loaded, 16)
            sp.dma_start(k.bqk[:], b_qk.rearrange("(m p) -> p m", p=P), allow_slow_non_contiguous=True).then_inc(loaded, 16)
            sp.dma_start(bv_col[:], b_v.rearrange("(m p) -> p m", p=P), allow_slow_non_contiguous=True).then_inc(loaded, 16)
            sp.dma_start(k.bp_row[:], b_proj.rearrange("(a n) -> a n", a=1)).then_inc(loaded, 16)
            sp.dma_start(k.wp[:], w_proj.rearrange("(k p) n -> p k n", p=P)).then_inc(loaded, 16)
            sp.dma_start(k.wg_sb[:], wg.rearrange("(k p) e -> p k e", p=P)).then_inc(loaded, 16)
            sp.dma_start(wm_rows[:].rearrange("p k n c -> p k (n c)"), wmod[:, 2 * C:6 * C].rearrange("(k p) n -> p k n", p=P)
                         ).then_inc(loaded, 16)
            sp.wait_ge(rows_step, 4)
            sp.dma_start(mod_d, mod_rows[:].rearrange("b n c -> b (n c)")).then_inc(rows_kept, 16)
            sp.wait_ge(rows_kept, 16)

        @block.tensor
        def _(pe):
            pe.wait_ge(loaded, 16 * NLOAD)
            pe.wait_ge(masked, 1)
            pe.matmul(line_ps[0:H, 0, :], table[:], oh_line[:, 0:512], start=True, stop=True).then_inc(line_made, 1)
            pe.matmul(line_ps[0:H, 1, 0:LIN - 512], table[:], oh_line[:, 512:LIN], start=True, stop=True
                      ).then_inc(line_made, 1)
            pe.wait_ge(silu_done, 1)
            for part in range(2):
                for m in range(KC):
                    col = (part * KC + m) * B
                    for kc in range(KC):
                        mm = pe.matmul(mod_ps[:, col:col + B], wmod_cols[:, kc, part * C + m * P:part * C + (m + 1) * P],
                                       k.sc[:, kc, :], start=(kc == 0), stop=(kc == KC - 1))
            mm.then_inc(mod_made, 1)
            for kc in range(KC):
                mm = pe.matmul(bv_ps[0:1, 0:C], bv_col[:, kc:kc + 1], k.wp[:, kc, :], start=(kc == 0), stop=(kc == KC - 1))
            mm.then_inc(bv_made, 1)
            for n in range(2):
                for kc in range(KC):
                    mm = pe.matmul(row_ps[0:B, n, :], k.sc[:, kc, :], wm_rows[:, kc, 2 * n:2 * n + 2, :].rearrange("p a n -> p (a n)"),
                                   start=(kc == 0), stop=(kc == KC - 1))
            mm.then_inc(rows_made, 1)

        @block.scalar
        def _(act):
            act.wait_ge(loaded, 16 * NLOAD)
            nc.scalar.activation(k.sc[:], c_raw[:], ACT.Silu).then_inc(silu_done, 1)
            nc.scalar.mul(k.wa[:, :, 0:C], k.wa[:, :, 0:C], D ** -0.5)
            nc.scalar.mul(k.bqk[:, 0:KC], k.bqk[:, 0:KC], D ** -0.5).then_inc(scaled, 1)
            act.wait_ge(line_made, 2)
            nc.scalar.copy(k.line[:, 0:512], line_ps[0:H, 0, :])
            nc.scalar.copy(k.line[:, 512:LIN], line_ps[0:H, 1, 0:LIN - 512])

        @block.vector
        def _(dve):
            v = nc.vector
            v.memset(table[NBUCKET:NBUCKET + 1, :], MASKED).then_inc(masked, 1)
            v.memset(k.carry[:], 0.0)
            v.memset(k.neghalf[:], -0.5)
            v.memset(k.zeros[:], 0.0)
            v.memset(k.to_next[:], float(T))
            dve.wait_ge(iotas, 4)
            for n, pad in enumerate((k.padding, k.preset)):
                v.memset(pad[:], 0.0).then_inc(pad_cleared, 1)
                dve.wait_ge(pad_cleared, n + 1)
                v.tensor_copy(pad[:, :, C], pad_i[:, n, :])
            v.tensor_copy(k.token[:], token_i[:])
            v.tensor_copy(k.iota_e[:], iota_i[:])
            v.tensor_copy(k.region[:], region_i[:])
            v.memset(k.bp_parts[:].bitcast(F32), 0.0).then_inc(bp_step, 1)
            dve.wait_ge(x0_in, 16)
            for tt in range(TT):
                ins = v.bn_stats(stats[:, tt, :], k.xin[:, tt, :])
            ins.then_inc(x0_step, 1)
            dve.wait_ge(x0_step, 1)
            for tt in range(TT):
                ins = v.bn_aggr(mv[:, tt, :], stats[:, tt, :])
            ins.then_inc(x0_step, 1)
            dve.wait_ge(x0_step, 2)
            v.tensor_scalar(var[:, :, 0], mv[:, :, 1], EPS, None, ALU.add).then_inc(x0_step, 1)
            dve.wait_ge(x0_step, 4)
            for tt in range(TT):
                v.tensor_scalar(k.xin[:, tt, :], k.xin[:, tt, :], mv[:, tt, 0:1], rstd[:, tt, :], ALU.subtract, ALU.mult)
            dve.wait_ge(mod_made, 1)
            v.tensor_copy(k.mod_c[:, 0, :, :], mod_ps[:, 0:KC * B].rearrange("p (k b) -> p k b", k=KC))
            v.tensor_scalar(k.mod_c[:, 1, :, :], mod_ps[:, KC * B:2 * KC * B].rearrange("p (k b) -> p k b", k=KC),
                            1.0, None, ALU.add)
            dve.wait_ge(bv_made, 1)
            v.tensor_tensor(k.bp_row[:], k.bp_row[:], bv_ps[0:1, 0:C], ALU.add).then_inc(bp_step, 1)
            dve.wait_ge(bp_step, 2)
            v.tensor_copy(k.bp_parts[0:1, :], k.bp_row[:]).then_inc(bp_step, 1)
            dve.wait_ge(bp_step, 3)
            v.tensor_tensor(k.bp_parts[32:33, :], k.bp_row[:], k.bp_parts[0:1, :].bitcast(F32), ALU.subtract)
            dve.wait_ge(ones_set, 1)
            v.tensor_copy(k.ones_r[:], k.ones[:])
            dve.wait_ge(rows_made, 1)
            v.tensor_copy(mod_rows[:], row_ps[0:B, :, :].rearrange("b a (n c) -> b (a n) c", n=2)).then_inc(rows_step, 1)
            dve.wait_ge(rows_step, 1)
            v.tensor_scalar(mod_rows[:, 2, :], mod_rows[:, 2, :], 1.0, None, ALU.add)
            v.tensor_scalar(sign[:], mod_g, 0.0, 2.0, ALU.is_ge, ALU.mult).then_inc(rows_step, 1)
            dve.wait_ge(rows_step, 2)
            v.tensor_scalar(sign[:], sign[:], -1.0, None, ALU.add).then_inc(rows_step, 1)
            dve.wait_ge(rows_step, 3)
            v.tensor_tensor(mod_g, sign[:], mod_g, ALU.mult).then_inc(g_signed, 1)
            dve.wait_ge(g_signed, 1)
            v.scalar_tensor_tensor(out=mod_g, in0=mod_g, scalar=0.25, in1=sign[:], op0=ALU.max, op1=ALU.mult
                                   ).then_inc(rows_step, 1)

        @block.gpsimd
        def _(pool):
            g = nc.gpsimd
            g.iota(iota_i[:], [[0, TT], [1, E]], base=0, channel_multiplier=0).then_inc(iotas, 1)
            g.iota(region_i[:], [[0, TT], [REGION, E]], base=0, channel_multiplier=0).then_inc(iotas, 1)
            g.iota(token_i[:], [[P, TT]], base=-T, channel_multiplier=1).then_inc(iotas, 1)
            g.iota(pad_i[:], [[FT, 2], [P, 2]], base=2 * B * T, channel_multiplier=1).then_inc(iotas, 1)
            g.memset(k.ones[:], 1.0).then_inc(ones_set, 1)
            pool.wait_ge(ones_set, 1)
            g.affine_select(k.ident[:], k.ones[:], [[1, P]], ALU.is_equal, 0.0, base=0, channel_multiplier=-1)
            g.affine_select(k.before[:], k.ones[:], [[1, P]], ALU.is_gt, 0.0, base=0, channel_multiplier=-1)
            pool.wait_ge(x0_step, 3)
            g.tensor_tensor(rstd[:, :, 0], var[:, :, 0], k.neghalf[:], ALU.pow).then_inc(x0_step, 1)


class Kept:
    pass


def attention(nc, sem, x, line_d, qk_d, x1_d, rows_d, mod_d, k):
    with ExitStack() as ctx:
        def sb(name, shape, dt=F32):
            return ctx.enter_context(nc.sbuf_tensor(name, shape, dt))

        q_st = [sb(f"q_st{m}", [P, HH, T], F32R) for m in range(2)]
        k_st = [sb(f"k_st{m}", [P, HH // 2, T], F32R) for m in range(2)]
        v_sb = [sb(f"v_sb{m}", [P, TT, HH, 2 * D]) for m in range(2)]
        probs = [sb(f"probs{i}", [P, NPROB]) for i in range(4)]
        probs_t = sb("probs_t", [P, 8, NPROB])
        neg_max = sb("neg_max", [P, 4, TT])
        part_hi = [sb(f"part_hi{i}", [P, T], F32R) for i in range(2)]
        part_lo = [sb(f"part_lo{i}", [P, T], F32R) for i in range(2)]
        mod_b = sb("mod_b", [P, 2, KC])
        xin = k.xin
        h_t = sb("h_t", [P, KC, T])
        stats = [sb(f"stats{i}", [P, TT, 6]) for i in range(2)]
        mv = [sb(f"mv{i}", [P, TT, 2]) for i in range(2)]
        var = [sb(f"var{i}", [P, TT]) for i in range(2)]
        shift = sb("shift", [P, TT])
        rstd = [sb(f"rstd{i}", [P, TT]) for i in range(2)]
        y_un = sb("y_un", [P, T])
        recips = sb("recips", [P, TT, 4])
        y_tok = sb("y_tok", [P, TT, C])
        y_t = sb("y_t", [P, KC, T])
        mod_row = sb("mod_row", [P, 3, C])
        rows = sb("rows", [P, TT, C + 2])
        h2 = rows[:, :, 0:C]
        x1 = sb("x1", [P, TT, C])
        h2_t = y_t
        logits = sb("logits", [P, TT, E])
        top8 = sb("top8", [P, TT, 8])
        idx8 = sb("idx8", [P, TT, 8], U32)
        idxf = sb("idxf", [P, 2, TT])
        chosen = sb("chosen", [P, 2, TT, E])
        both = sb("both", [P, TT, E])
        both_sum = sb("both_sum", [P, E])
        gap = sb("gap", [P, TT])
        gexp = sb("gexp", [P, TT])
        gden = sb("gden", [P, TT])
        gates = sb("gates", [P, 2, TT])
        place = sb("place", [P, TT, E])
        chosen_place = sb("chosen_place", [P, 2, TT, E])
        slot_f = sb("slot_f", [P, 2, TT])
        slot_b = sb("slot_b", [P, 2 * TT], I32)

        s_bank = [ctx.enter_context(nc.psum_tensor(f"s_bank{i}", [P, 512], F32)) for i in range(4)]
        t_bank = [ctx.enter_context(nc.psum_tensor(f"t_bank{i}", [P, 512], F32)) for i in range(2)]
        y_bank = ctx.enter_context(nc.psum_tensor("y_bank", [P, 512], F32))
        aux = ctx.enter_context(nc.psum_tensor("aux", [P, 512], F32))

        cleared = sem("cleared")
        x_in, xr_in, x1_kept, scattered, preset_in = (
            sem(n) for n in ("x_in", "xr_in", "x1_kept", "scattered", "preset_in"))
        bias_in = [sem(f"bias_in{i}") for i in range(4)]
        lines_out = [sem(f"lines_out{i}") for i in range(4)]
        scored, biased, exped, transposed = (sem(n) for n in ("scored", "biased", "exped", "transposed"))
        pt_dve, pt_act, pv_done, y_copied, y_recip = (sem(n) for n in ("pt_dve", "pt_act", "pv_done", "y_copied", "y_recip"))
        aux_ready, aux_free, hi_done = (sem(n) for n in ("aux_ready", "aux_free", "hi_done"))
        stored = [sem(f"stored{i}") for i in range(2)]
        stacked = [sem(f"stacked{i}") for i in range(2)]
        stats_done, mv_done, var_done, rstd_done, normed = (
            [sem(f"{n}{i}") for i in range(2)] for n in ("stats_done", "mv_done", "var_done", "rstd_done", "normed"))
        shift_step = sem("shift_step")
        mod_b_set, x1_done, h2_scaled, h2_done, rows_named, rows_free = (
            sem(n) for n in ("mod_b_set", "x1_done", "h2_scaled", "h2_done", "rows_named", "rows_free"))
        top_done, idx_done, idxf_done, chosen_done, both_done, summed, carried, gap_done, exp_done, den_done, g1_done, g2_done = (
            sem(n) for n in ("top_done", "idx_done", "idxf_done", "chosen_done", "both_done", "summed", "carried",
                             "gap_done", "exp_done", "den_done", "g1_done", "g2_done"))
        weighed, slot_f_done, slot_done, kept = (sem(n) for n in ("weighed", "slot_f_done", "slot_done", "kept"))

        def nth_part(kind, b, name):
            return 1 if kind == "pro" else 2 * b + (2 if name[1:] else 3)

        def write_lines(eng, g):
            heads = slice(4 * g, 4 * g + 4)
            eng.dma_start(line_d[heads, :, 0:LIN], k.line[heads, :].unsqueeze(1).to_broadcast([4, P, LIN])).then_inc(lines_out[g], 16)

        def load_bias(eng, g):
            heads = slice(4 * g, 4 * g + 4)
            eng.wait_ge(lines_out[g], 16)
            skewed = line_d[heads].rearrange("h r u -> h (r u)")[:, P - 1:P - 1 + P * LIN].rearrange("h (p u) -> p h u", u=LIN)
            eng.dma_start(k.bias_w[:, heads, :], skewed[:, :, 0:T]).then_inc(bias_in[g], 16)

        block = ctx.enter_context(nc.Block())

        @block.sync
        def _(sp):
            def load_x(b):
                sp.dma_start(xin[:], x[b].rearrange("(t p) c -> p t c", p=P)).then_inc(x_in, 16)

            def stack(kind, b, name):
                i, m = (0 if name[0] == "q" else 1), (1 if name[1:] else 0)
                sp.wait_ge(aux_free, turn_of(kind, b, name) + 1)
                d = qk_d[i][m]
                n = nth_part(kind, b, name)
                sp.dma_start(d[0], part_hi[i][:].bitcast(F32)).then_inc(stored[i], 16)
                sp.dma_start(d[1], part_lo[i][:].bitcast(F32)).then_inc(stored[i], 16)
                sp.wait_ge(stored[i], 32 * n)
                for hh in range(2):
                    for blk in range(4):
                        part = blk % 2 if i == 0 else blk // 2
                        rows = slice(64 * hh + D * blk, 64 * hh + D * (blk + 1))
                        src = d[part].rearrange("(r a d) t -> a d r t", a=2, d=D)[hh]
                        dst = (q_st[m][rows, hh:HH:2, :] if i == 0 else k_st[m][rows, :, :]).bitcast(F32)
                        sp.dma_start(dst, src).then_inc(stacked[i], 16)

            def load_residual(p):
                sp.wait_ge(rows_free, p + 1)
                sp.dma_start(h2, x[p].rearrange("(t p) c -> p t c", p=P)).then_inc(xr_in, 16)
                sp.dma_start(mod_row[:].rearrange("p n c -> p (n c)"),
                             mod_d[bass.ds(p, 1), 0:3 * C].partition_broadcast(P)).then_inc(xr_in, 16)

            def keep_x1(p):
                sp.wait_ge(x1_done, p + 1)
                sp.dma_start(x1_d[p].rearrange("(t p) c -> p t c", p=P), x1[:]).then_inc(x1_kept, 16)

            sp.sem_inc(x1_kept, 16)
            write_lines(sp, 0)
            load_bias(sp, 0)
            sp.wait_ge(cleared, 1)
            stack("pro", 0, "q")
            stack("pro", 0, "k")
            sp.wait_ge(aux_free, 2)
            load_x(1)
            def body(kind, b):
                if kind == "loop":
                    sp.wait_ge(aux_free, start_turn(kind, b))
                    load_x(b + 1)
                if kind == "first":
                    sp.wait_ge(cleared, 4)
                for i in range(STEPS):
                    if i == 2 and kind != "first":
                        load_residual(b - 1)
                    for name in step_tasks(kind, i):
                        if name in ("q1", "k1", "q", "k"):
                            stack(kind, b, name)
                    if i == 9 and kind != "first":
                        keep_x1(b - 1)

            each_batch(sp, body)
            sp.wait_ge(x1_kept, 16 * (B + 1))

        @block.tensor
        def _(pe):
            def task(kind, b, name):
                turn = turn_of(kind, b, name)
                if kind != "pro" or turn:
                    pe.wait_ge(aux_free, turn)
                bb = 0 if kind == "pro" else b + 1 if name in AHEAD else b - 1 if name in POST else b
                m = 1 if name[1:] == "1" else 0
                if name[:2] == "hT":
                    kc = int(name[-1])
                    if kind != "pro":
                        pe.wait_ge(normed[0], bb)
                    for tt in range(TT):
                        mm = pe.transpose(aux[:, tt * P:(tt + 1) * P], xin[:, tt, kc * P:(kc + 1) * P], k.ident[:])
                elif name in ("q", "q1", "k", "k1"):
                    col = (C if name[0] == "k" else 0) + m * P
                    for kc in range(KC):
                        mm = pe.matmul(aux[:, :], k.wa[:, kc, col:col + P], h_t[:, kc, :], start=(kc == 0), stop=(kc == KC - 1))
                elif name in ("v0", "v1"):
                    col = 2 * C + m * P
                    for tt in range(TT):
                        for kc in range(KC):
                            mm = pe.matmul(aux[:, tt * P:(tt + 1) * P], h_t[:, kc, tt * P:(tt + 1) * P],
                                           k.wa[:, kc, col:col + P], start=(kc == 0), stop=(kc == KC - 1))
                elif name[:3] == "ytr":
                    pe.wait_ge(y_copied, 4 * bb + int(name[-1]) + 1)
                    for tt in range(TT):
                        mm = pe.transpose(aux[:, tt * P:(tt + 1) * P], y_un[:, tt * P:(tt + 1) * P], k.ident[:])
                elif name[:2] == "yT":
                    kc = int(name[-1])
                    for tt in range(TT):
                        mm = pe.transpose(aux[:, tt * P:(tt + 1) * P], y_tok[:, tt, kc * P:(kc + 1) * P], k.ident[:])
                elif name[:2] == "pr":
                    for u in range(2):
                        tt = 2 * int(name[-1]) + u
                        cols = slice(u * C, (u + 1) * C)
                        for kc in range(KC):
                            pe.matmul(aux[:, cols], y_t[:, kc, tt * P:(tt + 1) * P], k.wp[:, kc, :], start=(kc == 0), stop=False)
                        mm = pe.matmul(aux[:, cols], k.ones_r[:], k.bp_parts[:], start=False, stop=True)
                elif name[:3] == "h2T":
                    kc = int(name[-1])
                    pe.wait_ge(h2_done, bb + 1)
                    for tt in range(TT):
                        mm = pe.transpose(aux[:, tt * P:(tt + 1) * P], h2[:, tt, kc * P:(kc + 1) * P], k.ident[:])
                elif name == "lg":
                    for tt in range(TT):
                        for kc in range(KC):
                            mm = pe.matmul(aux[:, tt * E:(tt + 1) * E], h2_t[:, kc, tt * P:(tt + 1) * P], k.wg_sb[:, kc, :],
                                           start=(kc == 0), stop=(kc == KC - 1))
                elif name == "pos":
                    pe.wait_ge(both_done, bb + 1)
                    pe.wait_ge(carried, bb + 1)
                    pe.matmul(aux[:, 0:TT * E], k.before[:], both[:].rearrange("p t e -> p (t e)"), start=True, stop=False)
                    for u in range(TT - 1):
                        pe.matmul(aux[:, (u + 1) * E:TT * E], k.ones[:], both[:, u:u + 1, :].to_broadcast([P, TT - 1 - u, E]),
                                  start=False, stop=False)
                    mm = pe.matmul(aux[:, 0:TT * E], k.ones[:], k.carry[:].unsqueeze(1).to_broadcast([P, TT, E]),
                                   start=False, stop=True)
                mm.then_inc(aux_ready, 1)

            def scores(kind, b, h, slots):
                m, hl = h // HH, h % HH
                if hl == 0 and 0 in slots:
                    for i in range(2):
                        pe.wait_ge(stacked[i], 128 * (2 * b + m + 1))
                for j in TILE_ORDER:
                    slot, col = TILE_AT[j]
                    if slot not in slots:
                        continue
                    n = 3 * h + slot
                    if col == 0 and (kind != "first" or n >= 4):
                        pe.wait_ge(exped, 4 * H * b + 4 * ((n - 4) // 3) + EXPS_AFTER_SLOT[(n - 4) % 3])
                    w = (j + 1) * P
                    mm = pe.matmul(s_bank[n % 4][:, col:col + w], q_st[m][:, hl, j * P:(j + 1) * P],
                                   k_st[m][:, hl // 2, 0:w], start=True, stop=True)
                    if j != 2:
                        mm.then_inc(scored, 1)

            def transposes(kind, b, h, slots):
                if 0 in slots:
                    pe.wait_ge(exped, 4 * H * b + 4 * (h + 1))
                for slot in slots:
                    n = 3 * h + slot
                    if n >= 2 or kind != "first":
                        hp, sp_ = (n - 2) // 3, (n - 2) % 3
                        if sp_ == 0:
                            pe.wait_ge(pt_dve, H * b + hp + 1)
                        else:
                            pe.wait_ge(pt_act, 2 * H * b + 2 * hp + sp_)
                    for st in (s for s in (0, 1, 3, 2) if TR_AT[s][0] == slot):
                        for j in range(st, TT):
                            col = TR_AT[st][1] + (j - st) * P
                            src = P_AT[j] + st * P
                            mm = pe.transpose(t_bank[n % 2][:, col:col + P], probs[h % 4][:, src:src + P], k.ident[:])
                    mm.then_inc(transposed, 1)

            def values(kind, b, g, part):
                m = g // 2
                if part == 0:
                    pe.wait_ge(pt_dve, H * b + 4 * (g + 1))
                    pe.wait_ge(pt_act, 2 * H * b + 8 * (g + 1))
                    if kind != "first" or g:
                        pe.wait_ge(y_copied, 4 * b + g)
                for st in PV_PARTS[part]:
                    w = (TT - st) * P
                    for hq in range(4):
                        h = 4 * g + hq
                        mm = pe.matmul(y_bank[32 * hq:32 * hq + 32, st * P:T], v_sb[m][:, st, h % HH, :],
                                       probs_t[:, h % 8, PT_AT[st]:PT_AT[st] + w], start=(st == 0), stop=(st == TT - 1),
                                       skip_group_check=True)
                if part == len(PV_PARTS) - 1:
                    mm.then_inc(pv_done, 1)

            for name in AUX_PRO:
                task("pro", 0, name)
            scores("first", 0, 0, (0, 1))

            def body(kind, b):
                for i in range(STEPS):
                    turned, part = transposed_head(kind, b, i), values_part(kind, b, i)
                    after = ((kind, b, i + 1) if i + 1 < H else ("loop", b + 1, 0)) if kind != "end" else None
                    if kind == "last" and i + 1 == H:
                        after = None
                    if kind != "end":
                        scores(kind, b, i, (2,))
                    if turned:
                        transposes(kind, *turned, (1,))
                    if after:
                        scores(*after, (0,))
                    for name in step_tasks(kind, i, [AUX_MID]):
                        task(kind, b, name)
                    if turned:
                        transposes(kind, *turned, (2,))
                    if after:
                        scores(*after, (1,))
                    if i + 1 < STEPS:
                        turned = transposed_head(kind, b, i + 1)
                    else:
                        turned = (b, H - LAG) if kind != "end" else None
                    if turned:
                        transposes(kind if i + 1 < STEPS else "loop", *turned, (0,))
                    if part:
                        values(kind, *part)
                    for name in step_tasks(kind, i, [AUX_END]):
                        task(kind, b, name)

            each_batch(pe, body)

        @block.scalar
        def _(act):
            def task(kind, b, name):
                turn = turn_of(kind, b, name)
                bb = 0 if kind == "pro" else b + 1 if name in AHEAD else b - 1 if name in POST else b
                if name == "pos":
                    act.wait_ge(gap_done, bb + 1)
                    nc.scalar.activation(gexp[:], gap[:], ACT.Exp).then_inc(exp_done, 1)
                if name not in ("hT0", "hT1", "q", "q1", "k", "k1", "v0", "v1", "yT0", "yT1", "h2T0", "h2T1"):
                    return
                act.wait_ge(aux_ready, turn + 1)
                m = 1 if name[1:] == "1" else 0
                if name[:2] == "hT":
                    kc = int(name[-1])
                    act.wait_ge(mod_b_set, bb + 1)
                    nc.scalar.activation(h_t[:, kc, :], aux[:, :], ACT.Identity, bias=mod_b[:, 0, kc:kc + 1],
                                         scale=mod_b[:, 1, kc:kc + 1]).then_inc(aux_free, 1)
                elif name[0] in "qk":
                    i = 0 if name[0] == "q" else 1
                    if kind != "pro":
                        act.wait_ge(stored[i], 32 * (nth_part(kind, b, name) - 1))
                    nc.scalar.activation(part_hi[i][:], aux[:, :], ACT.Identity, bias=k.bqk[:, 2 * i + m:2 * i + m + 1]
                                         ).then_inc(hi_done, 1)
                elif name[0] == "v":
                    if kind == "first":
                        act.wait_ge(cleared, 4)
                    nc.scalar.copy(v_sb[m][:, :, :, 0:D], aux[:, :].rearrange("p (t h d) -> p t h d", t=TT, d=D)
                                   ).then_inc(aux_free, 1)
                elif name[:2] == "yT":
                    nc.scalar.copy(y_t[:, int(name[-1]), :], aux[:, :]).then_inc(aux_free, 1)
                elif name[:3] == "h2T":
                    nc.scalar.copy(h2_t[:, int(name[-1]), :], aux[:, :]).then_inc(aux_free, 1)

            def exps(kind, b, i, slots):
                if 0 in slots and (kind != "first" or i >= 4):
                    act.wait_ge(transposed, 3 * H * b + 3 * (i - 3))
                for j in TILE_ORDER:
                    slot, col = TILE_AT[j]
                    if slot not in slots:
                        continue
                    w = (j + 1) * P
                    act.wait_ge(biased, 4 * H * b + 4 * i + EXPS_AFTER_SLOT[slot])
                    nc.scalar.activation(probs[i % 4][:, P_AT[j]:P_AT[j] + w], s_bank[(3 * i + slot) % 4][:, col:col + w],
                                         ACT.Exp, bias=neg_max[:, i % 4, j:j + 1], scale=-1.0).then_inc(exped, 1)

            def copy_transposed(kind, b, h, slot):
                act.wait_ge(transposed, 3 * H * b + 3 * h + slot + 1)
                if slot == 1 and (kind != "first" or h >= 8):
                    act.wait_ge(pv_done, 4 * b + h // 4 - 1)
                at, w = TR_SLOT[slot]
                nc.scalar.copy(probs_t[:, h % 8, at:at + w], t_bank[(3 * h + slot) % 2][:, 0:w]).then_inc(pt_act, 1)

            def copy_sums(kind, b, i, p, g):
                act.wait_ge(pv_done, 4 * p + g + 1)
                if g == 2:
                    act.wait_ge(aux_free, start_turn(kind, b))
                elif g or kind != "first":
                    act.wait_ge(aux_free, turn_of(kind, b, f"ytr{(g - 1) % 4}") + 1)
                nc.scalar.copy(y_un[:, :], y_bank[:, :]).then_inc(y_copied, 1)

            for name in AUX_PRO:
                task("pro", 0, name)

            def body(kind, b):
                for i in range(STEPS):
                    turned, part = transposed_head(kind, b, i), values_part(kind, b, i - 1)
                    if kind == "first" and i in (1, 4, 8):
                        write_lines(act, (1, 4, 8).index(i) + 1)
                    if kind == "first" and i in (3, 6, 10):
                        load_bias(act, (3, 6, 10).index(i) + 1)
                    if kind == "first" and i == 12:
                        for e in range(E):
                            act.dma_start(rows_d[e * REGION + FT:e * REGION + 2 * FT, :].rearrange("(u p) c -> p u c", p=P), k.preset[:]
                                         ).then_inc(preset_in, 16)
                    if kind != "end":
                        exps(kind, b, i, (0,))
                    if turned:
                        copy_transposed(kind, *turned, 1)
                    if kind != "end":
                        exps(kind, b, i, (1,))
                    if part and part[2] == len(PV_PARTS) - 1:
                        copy_sums(kind, b, i, *part[:2])
                    for name in reads_of(kind, i, 0):
                        task(kind, b, name)
                    for name in reads_of(kind, i, 1):
                        if name in LONG:
                            task(kind, b, name)
                    if turned:
                        copy_transposed(kind, *turned, 2)
                    if kind != "end":
                        exps(kind, b, i, (2,))
                    for name in reads_of(kind, i, 1):
                        if name not in LONG:
                            task(kind, b, name)
                    if i == NORM_STEP and kind in ("loop", "last"):
                        act.wait_ge(shift_step, 2 * b)
                        for tt in range(TT):
                            ins = nc.scalar.activation(rows[:, tt, 0:C], x1[:, tt, :], ACT.Identity, bias=shift[:, tt:tt + 1],
                                                       scale=rstd[1][:, tt:tt + 1])
                        ins.then_inc(normed[1], 1)

            each_batch(act, body)

        @block.vector
        def _(dve):
            v = nc.vector

            def ln_stats(i, n, src, ready, value):
                dve.wait_ge(ready, value)
                dve.nop(nofuse=True)
                for tt in range(TT):
                    ins = v.bn_stats(stats[i][:, tt, :], src[:, tt, :])
                ins.then_inc(stats_done[i], 1)
                dve.wait_ge(stats_done[i], n)
                dve.nop(nofuse=True)
                for tt in range(TT):
                    ins = v.bn_aggr(mv[i][:, tt, :], stats[i][:, tt, :])
                ins.then_inc(mv_done[i], 1)

            def router_choice(p, turn):
                dve.wait_ge(rows_free, p + 1)
                v.tensor_copy(logits[:], aux[:, 0:TT * E].rearrange("p (t e) -> p t e", t=TT)).then_inc(aux_free, 1)
                dve.wait_ge(aux_free, turn + 1)
                dve.nop(nofuse=True)
                for tt in range(TT):
                    ins = v.max(top8[:, tt, :], logits[:, tt, :])
                ins.then_inc(top_done, 1)
                dve.wait_ge(top_done, p + 1)
                dve.nop(nofuse=True)
                for tt in range(TT):
                    ins = v.max_index(idx8[:, tt, :], top8[:, tt, :], logits[:, tt, :])
                ins.then_inc(idx_done, 1)
                v.tensor_tensor(gap[:], top8[:, :, 1], top8[:, :, 0], ALU.subtract).then_inc(gap_done, 1)
                dve.wait_ge(idx_done, p + 1)
                v.tensor_copy(idxf[:], idx8[:, :, 0:2].rearrange("p t n -> p n t")).then_inc(idxf_done, 1)
                dve.wait_ge(idxf_done, p + 1)
                for n in range(2):
                    ins = v.tensor_tensor(chosen[:, n, :, :], k.iota_e[:],
                                          idxf[:, n, :].unsqueeze(2).to_broadcast([P, TT, E]), ALU.is_equal)
                ins.then_inc(chosen_done, 1)
                dve.wait_ge(chosen_done, p + 1)
                v.tensor_tensor(both[:], chosen[:, 0, :, :], chosen[:, 1, :, :], ALU.add).then_inc(both_done, 1)

            def router_slots(p, turn):
                v.tensor_tensor(place[:], aux[:, 0:TT * E].rearrange("p (t e) -> p t e", t=TT), k.region[:], ALU.add
                                ).then_inc(aux_free, 1)
                v.tensor_reduce(both_sum[:], both[:].rearrange("p t e -> p e t"), AX.X, ALU.add).then_inc(summed, 1)
                dve.wait_ge(summed, p + 1)
                v.tensor_tensor(k.carry[:], k.carry[:], both_sum[:], ALU.add).then_inc(carried, 1)
                dve.wait_ge(aux_free, turn + 1)
                for n in range(2):
                    ins = v.tensor_tensor(chosen_place[:, n, :, :], chosen[:, n, :, :], place[:], ALU.mult)
                ins.then_inc(weighed, 1)
                dve.wait_ge(weighed, p + 1)
                v.tensor_reduce(slot_f[:], chosen_place[:], AX.X, ALU.add).then_inc(slot_f_done, 1)
                dve.wait_ge(slot_f_done, p + 1)
                v.tensor_copy(slot_b[:], slot_f[:].rearrange("p n t -> p (n t)")).then_inc(slot_done, 1)
                dve.wait_ge(exp_done, p + 1)
                v.tensor_scalar(gden[:], gexp[:], 1.0, None, ALU.add).then_inc(den_done, 1)
                dve.wait_ge(den_done, p + 1)
                v.reciprocal(gates[:, 0, :], gden[:]).then_inc(g1_done, 1)
                dve.wait_ge(g1_done, p + 1)
                v.tensor_tensor(gates[:, 1, :], gexp[:], gates[:, 0, :], ALU.mult).then_inc(g2_done, 1)

            def task(kind, b, name):
                turn = turn_of(kind, b, name)
                bb = b - 1 if name in POST else b
                if name in ("hT0", "hT1", "v0", "v1", "yT0", "yT1", "h2T0", "h2T1"):
                    return
                m = 1 if name[1:] == "1" else 0
                if name in ("q", "q1", "k", "k1"):
                    i = 0 if name[0] == "q" else 1
                    dve.wait_ge(hi_done, 2 * nth_part(kind, b, name) - 1 + i)
                    v.scalar_tensor_tensor(out=part_lo[i][:], in0=aux[:, :], scalar=k.bqk[:, 2 * i + m:2 * i + m + 1],
                                           in1=part_hi[i][:].bitcast(F32), op0=ALU.add, op1=ALU.subtract).then_inc(aux_free, 1)
                    return
                dve.wait_ge(aux_ready, turn + 1)
                if name[:3] == "ytr":
                    g = int(name[-1])
                    ps = aux[:, :].rearrange("p (t h d) -> p t h d", t=TT, h=4)
                    v.reciprocal(recips[:], ps[:, :, :, D]).then_inc(y_recip, 1)
                    dve.wait_ge(y_recip, 4 * bb + g + 1)
                    v.tensor_tensor(y_tok[:, :, 4 * D * g:4 * D * (g + 1)].rearrange("p t (h d) -> p t h d", h=4),
                                    ps[:, :, :, 0:D], recips[:].unsqueeze(3).to_broadcast([P, TT, 4, D]), ALU.mult
                                    ).then_inc(aux_free, 1)
                elif name[:2] == "pr":
                    i = int(name[-1])
                    dve.wait_ge(x1_kept, 16 * (bb + 1))
                    dve.wait_ge(xr_in, 32 * (bb + 1))
                    v.tensor_tensor(x1[:, 2 * i:2 * i + 2, :], aux[:, :].rearrange("p (u c) -> p u c", u=2),
                                    mod_row[:, 0:1, :].to_broadcast([P, 2, C]), ALU.mult).then_inc(aux_free, 1)
                elif name == "lg":
                    router_choice(bb, turn)
                elif name == "pos":
                    router_slots(bb, turn)

            dve.sem_inc(carried, 1)
            v.memset(q_st[0][:].bitcast(F32), 0.0).then_inc(cleared, 1)
            for name in AUX_PRO:
                task("pro", 0, name)
            v.memset(v_sb[0][:], 1.0).then_inc(cleared, 1)
            v.memset(q_st[1][:].bitcast(F32), 0.0).then_inc(cleared, 1)
            v.memset(v_sb[1][:], 1.0).then_inc(cleared, 1)

            def modulate(n):
                dve.wait_ge(rstd_done[1], n)
                for tt in range(TT):
                    ins = v.scalar_tensor_tensor(out=rows[:, tt, 0:C], in0=x1[:, tt, :], scalar=mv[1][:, tt, 0:1],
                                                 in1=mod_row[:, 2, :], op0=ALU.subtract, op1=ALU.mult)
                ins.then_inc(h2_scaled, 1)

            def modulate_end(n):
                dve.wait_ge(h2_scaled, n)
                for tt in range(TT):
                    ins = v.scalar_tensor_tensor(out=rows[:, tt, 0:C], in0=rows[:, tt, 0:C], scalar=rstd[1][:, tt:tt + 1],
                                                 in1=mod_row[:, 1, :], op0=ALU.mult, op1=ALU.add)
                ins.then_inc(h2_done, 1)

            def add_bias(kind, b, i, slots):
                for j in TILE_ORDER:
                    slot, col = TILE_AT[j]
                    if slot not in slots:
                        continue
                    w = (j + 1) * P
                    s = s_bank[(3 * i + slot) % 4][:, col:col + w]
                    if j != 0:
                        dve.wait_ge(scored, 3 * H * b + 3 * i + slot + 1)
                        dve.nop(nofuse=True)
                    v.tensor_tensor_reduce(s, s, k.bias_w[:, i, T - w:T], -1.0, BIG, ALU.add, ALU.min,
                                           neg_max[:, i % 4, j:j + 1]).then_inc(biased, 1)

            def copy_transposed(kind, b, h, slot):
                if kind != "first" or h >= 8:
                    dve.wait_ge(pv_done, 4 * b + h // 4 - 1)
                at, w = TR_SLOT[slot]
                dve.wait_ge(transposed, 3 * H * b + 3 * h + slot + 1)
                v.tensor_copy(probs_t[:, h % 8, at:at + w], t_bank[(3 * h + slot) % 2][:, 0:w]).then_inc(pt_dve, 1)

            def body(kind, b):
                for i in range(STEPS):
                    turned = transposed_head(kind, b, i)
                    if kind == "first" and i % 4 == 0:
                        dve.wait_ge(bias_in[i // 4], 16)
                    if kind != "end":
                        add_bias(kind, b, i, (0,))
                    if turned:
                        copy_transposed(kind, *turned, 0)
                    if kind != "end":
                        add_bias(kind, b, i, (1,))
                    if i == 2 and kind in ("first", "loop"):
                        ln_stats(0, b + 1, xin, x_in, 16 * (b + 1))
                    if i == 10 and kind != "first":
                        if kind == "end":
                            dve.wait_ge(aux_free, turn_of(kind, b, "pr1") + 1)
                            v.tensor_tensor(x1[:], x1[:], h2, ALU.add).then_inc(x1_done, 1)
                        ln_stats(1, b, x1, x1_done, b)
                        if kind == "end":
                            modulate(B)
                            modulate_end(B)
                    if kind != "end":
                        add_bias(kind, b, i, (2,))
                    for name in reads_of(kind, i, 0):
                        task(kind, b, name)
                    for name in reads_of(kind, i, 1):
                        task(kind, b, name)

            each_batch(dve, body)

        @block.gpsimd
        def _(pool):
            g = nc.gpsimd

            def deviations(i, n):
                pool.wait_ge(mv_done[i], n)
                pool.nop(nofuse=True)
                g.tensor_scalar(var[i][:], mv[i][:, :, 1], EPS, None, ALU.add).then_inc(var_done[i], 1)
                pool.wait_ge(var_done[i], n)
                pool.nop(nofuse=True)
                g.tensor_tensor(rstd[i][:], var[i][:], k.neghalf[:], ALU.pow).then_inc(rstd_done[i], 1)

            def normalise(i, n, src, dst):
                deviations(i, n)
                pool.wait_ge(rstd_done[i], n)
                pool.nop(nofuse=True)
                for tt in range(TT):
                    ins = g.tensor_scalar(dst[:, tt, :], src[:, tt, :], mv[i][:, tt, 0:1], rstd[i][:, tt:tt + 1],
                                          ALU.subtract, ALU.mult)
                ins.then_inc(normed[i], 1)

            def set_mod_b(b):
                g.tensor_copy(mod_b[:].unsqueeze(3), k.mod_c[:, :, :, bass.ds(b, 1)]).then_inc(mod_b_set, 1)

            def after(kind, b):
                p = b - 1
                if kind == "end":
                    deviations(1, B)
                else:
                    pool.wait_ge(aux_free, turn_of(kind, b, "pr1") + 1)
                    pool.wait_ge(xr_in, 32 * (p + 1))
                    g.tensor_tensor(x1[:], x1[:], h2, ALU.add).then_inc(x1_done, 1)
                    pool.wait_ge(x1_done, p + 1)
                    deviations(1, p + 1)
                    pool.wait_ge(rstd_done[1], p + 1)
                    g.tensor_tensor(shift[:], mv[1][:, :, 0], rstd[1][:], ALU.mult).then_inc(shift_step, 1)
                    pool.wait_ge(shift_step, 2 * p + 1)
                    g.tensor_tensor(shift[:], k.zeros[:], shift[:], ALU.subtract).then_inc(shift_step, 1)
                    pool.wait_ge(normed[1], p + 1)
                    g.tensor_tensor(h2, h2, mod_row[:, 2:3, :].to_broadcast([P, TT, C]), ALU.mult).then_inc(h2_scaled, 1)
                    pool.wait_ge(h2_scaled, p + 1)
                    g.tensor_tensor(h2, h2, mod_row[:, 1:2, :].to_broadcast([P, TT, C]), ALU.add).then_inc(h2_done, 1)
                g.tensor_tensor(rows[:, :, C], rows[:, :, C], k.to_next[:], ALU.add)
                pool.wait_ge(slot_done, p + 1)
                pool.wait_ge(g2_done, p + 1)
                pool.nop(nofuse=True)
                g.tensor_copy(rows[:, :, C + 1], idxf[:, 0, :]).then_inc(rows_named, 1)
                g.tensor_copy(k.gates_all[:, bass.ds(p, 1), :], gates[:].rearrange("p n t -> p (n t)").unsqueeze(1)
                              ).then_inc(kept, 1)
                pool.wait_ge(preset_in, 16 * E)
                pool.wait_ge(rows_named, p + 1)
                pool.nop(nofuse=True)
                for n in range(2 * TT):
                    g.indirect_dma_start(rows_d, bass.IndirectOffsetOnAxis(ap=slot_b[:, n:n + 1].bitcast(U32), axis=0),
                                         rows[:, n % TT, :], None).then_inc(scattered, 16)
                pool.wait_ge(kept, p + 1)
                pool.wait_ge(scattered, 16 * 2 * TT * (p + 1))
                pool.sem_inc(rows_free, 1)

            pool.sem_inc(rows_free, 1)
            g.tensor_copy(rows[:, :, C], k.token[:])
            set_mod_b(0)

            def body(kind, b):
                if kind in ("first", "loop"):
                    pool.wait_ge(aux_free, start_turn(kind, b))
                    pool.nop(nofuse=True)
                    set_mod_b(b + 1)
                    normalise(0, b + 1, xin, xin)
                if kind != "first":
                    after(kind, b)

            each_batch(pool, body)
def experts(nc, sem, w_all, low_all, b13_all, b2, rows_d, y_d, x1_d, mod_d, k):
    with ExitStack() as ctx:
        def sb(name, shape, dt=F32):
            return ctx.enter_context(nc.sbuf_tensor(name, shape, dt))

        raw = [sb(f"raw{i}", [P, 6, HID]) for i in range(2)]
        w_hi = [sb(f"w_hi{i}", [P, 6, HID], F32R) for i in range(2)]
        w_lo = [sb(f"w_lo{i}", [P, 6, HID], F32R) for i in range(2)]
        low_raw = [sb(f"low_raw{i}", [LOWROWS, LOWCOLS]) for i in range(2)]
        low_parts = [sb(f"low_parts{i}", [LOWROWS, LOWCOLS], F32R) for i in range(2)]
        b13 = sb("b13", [P, 2, E, HK])
        b2_rows = sb("b2_rows", [P, E, C])
        tile_in = sb("tile_in", [P, 2, C + 2])
        second = sb("second", [P, 2])
        names = sb("names", [P, 2, 2])
        goal = sb("goal", [P, 2], I32)
        x_hi = sb("x_hi", [P, KC, FT], F32R)
        x_lo = sb("x_lo", [P, KC, FT], F32R)
        silu = sb("silu", [P, HK, FT])
        g_full = sb("g_full", [P, HK, FT])
        g_hi = sb("g_hi", [P, HK, FT], F32R)
        g_lo = sb("g_lo", [P, HK, FT], F32R)
        y_sb = sb("y_sb", [P, 2, C])
        cnt = sb("cnt", [P, E], I32)
        cnt_up = sb("cnt_up", [P, E], I32)
        cnt_sh = sb("cnt_sh", [P, E], I32)
        n_tiles = sb("n_tiles", [P, E], I32)
        h_bank = [ctx.enter_context(nc.psum_tensor(f"h_bank{i}", [P, 512], F32)) for i in range(4)]
        yb = [ctx.enter_context(nc.psum_tensor(f"yb{i}", [P, 512], F32)) for i in range(2)]
        turn_bank = ctx.enter_context(nc.psum_tensor("turn_bank", [P, 512], F32))
        fold_bank = ctx.enter_context(nc.psum_tensor("fold_bank", [P, 512], F32))
        cnt_bank = fold_bank

        biases_in, x1_in, low_high_done, low_a_done, low_done, counted, cnt_done, padded = (
            sem(n) for n in ("biases_in", "x1_in", "low_high_done", "low_a_done", "low_done", "counted", "cnt_done", "padded"))
        low_in = [sem(f"low_in{i}") for i in range(2)]
        raw_in = [sem(f"raw_in{i}") for i in range(2)]
        folded, merged, split_hi, split_done = (sem(n) for n in ("folded", "merged", "split_hi", "split_done"))
        rows_in, turned, x_hi_done, x_split = (sem(n) for n in ("rows_in", "turned", "x_hi_done", "x_split"))
        names_taken, second_done, goal_set = (sem(n) for n in ("names_taken", "second_done", "goal_set"))
        h_ready, silu_ready, h_read, g_hi_done, g_split, y_ready, y_read, y_kept, y_gone = (
            sem(n) for n in ("h_ready", "silu_ready", "h_read", "g_hi_done", "g_split", "y_ready", "y_read", "y_kept", "y_gone"))

        def tile_counts(eng):
            eng.wait_ge(cnt_done, 4)
            n, base = [], [0]
            for e in range(E):
                n.append(eng.value_load(n_tiles[0:1, e:e + 1], min_val=1, max_val=B * T // FT))
                base.append(eng.snap(base[-1] + n[-1]))
            return n, base

        def low_low(eng, ops, e):
            eng.wait_ge(low_high_done, e + 1)
            at = (slice(64, 64 + R), slice(0, ACOLS))
            ops.tensor_tensor(low_parts[e % 2][at], low_raw[e % 2][at], low_parts[e % 2][at].bitcast(F32), ALU.subtract
                              ).then_inc(low_a_done, 1)
            eng.wait_ge(low_a_done, e + 1)
            at = (slice(32, 32 + R), slice(ACOLS, LOWCOLS))
            ops.tensor_tensor(low_parts[e % 2][at], low_raw[e % 2][at], low_parts[e % 2][at].bitcast(F32), ALU.subtract
                              ).then_inc(low_done, 1)

        block = ctx.enter_context(nc.Block())

        @block.sync
        def _(sp):
            def load_weights(e):
                sp.dma_start(raw[e % 2][:], w_all[e]).then_inc(raw_in[e % 2], 16)

            def load_low(e):
                sp.dma_start(low_raw[e % 2][:], low_all[e]).then_inc(low_in[e % 2], 16)

            load_low(0)
            load_weights(0)
            n, base = tile_counts(sp)
            for e in range(E):
                last = sp.value_load(cnt[0:1, e:e + 1], min_val=0, max_val=B * T)
                sp.dma_start(rows_d[bass.ds(last + e * REGION, FT), :].rearrange("(u p) c -> p u c", p=P), k.padding[:]
                             ).then_inc(padded, 16)
            sp.wait_ge(padded, 16 * E)

            def load_rows(first_row, g):
                sp.wait_ge(turned, g + 1)
                sp.wait_ge(names_taken, g + 1)
                sp.dma_start(tile_in[:], rows_d[bass.ds(first_row, FT), :].rearrange("(u p) c -> p u c", p=P)
                             ).then_inc(rows_in, 16)

            load_rows(0, 0)
            load_low(1)
            sp.dma_start(b13[:], b13_all).then_inc(biases_in, 16)
            sp.dma_start(b2_rows[:], b2.rearrange("e c -> (e c)").partition_broadcast(P).rearrange("p (e c) -> p e c", e=E)
                         ).then_inc(biases_in, 16)
            load_weights(1)
            def load_ahead(e):
                if e + 3 < E:
                    sp.wait_ge(low_done, e + 2)
                    load_low(e + 3)
                if e + 2 < E:
                    sp.wait_ge(split_done, e + 1)
                    load_weights(e + 2)

            for e in range(E):
                if e:
                    load_rows(e * REGION, base[e])
                if e == 0:
                    sp.wait_ge(low_done, 1)
                    load_low(2)
                else:
                    load_ahead(e)
                with sp.Fori(1, n[e]) as i:
                    load_rows(i * FT + e * REGION, base[e] + i)
                if e == 0:
                    load_ahead(0)
                for b in range(e * B // E, (e + 1) * B // E):
                    sp.dma_start(k.x1_all[:, b, :, :], x1_d[b].rearrange("(t p) c -> p t c", p=P)).then_inc(x1_in, 16)
                    sp.dma_start(k.gb_all[:, b, :], mod_d[b:b + 1, 3 * C:4 * C].partition_broadcast(P)).then_inc(x1_in, 16)
            load_rows(0, base[E])
            sp.wait_ge(x1_in, 32 * B)

        @block.tensor
        def _(pe):
            pe.matmul(cnt_bank[:, 0:E], k.ones[:], k.carry[:], start=True, stop=True).then_inc(counted, 1)

            def fold(e, j):
                if e == 0:
                    bank = h_bank[j % 4]
                    if j >= 4:
                        pe.wait_ge(merged, j - 3)
                else:
                    bank = fold_bank
                    pe.wait_ge(merged, 6 * e + j)
                if j == 0:
                    pe.wait_ge(low_done, e + 1)
                low = low_parts[e % 2]
                if j < 4:
                    mm = pe.matmul(bank[:, :], low[:, j * P:(j + 1) * P], low[:, ACOLS + (j // 2) * HID:ACOLS + (j // 2 + 1) * HID],
                                   start=True, stop=True)
                else:
                    for u in range(2):
                        mc = 2 * (j - 4) + u
                        mm = pe.matmul(bank[:, u * C:(u + 1) * C], low[:, 2 * C + mc * P:2 * C + (mc + 1) * P],
                                       low[:, ACOLS + 2 * HID:ACOLS + 2 * HID + C], start=True, stop=True)
                mm.then_inc(folded, 1)

            def turn():
                for u in range(2):
                    for kc in range(KC):
                        mm = pe.transpose(turn_bank[:, kc * FT + u * P:kc * FT + (u + 1) * P],
                                          tile_in[:, u, kc * P:(kc + 1) * P], k.ident[:])
                mm.then_inc(turned, 1)

            def tile(e, g, folds):
                hi, lo = w_hi[e % 2], w_lo[e % 2]
                pe.wait_ge(x_split, g + 1)
                for m in range(HK):
                    pe.wait_ge(h_read, 4 * g + (m + 1))
                    for which in range(2):
                        parts = [(kc, w, xs) for kc in range(KC) for w, xs in ((hi, x_hi), (hi, x_lo), (lo, x_hi))]
                        for q, (kc, w, xs) in enumerate(parts):
                            mm = pe.matmul(h_bank[m][:, which * FT:(which + 1) * FT], w[:, 2 * which + kc, m * P:(m + 1) * P],
                                           xs[:, kc, :], start=(q == 0), stop=(q == len(parts) - 1))
                    mm.then_inc(h_ready, 1)
                    if folds:
                        fold(e + 1, m)
                pe.wait_ge(rows_in, 16 * g + 32)
                turn()
                pe.wait_ge(y_read, g + 1)
                for m in range(HK):
                    pe.wait_ge(g_split, 4 * g + (m + 1))
                    for u in range(2):
                        for q, (gs, w) in enumerate(((g_hi, hi), (g_lo, hi), (g_hi, lo))):
                            mm = pe.matmul(yb[u][:, 0:C], gs[:, m, u * P:(u + 1) * P],
                                           w[:, 4 + m // 2, (m % 2) * C:(m % 2 + 1) * C],
                                           start=(m == 0 and q == 0), stop=(m == HK - 1 and q == 2))
                    if m == HK - 1:
                        mm.then_inc(y_ready, 1)
                    if folds and m % 2 == 1:
                        fold(e + 1, 4 + m // 2)

            pe.sem_inc(turned, 1)
            pe.sem_inc(y_ready, 1)
            n, base = tile_counts(pe)
            for j in range(6):
                fold(0, j)
            pe.wait_ge(rows_in, 16)
            turn()
            for e in range(E):
                pe.wait_ge(split_done, e + 1)
                tile(e, base[e], e + 1 < E)
                with pe.Fori(1, n[e]) as i:
                    tile(e, base[e] + i, False)

        @block.scalar
        def _(act):
            n, base = tile_counts(act)

            def split_high(e, j):
                act.wait_ge(merged, 6 * e + j + 1)
                nc.scalar.copy(w_hi[e % 2][:, j, :], raw[e % 2][:, j, :]).then_inc(split_hi, 1)

            def low_high(e):
                act.wait_ge(low_in[e % 2], 16 * (e // 2 + 1))
                if e >= 2:
                    act.wait_ge(folded, 6 * (e - 1))
                nc.scalar.copy(low_parts[e % 2][:], low_raw[e % 2][:]).then_inc(low_high_done, 1)

            def take_high(g):
                act.wait_ge(turned, g + 2)
                nc.scalar.copy(x_hi[:], turn_bank[:, :].rearrange("p (k t) -> p k t", k=KC)).then_inc(x_hi_done, 1)

            def tile(e, g, splits):
                for m in range(HK + 1):
                    if m < HK:
                        act.wait_ge(h_ready, 4 * g + (m + 1))
                        act.wait_ge(h_read, 4 * g + (m + 1))
                        nc.scalar.activation(silu[:, m, :], h_bank[m][:, 0:FT], ACT.Silu, bias=b13[:, 0, e, m:m + 1]
                                             ).then_inc(silu_ready, 1)
                    if m:
                        if m == 1:
                            act.wait_ge(y_ready, g + 1)
                        act.wait_ge(h_read, 4 * g + (m + 4))
                        nc.scalar.copy(g_hi[:, m - 1, :], g_full[:, m - 1, :]).then_inc(g_hi_done, 1)
                        if splits:
                            split_high(e + 1, m - 1)
                take_high(g + 1)
                if splits:
                    split_high(e + 1, 4)
                    split_high(e + 1, 5)
                    if e == 0:
                        low_high(2)

            low_high(0)
            for j in range(6):
                split_high(0, j)
            take_high(0)
            low_high(1)
            act.wait_ge(biases_in, 32)
            for e in range(E):
                tile(e, base[e], e + 1 < E)
                with act.Fori(1, n[e]) as i:
                    tile(e, base[e] + i, False)
                if e + 3 < E:
                    low_high(e + 3)

        @block.vector
        def _(dve):
            v = nc.vector
            dve.wait_ge(counted, 1)
            v.tensor_copy(cnt[:], cnt_bank[:, 0:E])
            v.tensor_scalar(cnt_up[:], cnt_bank[:, 0:E], float(FT - 1), None, ALU.add).then_inc(cnt_done, 1)
            dve.wait_ge(cnt_done, 1)
            v.tensor_scalar(cnt_sh[:], cnt_up[:], FT.bit_length() - 1, None, ALU.logical_shift_right).then_inc(cnt_done, 1)
            dve.wait_ge(cnt_done, 2)
            v.tensor_scalar(n_tiles[:], cnt_sh[:], 2.0, None, ALU.max).then_inc(cnt_done, 1)
            dve.wait_ge(cnt_done, 3)
            dve.sem_inc(cnt_done, 1)
            dve.sem_inc(h_read, 4)
            dve.sem_inc(y_read, 1)
            dve.sem_inc(y_gone, 1)
            dve.sem_inc(names_taken, 1)
            n, base = tile_counts(dve)

            def merge(e, j):
                if j == 0:
                    dve.wait_ge(raw_in[e % 2], 16 * (e // 2 + 1))
                dve.wait_ge(folded, 6 * e + j + 1)
                bank = fold_bank if e else h_bank[j % 4]
                v.tensor_tensor(raw[e % 2][:, j, :], raw[e % 2][:, j, :], bank[:, :], ALU.add).then_inc(merged, 1)

            def take_low(g):
                dve.wait_ge(x_hi_done, g + 1)
                v.tensor_tensor(x_lo[:], turn_bank[:, :].rearrange("p (k t) -> p k t", k=KC), x_hi[:].bitcast(F32),
                                ALU.subtract).then_inc(x_split, 1)

            def take_names(g):
                dve.wait_ge(x_hi_done, g + 1)
                v.tensor_copy(names[:], tile_in[:, :, C:C + 2]).then_inc(names_taken, 1)

            def tile(e, g, merges):
                for m in range(HK + 1):
                    if m < HK:
                        dve.wait_ge(silu_ready, 4 * g + (m + 1))
                        v.scalar_tensor_tensor(out=g_full[:, m, :], in0=h_bank[m][:, FT:2 * FT], scalar=b13[:, 1, e, m:m + 1],
                                               in1=silu[:, m, :], op0=ALU.add, op1=ALU.mult).then_inc(h_read, 1)
                        if merges:
                            merge(e + 1, m)
                    if m:
                        dve.wait_ge(g_hi_done, 4 * g + m)
                        v.tensor_tensor(g_lo[:, m - 1, :], g_full[:, m - 1, :], g_hi[:, m - 1, :].bitcast(F32), ALU.subtract
                                        ).then_inc(g_split, 1)
                dve.wait_ge(y_gone, g + 1)
                dve.wait_ge(names_taken, g + 2)
                v.tensor_scalar(second[:], names[:, :, 1], float(e), float(B * T), ALU.not_equal, ALU.mult
                                ).then_inc(second_done, 1)
                dve.wait_ge(second_done, g + 1)
                v.tensor_tensor(goal[:], second[:], names[:, :, 0], ALU.add).then_inc(goal_set, 1)
                take_low(g + 1)
                dve.wait_ge(goal_set, g + 1)
                take_names(g + 1)
                if merges:
                    merge(e + 1, 4)
                dve.wait_ge(y_ready, g + 2)
                for u in range(2):
                    ins = v.tensor_tensor(y_sb[:, u, :], yb[u][:, 0:C], b2_rows[:, e, :], ALU.add)
                ins.then_inc(y_read, 1)
                if merges:
                    merge(e + 1, 5)

            low_low(dve, v, 0)
            for j in range(6):
                merge(0, j)
            for j in range(6):
                dve.wait_ge(split_hi, j + 1)
                ins = v.tensor_tensor(w_lo[0][:, j, :], raw[0][:, j, :], w_hi[0][:, j, :].bitcast(F32), ALU.subtract)
            ins.then_inc(split_done, 1)
            take_low(0)
            take_names(0)
            low_low(dve, v, 1)
            for e in range(E):
                tile(e, base[e], e + 1 < E)
                if e == 0:
                    low_low(dve, v, 2)
                with dve.Fori(1, n[e]) as i:
                    tile(e, base[e] + i, False)

        @block.gpsimd
        def _(pool):
            g = nc.gpsimd
            n, base = tile_counts(pool)

            def scatter(t):
                pool.wait_ge(goal_set, t + 1)
                pool.wait_ge(y_read, t + 2)
                pool.nop(nofuse=True)
                for u in range(2):
                    g.indirect_dma_start(y_d, bass.IndirectOffsetOnAxis(ap=goal[:, u:u + 1].bitcast(U32), axis=0),
                                         y_sb[:, u, :], None).then_inc(y_kept, 16)
                pool.wait_ge(y_kept, 32 * t + 32)
                pool.sem_inc(y_gone, 1)

            for e in range(E):
                scatter(base[e])
                if e + 1 < E:
                    i = (e + 1) % 2
                    for j in range(6):
                        pool.wait_ge(split_hi, 6 * (e + 1) + j + 1)
                        ins = g.tensor_tensor(w_lo[i][:, j, :], raw[i][:, j, :], w_hi[i][:, j, :].bitcast(F32), ALU.subtract)
                    ins.then_inc(split_done, 1)
                with pool.Fori(1, n[e]) as i:
                    scatter(base[e] + i)
                if e + 3 < E:
                    pool.wait_ge(split_done, e + 2)
                    low_low(pool, g, e + 3)
                    pool.wait_ge(low_done, e + 4)


def combine(nc, sem, y_d, out, k):
    with ExitStack() as ctx:
        def sb(name, shape, dt=F32):
            return ctx.enter_context(nc.sbuf_tensor(name, shape, dt))

        y12 = [sb(f"y12_{i}", [P, 2, TT, C]) for i in range(4)]
        first = [sb(f"first{i}", [P, TT, C]) for i in range(2)]
        mixed = [sb(f"mixed{i}", [P, TT, C]) for i in range(2)]
        scaled = [sb(f"scaled_mix{i}", [P, TT, C]) for i in range(2)]
        res = [sb(f"res{i}", [P, TT, C]) for i in range(2)]
        y_in = [sem(f"y_in{i}") for i in range(4)]
        res_kept = [sem(f"res_kept{i}") for i in range(2)]
        weighted, mix_done, mix_scaled, res_done = (sem(n) for n in ("weighted", "mix_done", "mix_scaled", "res_done"))
        block = ctx.enter_context(nc.Block())

        @block.sync
        def _(sp):
            for b in range(B):
                if b >= 4:
                    sp.wait_ge(mix_done, b - 3)
                for n in range(2):
                    at = n * B * T + b * T
                    sp.dma_start(y12[b % 4][:, n, :, :], y_d[at:at + T, :].rearrange("(t p) c -> p t c", p=P)).then_inc(y_in[b % 4], 16)

        @block.scalar
        def _(act):
            def keep(b):
                act.wait_ge(res_done, b + 1)
                act.dma_start(out[b].rearrange("(t p) c -> p t c", p=P), res[b % 2][:]).then_inc(res_kept[b % 2], 16)

            for b in range(B):
                i = b % 2
                act.wait_ge(y_in[b % 4], 32 * (b // 4 + 1))
                if b >= 2:
                    act.wait_ge(mix_done, b - 1)
                for tt in range(TT):
                    ins = nc.scalar.activation(first[i][:, tt, :], y12[b % 4][:, 0, tt, :], ACT.Copy, scale=k.gates_all[:, b, tt:tt + 1])
                ins.then_inc(weighted, 1)
                if b:
                    keep(b - 1)
            keep(B - 1)
            for i in range(2):
                act.wait_ge(res_kept[i], 16 * (B // 2))

        @block.vector
        def _(dve):
            v = nc.vector
            for b in range(B):
                i = b % 2
                dve.wait_ge(weighted, b + 1)
                for tt in range(TT):
                    ins = v.scalar_tensor_tensor(out=mixed[i][:, tt, :], in0=y12[b % 4][:, 1, tt, :],
                                                 scalar=k.gates_all[:, b, TT + tt:TT + tt + 1], in1=first[i][:, tt, :],
                                                 op0=ALU.mult, op1=ALU.add)
                ins.then_inc(mix_done, 1)
                dve.wait_ge(mix_done, b + 1)
                v.tensor_tensor(scaled[i][:], mixed[i][:], k.gb_all[:, b:b + 1, :].to_broadcast([P, TT, C]), ALU.mult
                                ).then_inc(mix_scaled, 1)
                if b >= 2:
                    dve.wait_ge(res_kept[i], 16 * (b // 2))
                dve.wait_ge(mix_scaled, b + 1)
                v.tensor_tensor(res[i][:], scaled[i][:], k.x1_all[:, b, :, :], ALU.add).then_inc(res_done, 1)
def build(nc, x, w_attn, b_qk, b_v, w_proj, b_proj, bias_table, onehot, wg, cT, wmod,
          w_all, low_all, b13_all, b2, out):
    with ExitStack() as ctx:
        def dram(name, shape, dt=F32):
            return nc.dram_tensor(name, shape, dt, kind="Internal").ap()

        def sem(name):
            return ctx.enter_context(nc.semaphore(name))

        def sb(inner, name, shape, dt=F32):
            return inner.enter_context(nc.sbuf_tensor(name, shape, dt))

        line_d = dram("line_d", [H, P, LIN + 1])
        qk_d = [[dram(f"qk_d{i}{m}", [2, P, T]) for m in range(2)] for i in range(2)]
        x1_d = dram("x1_d", [B, T, C])
        rows_d = dram("rows_d", [E * REGION, C + 2])
        y_d = dram("y_d", [3 * B * T + 2 * FT, C])
        mod_d = dram("mod_d", [B, 4 * C])
        k = Kept()
        k.ident = sb(ctx, "ident", [P, P])
        k.ones = sb(ctx, "ones", [P, P])
        k.carry = sb(ctx, "carry", [P, E])
        k.padding = sb(ctx, "padding", [P, 2, C + 2])
        k.gates_all = sb(ctx, "gates_all", [P, B, 2 * TT])
        with ExitStack() as inner:
            k.before = sb(inner, "before", [P, P])
            k.iota_e = sb(inner, "iota_e", [P, TT, E])
            k.region = sb(inner, "region", [P, TT, E])
            k.neghalf = sb(inner, "neghalf", [P, TT])
            k.bias_w = sb(inner, "bias_w", [P, H, T])
            k.wa = sb(inner, "wa", [P, KC, 3 * C])
            k.wp = sb(inner, "wp", [P, KC, C])
            k.wg_sb = sb(inner, "wg_sb", [P, KC, E])
            k.bqk = sb(inner, "bqk", [P, 2 * KC])
            k.xin = sb(inner, "xin", [P, TT, C])
            k.zeros = sb(inner, "zeros", [P, TT])
            k.bp_parts = sb(inner, "bp_parts", [P, C], F32R)
            k.ones_r = sb(inner, "ones_r", [P, P], F32R)
            k.bp_row = sb(inner, "bp_row", [1, C])
            k.sc = sb(inner, "sc", [P, KC, B])
            k.preset = sb(inner, "preset", [P, 2, C + 2])
            k.line = sb(inner, "line", [H, LIN])
            k.token = sb(inner, "token", [P, TT])
            k.to_next = sb(inner, "to_next", [P, TT])
            k.mod_c = sb(inner, "mod_c", [P, 2, KC, B])
            setup(nc, sem, x, w_attn, b_qk, b_v, w_proj, b_proj, bias_table, onehot, wg, cT, wmod, mod_d, k)
            attention(nc, sem, x, line_d, qk_d, x1_d, rows_d, mod_d, k)
        with ExitStack() as inner:
            k.x1_all = sb(inner, "x1_all", [P, B, TT, C])
            k.gb_all = sb(inner, "gb_all", [P, B, C])
            experts(nc, sem, w_all, low_all, b13_all, b2, rows_d, y_d, x1_d, mod_d, k)
            combine(nc, sem, y_d, out, k)


def kernel(L0_attn_x, L0_attn_W_attn, L0_attn_b_attn, L0_attn_W_proj, L0_attn_b_proj, L0_attn_bias_table,
           L0_ffn_Wg, L0_ffn_W1, L0_ffn_b1, L0_ffn_A1, L0_ffn_B1, L0_ffn_W2, L0_ffn_b2, L0_ffn_A2, L0_ffn_B2,
           L0_ffn_W3, L0_ffn_b3, L0_ffn_A3, L0_ffn_B3, L0_c, L0_wmod):
    from concourse import bacc
    from concourse.bass_utils import run_bass_kernel_spmd

    def t(a, *axes):
        return np.transpose(np.asarray(a), axes)

    w_in = np.stack([t(L0_ffn_W1, 0, 2, 1), t(L0_ffn_W3, 0, 2, 1)], 1).reshape(E, 2 * KC, P, HID)
    w_out = t(L0_ffn_W2, 0, 2, 1).reshape(E, 2, 2, P, C).transpose(0, 1, 3, 2, 4).reshape(E, 2, P, 2 * C)
    w_all = np.concatenate([w_in, w_out], 1).transpose(0, 2, 1, 3)
    low = np.concatenate([np.asarray(a) for a in (L0_ffn_A1, L0_ffn_A3, L0_ffn_A2)]
                         + [t(a, 0, 2, 1) for a in (L0_ffn_B1, L0_ffn_B3, L0_ffn_B2)], 2)
    low_all = np.zeros((E, 3, LOWROWS // 3, LOWCOLS), low.dtype)
    low_all[:, :, 0:R, :] = low[:, None]
    low_all = low_all.reshape(E, LOWROWS, LOWCOLS)
    b13_all = np.stack([L0_ffn_b1, L0_ffn_b3]).reshape(2, E, HK, P).transpose(3, 0, 1, 2)
    arrays = dict(
        x=L0_attn_x, w_attn=L0_attn_W_attn, b_qk=L0_attn_b_attn[:2 * C], b_v=L0_attn_b_attn[2 * C:],
        w_proj=L0_attn_W_proj, b_proj=L0_attn_b_proj, bias_table=L0_attn_bias_table, onehot=constants(),
        wg=t(L0_ffn_Wg, 1, 0), cT=t(L0_c, 1, 0), wmod=L0_wmod,
        w_all=w_all, low_all=low_all, b13_all=b13_all, b2=L0_ffn_b2)
    arrays = {f"in_{name}": np.ascontiguousarray(a) for name, a in arrays.items()}
    nc = bacc.Bacc("TRN2", target_bir_lowering=False, num_devices=1)
    args = {name[3:]: nc.dram_tensor(name, a.shape, mybir.dt.from_np(a.dtype), kind="ExternalInput").ap()
            for name, a in arrays.items()}
    out = nc.dram_tensor("out_x", [B, T, C], F32, kind="ExternalOutput").ap()
    build(nc, out=out, **args)
    result = run_bass_kernel_spmd(nc, [arrays], core_ids=[0])
    return result.results[0]["out_x"]
```
